# Optimizing a Trainium2 kernel written in Bass

```python
import numpy as np
import jax
import jax.numpy as jnp

def _softmax(x, axis=-1):
    return jax.nn.softmax(x, axis=axis)

def _gelu(x):
    return jax.nn.gelu(x, approximate=True)

def _silu(x):
    return jax.nn.silu(x)

def _sigmoid(x):
    return jax.nn.sigmoid(x)

def _layernorm(x, axis=-1, eps=1e-05):
    m = jnp.mean(x, axis=axis, keepdims=True)
    v = jnp.var(x, axis=axis, keepdims=True)
    return (x - m) / jnp.sqrt(v + eps)

def _scatter_add(tgt, idx, src, axis=0):
    return tgt.at[idx].add(src)

def _segment_sum(src, seg, n):
    return jax.ops.segment_sum(src, seg, n)
kernel_name = 'mk_decoder_postln_d1_seqx_r4_f5e23c'

def setup_inputs(seed: int=0):
    np.random.seed(seed)
    _w = jnp.asarray

    def _rec_inputs():
        import jax
        import jax.numpy as jnp
        _rk = jax.random.key(seed)
        x = 7.22e-05 + 1 * jax.random.normal(jax.random.fold_in(_rk, 1), (2, 1024, 256), jnp.float32)
        _lenS = 1024 - jax.random.randint(jax.random.fold_in(_rk, 7), (2,), 0, max(1, 1024 // 4) + 1, jnp.int32)
        _lenS2 = 77 - jax.random.randint(jax.random.fold_in(_rk, 8), (2,), 0, max(1, 77 // 4) + 1, jnp.int32)
        _ctx_1024P = jax.random.normal(jax.random.fold_in(_rk, 11), (2, 16, 256), jnp.float32)
        _ctx_1024c = jax.random.dirichlet(jax.random.fold_in(_rk, 511), 0.3 * jnp.ones((16,), jnp.float32), (2, 77))
        _ctx_1024t = jnp.einsum('bsk,bkd->bsd', _ctx_1024c, _ctx_1024P)
        _ctx_1024t = _ctx_1024t * jax.lax.rsqrt(jnp.mean(jnp.square(_ctx_1024t)) + 1e-12) * 0.953939
        ctx_1024 = 4.13588e-05 + 0.999923 * (_ctx_1024t + 0.3 * jax.random.normal(jax.random.fold_in(_rk, 611), (2, 77, 256), jnp.float32))
        _validS = jnp.arange(1024)[None, :] < _lenS[:, None]
        _validS2 = jnp.arange(77)[None, :] < _lenS2[:, None]
        _causal = jnp.tril(jnp.ones((1024, 1024), dtype=bool))
        mask_Bx1xSxS2_fk0 = jnp.where(jnp.broadcast_to(_validS2[:, None, None, :], (2, 1, 1024, 77)), 0.0, 1.0).astype(jnp.float32)
        return (x, ctx_1024, mask_Bx1xSxS2_fk0)
    x, ctx_1024, mask_Bx1xSxS2_fk0 = _rec_inputs()

    def _L0_attn_setup():
        import jax, jax.numpy as jnp
        import numpy as np
        HEADS = 16

        def _binarize(W):
            alpha = jnp.mean(jnp.abs(W), axis=tuple(range(1, W.ndim)), keepdims=True)
            B = W + jax.lax.stop_gradient(jnp.sign(W) - W)
            return alpha * B

        def _binlinear(x, W, b):
            Wb = _binarize(W)
            return jnp.einsum('btc,oc->bto', x, Wb) + b
        key = jax.random.key(seed)
        ks = jax.random.split(key, 9)
        dim = 256
        B, T = (4, 512)
        inp = {'x': jax.random.normal(ks[0], (B, T, dim), jnp.float32), 'Wq': jax.random.normal(ks[1], (dim, dim), jnp.float32) * 0.02, 'bq': jax.random.normal(ks[2], (dim,), jnp.float32) * 0.02, 'Wk': jax.random.normal(ks[3], (dim, dim), jnp.float32) * 0.02, 'bk': jax.random.normal(ks[4], (dim,), jnp.float32) * 0.02, 'Wv': jax.random.normal(ks[5], (dim, dim), jnp.float32) * 0.02, 'bv': jax.random.normal(ks[6], (dim,), jnp.float32) * 0.02, 'Wp': jax.random.normal(ks[7], (dim, dim), jnp.float32) * 0.02, 'bp': jax.random.normal(ks[8], (dim,), jnp.float32) * 0.02}
        return inp
    _L0_attn_all = _L0_attn_setup()
    _L0_attn_in = {k: v for k, v in _L0_attn_all.items() if k in ('Wq', 'bq', 'Wk', 'bk', 'Wv', 'bv', 'Wp', 'bp')}
    del _L0_attn_all

    def _L0_xattn_setup():
        import jax, jax.numpy as jnp
        import numpy as np
        D_MODEL = 256
        NUM_HEADS = 16
        DEPTH = D_MODEL // NUM_HEADS
        B, S = (4, 512)

        def _split(t):
            b, s, _ = t.shape
            return t.reshape(b, s, NUM_HEADS, DEPTH).transpose(0, 2, 1, 3)
        key = jax.random.key(seed)
        ks = jax.random.split(key, 13)
        sd = 1.0 / np.sqrt(D_MODEL)
        inp = {'q_in': jax.random.normal(ks[0], (B, S, D_MODEL), jnp.float32), 'k_in': jax.random.normal(ks[1], (B, S, D_MODEL), jnp.float32), 'v_in': jax.random.normal(ks[2], (B, S, D_MODEL), jnp.float32), 'm_in': (jax.random.uniform(ks[3], (B, 1, S, S)) < 0.1).astype(jnp.float32), 'Wq': jax.random.normal(ks[4], (D_MODEL, D_MODEL), jnp.float32) * sd, 'bq': jax.random.normal(ks[5], (D_MODEL,), jnp.float32) * 0.01, 'Wk': jax.random.normal(ks[6], (D_MODEL, D_MODEL), jnp.float32) * sd, 'bk': jax.random.normal(ks[7], (D_MODEL,), jnp.float32) * 0.01, 'Wv': jax.random.normal(ks[8], (D_MODEL, D_MODEL), jnp.float32) * sd, 'bv': jax.random.normal(ks[9], (D_MODEL,), jnp.float32) * 0.01, 'Wo': jax.random.normal(ks[10], (D_MODEL, D_MODEL), jnp.float32) * sd, 'bo': jax.random.normal(ks[11], (D_MODEL,), jnp.float32) * 0.01}
        return inp
    _L0_xattn_all = _L0_xattn_setup()
    _L0_xattn_in = {k: v for k, v in _L0_xattn_all.items() if k in ('Wq', 'bq', 'Wk', 'bk', 'Wv', 'bv', 'Wo', 'bo')}
    del _L0_xattn_all

    def _L0_ffn_setup():
        import jax, jax.numpy as jnp
        import numpy as np
        E = 8
        D = 256
        H = 512
        TOP_K = 2
        key = jax.random.key(seed)
        k_x, k_g, k_w1, k_w2 = jax.random.split(key, 4)
        B, S = (4, 512)
        inp = {'input': jax.random.normal(k_x, (B, S, D), dtype=jnp.float32), 'Wg': jax.random.normal(k_g, (D, E), dtype=jnp.float32) * 0.02, 'W1': jax.random.normal(k_w1, (E, D, H), dtype=jnp.float32) * 0.02, 'b1': jnp.zeros((E, H), dtype=jnp.float32), 'W2': jax.random.normal(k_w2, (E, H, D), dtype=jnp.float32) * 0.02, 'b2': jnp.zeros((E, D), dtype=jnp.float32)}
        return inp
    _L0_ffn_all = _L0_ffn_setup()
    _L0_ffn_in = {k: v for k, v in _L0_ffn_all.items() if k in ('Wg', 'W1', 'b1', 'W2', 'b2')}
    del _L0_ffn_all
    return {'x': x, 'ctx_1024': ctx_1024, 'mask_Bx1xSxS2_fk0': mask_Bx1xSxS2_fk0, 'L0_attn_Wq': _L0_attn_in['Wq'], 'L0_attn_bq': _L0_attn_in['bq'], 'L0_attn_Wk': _L0_attn_in['Wk'], 'L0_attn_bk': _L0_attn_in['bk'], 'L0_attn_Wv': _L0_attn_in['Wv'], 'L0_attn_bv': _L0_attn_in['bv'], 'L0_attn_Wp': _L0_attn_in['Wp'], 'L0_attn_bp': _L0_attn_in['bp'], 'L0_xattn_Wq': _L0_xattn_in['Wq'], 'L0_xattn_bq': _L0_xattn_in['bq'], 'L0_xattn_Wk': _L0_xattn_in['Wk'], 'L0_xattn_bk': _L0_xattn_in['bk'], 'L0_xattn_Wv': _L0_xattn_in['Wv'], 'L0_xattn_bv': _L0_xattn_in['bv'], 'L0_xattn_Wo': _L0_xattn_in['Wo'], 'L0_xattn_bo': _L0_xattn_in['bo'], 'L0_ffn_Wg': _L0_ffn_in['Wg'], 'L0_ffn_W1': _L0_ffn_in['W1'], 'L0_ffn_b1': _L0_ffn_in['b1'], 'L0_ffn_W2': _L0_ffn_in['W2'], 'L0_ffn_b2': _L0_ffn_in['b2']}

def reference(x, ctx_1024, mask_Bx1xSxS2_fk0, L0_attn_Wq, L0_attn_bq, L0_attn_Wk, L0_attn_bk, L0_attn_Wv, L0_attn_bv, L0_attn_Wp, L0_attn_bp, L0_xattn_Wq, L0_xattn_bq, L0_xattn_Wk, L0_xattn_bk, L0_xattn_Wv, L0_xattn_bv, L0_xattn_Wo, L0_xattn_bo, L0_ffn_Wg, L0_ffn_W1, L0_ffn_b1, L0_ffn_W2, L0_ffn_b2):
    import jax
    import jax.numpy as jnp

    def _L0_attn_ref(x, Wq, bq, Wk, bk, Wv, bv, Wp, bp):
        import jax, jax.numpy as jnp
        import numpy as np
        HEADS = 16

        def _binarize(W):
            alpha = jnp.mean(jnp.abs(W), axis=tuple(range(1, W.ndim)), keepdims=True)
            B = W + jax.lax.stop_gradient(jnp.sign(W) - W)
            return alpha * B

        def _binlinear(x, W, b):
            Wb = _binarize(W)
            return jnp.einsum('btc,oc->bto', x, Wb) + b
        B, T, C = x.shape
        H = HEADS
        Dh = C // H
        scale = Dh ** (-0.5)

        def split_heads(t):
            return t.reshape(B, T, H, Dh).transpose(0, 2, 1, 3)
        q = split_heads(_binlinear(x, Wq, bq))
        k = split_heads(_binlinear(x, Wk, bk))
        v = split_heads(_binlinear(x, Wv, bv))
        att = jnp.einsum('bhtd,bhsd->bhts', q, k) * scale
        att = jax.nn.softmax(att, axis=-1)
        y = jnp.einsum('bhts,bhsd->bhtd', att, v)
        y = y.transpose(0, 2, 1, 3).reshape(B, T, C)
        return _binlinear(y, Wp, bp)

    def _L0_xattn_ref(q_in, k_in, v_in, m_in, Wq, bq, Wk, bk, Wv, bv, Wo, bo):
        import jax, jax.numpy as jnp
        import numpy as np
        D_MODEL = 256
        NUM_HEADS = 16
        DEPTH = D_MODEL // NUM_HEADS
        B, S = (4, 512)

        def _split(t):
            b, s, _ = t.shape
            return t.reshape(b, s, NUM_HEADS, DEPTH).transpose(0, 2, 1, 3)
        q = _split(q_in @ Wq.T + bq)
        k = _split(k_in @ Wk.T + bk)
        v = _split(v_in @ Wv.T + bv)
        scale = jnp.sqrt(jnp.asarray(DEPTH, jnp.float32))
        scores = jnp.einsum('bhqd,bhkd->bhqk', q, k) / scale
        scores = scores - m_in * 1000000.0
        attn = jax.nn.softmax(scores, axis=-1)
        out = jnp.einsum('bhqk,bhkd->bhqd', attn, v)
        out = out.transpose(0, 2, 1, 3).reshape(q_in.shape[0], -1, D_MODEL)
        return out @ Wo.T + bo

    def _L0_ffn_ref(input, Wg, W1, b1, W2, b2):
        import jax, jax.numpy as jnp
        import numpy as np
        E = 8
        D = 256
        H = 512
        TOP_K = 2
        logits = jnp.einsum('bsd,de->bse', input, Wg)
        probs = jax.nn.softmax(logits, axis=-1)
        top_vals, top_idx = jax.lax.top_k(probs, TOP_K)
        top_vals = top_vals / jnp.sum(top_vals, axis=-1, keepdims=True)
        onehot = jax.nn.one_hot(top_idx, E, dtype=input.dtype)
        mask = jnp.sum(onehot, axis=2)
        scores = jnp.sum(onehot * top_vals[..., None], axis=2)
        xm = input[None] * jnp.moveaxis(mask, -1, 0)[..., None]
        h = jnp.einsum('ebsd,edh->ebsh', xm, W1) + b1[:, None, None, :]
        h = jax.nn.relu(h)
        y = jnp.einsum('ebsh,ehd->ebsd', h, W2) + b2[:, None, None, :]
        out = jnp.sum(y * jnp.moveaxis(scores, -1, 0)[..., None], axis=0)
        return out
    x = _layernorm(x + _L0_attn_ref(x, L0_attn_Wq, L0_attn_bq, L0_attn_Wk, L0_attn_bk, L0_attn_Wv, L0_attn_bv, L0_attn_Wp, L0_attn_bp), axis=-1)
    x = _layernorm(x + _L0_xattn_ref(x, ctx_1024, ctx_1024, mask_Bx1xSxS2_fk0, L0_xattn_Wq, L0_xattn_bq, L0_xattn_Wk, L0_xattn_bk, L0_xattn_Wv, L0_xattn_bv, L0_xattn_Wo, L0_xattn_bo), axis=-1)
    x = _layernorm(x + _L0_ffn_ref(x, L0_ffn_Wg, L0_ffn_W1, L0_ffn_b1, L0_ffn_W2, L0_ffn_b2), axis=-1)
    return x

_drawn_inputs = setup_inputs


def setup_inputs(seed=0):
    import zlib

    import numpy as np

    out = dict(_drawn_inputs(seed))
    spreads = {'L0_ffn_b1': (0.0, 0.367), 'L0_ffn_b2': (0.0, 0.1)}
    factors = {'L0_attn_Wq': 8.0,
     'L0_attn_bq': 8.0,
     'L0_attn_Wk': 8.0,
     'L0_attn_bk': 64.0,
     'L0_attn_Wv': 8.0,
     'L0_attn_bv': 7.333,
     'L0_attn_Wp': 6.608,
     'L0_xattn_bq': 8.0,
     'L0_xattn_bk': 64.0,
     'L0_xattn_bv': 4.453,
     'L0_xattn_bo': 4.764,
     'L0_attn_bp': 4.499}
    for name, (base, spread) in spreads.items():
        noise = np.random.default_rng([zlib.crc32(name.encode()), seed]).standard_normal(out[name].shape)
        drawn = base * np.exp(spread * noise) if base else spread * noise
        out[name] = jnp.asarray(drawn.astype(out[name].dtype))
    for name, factor in factors.items():
        out[name] = (out[name] * factor).astype(out[name].dtype)
    return out
```

```python
from contextlib import ExitStack

import concourse.bass as bass
from concourse import mybir

F32 = mybir.dt.float32
BF16 = mybir.dt.bfloat16
ALU = mybir.AluOpType
ACT = mybir.ActivationFunctionType
AX = mybir.AxisListType.X

P = 128
EPS = 1e-5
MASK_WEIGHT = 1000000.0


def decoder_layer(nc, x, ctx_in, mask, attn_w, attn_b, cross_w, cross_b, Wg, W1, b1, W2, b2, out):
    B, T, C = x.shape
    S2 = ctx_in.shape[1]
    H = 16
    DH = C // H
    CT = C // P
    NT = B * T // P
    TB = T // P
    E, _, HID = W1.shape
    HT = HID // P
    G = 4
    NG = H // G
    BLOCKS = B * NG
    HALF = 512
    UNITS = BLOCKS * (T // HALF)
    QT = HALF // P
    STACK = 6 * DH
    SCALE = float(DH) ** -0.5
    BLOCK_COLS = G * T

    with ExitStack() as scope:
        def sb(name, shape, dt=F32):
            return scope.enter_context(nc.sbuf_tensor(name, shape, dt))

        def sem(name):
            return scope.enter_context(nc.semaphore(name))

        def dram(name, shape, dt):
            return nc.dram_tensor(name, shape, dt).ap()

        qk_parts = dram("qk_parts", (2, 3, C, B * T), BF16)
        v_heads = dram("v_heads", (BLOCKS, T, G * 32), F32)
        shift_rows = dram("shift_rows", (2, 3 * G * QT, P), BF16)

        big = sb("big", [P, 2 * BLOCKS * BLOCK_COLS], BF16)
        q_stack = big[:, 0:BLOCKS * BLOCK_COLS]
        k_stack = big[:, BLOCKS * BLOCK_COLS:]
        big_f = big[:].bitcast(F32)
        xt = sb("xt", [P, CT, B * T])
        probs = xt[:].rearrange("p a t -> p (a t)").rearrange("p (s q) -> p s q", q=HALF)
        v_ring = sb("v_ring", [P, 2, T // P, G * 32])
        y = sb("y", [P, TB, BLOCKS, G * DH])
        x_sb = sb("x_sb", [P, NT, C])
        wt = sb("wt", [P, 8, CT, C])
        ident = sb("ident", [P, P])
        ident_b = sb("ident_b", [P, P], BF16)
        bias_col = sb("bias_col", [P, 4, CT])
        bias_row = sb("bias_row", [P, 2, C])
        o_sb = sb("o_sb", [P, HALF])
        alpha = sb("alpha", [P, 8])
        stat = sb("stat", [P, 2, G * QT])
        mparts = sb("mparts", [P, 2, P // (G * QT), G * QT], BF16)
        minus_one = sb("minus_one", [P, G * QT])
        mres = sb("mres", [P, 2, G * QT])
        m_rows = sb("m_rows", [P, 2, P], BF16)
        rsum = sb("rsum", [P, QT, G])
        head_mask = sb("head_mask", [P, P // DH])
        bn = sb("bn", [P, 4, 6])
        mv = sb("mv", [P, 4, 2])
        std = sb("std", [P, 4])

        y_flat = y[:].rearrange("p t n c -> p (t n c)")
        w_raw = y_flat.rearrange("p (m a c) -> p m a c", m=8, a=CT)
        resid = y_flat[:, 0:1024].rearrange("p (s q) -> p s q", s=2)
        split = y_flat[:, 1024:4096].bitcast(BF16).rearrange("p (s j q) -> p s j q", s=4, j=3)
        v_flat = v_ring[:].rearrange("p s k c -> p (s k c)")
        w_bin = v_flat.rearrange("p (m a c) -> p m a c", m=4, a=CT)
        v_stage = v_flat.rearrange("p (s k h d) -> p s k h d", s=2, k=2, h=H)

        psum = scope.enter_context(nc.psum_tensor("psum", [P, 8, 512], F32))

        pos = [0]

        def carve(n):
            pos[0] += n
            return big_f[:, pos[0] - n:pos[0]]

        w1_sb = carve(E * CT * HID).rearrange("p (e a h) -> p e a h", e=E, a=CT)
        q2t = carve(CT * B * T).rearrange("p (a t) -> p a t", a=CT)
        pt = carve(H * HALF).rearrange("p (h q) -> p h q", h=H)
        HB = P // DH
        k2bd = carve(B * CT * HB * S2).rearrange("p (b a k) -> p b a k", b=B, a=CT)
        v2 = carve(B * H * 32).rearrange("p (b h d) -> p b h d", b=B, h=H)
        ctx_sb = carve(B * C).rearrange("p (b c) -> p b c", b=B)
        ctx_t = carve(CT * B * S2).rearrange("p (a b k) -> p a b k", a=CT, b=B)
        k2t = carve(CT * B * S2).rearrange("p (a b k) -> p a b k", a=CT, b=B)
        bias2_row = carve(2 * C).rearrange("p (i c) -> p i c", i=2)
        mask_sb = carve(NT * S2).rearrange("p (t k) -> p t k", t=NT)
        sc = carve(2 * HB * S2).rearrange("p (s h k) -> p s h k", s=2, h=HB)
        pc = carve(2 * HB * S2).rearrange("p (s h k) -> p s h k", s=2, h=HB)
        mx2 = carve(2 * HB).rearrange("p (s h) -> p s h", s=2)
        o2_sb = carve(2 * HALF).rearrange("p (g q) -> p g q", g=2)
        yt = carve(2 * C).rearrange("p (s a q) -> p s a q", s=2, a=CT)
        assert pos[0] <= big_f.shape[1]
        pos[0] = E * CT * HID
        w2_sb = carve(E * HT * C).rearrange("p (e a c) -> p e a c", e=E, a=HT)
        b1_col = carve(E * HT).rearrange("p (e a) -> p e a", e=E)
        b2_sb = carve(C)
        wg_sb = carve(CT * E).rearrange("p (a e) -> p a e", a=CT)
        h_ring = carve(2 * HT * 512).rearrange("p (s a q) -> p s a q", s=2, a=HT)
        NR = 10
        route = carve(NR * NT * E).rearrange("p (n t e) -> p n t e", n=NR, t=NT)
        rowst = carve(8 * NT).rearrange("p (n t) -> p n t", n=8)
        score_t = carve(2 * P).rearrange("p (s q) -> p s q", s=2)

        s_ident, s_identb = sem("s_ident"), sem("s_identb")
        s_hm = sem("s_hm")
        ld_x, ld_w, ld_bias = sem("ld_x"), sem("ld_w"), sem("ld_bias")
        s_sign, s_bin = sem("s_sign"), sem("s_bin")
        s_ones = sem("s_ones")
        t_ready, t_evac = sem("t_ready"), sem("t_evac")
        qk_ready, hi_done, r_done, mid_done, lo_done = (sem(n) for n in ("qk_ready", "hi_done", "r_done", "mid_done", "lo_done"))
        part_stored = [sem(f"part_stored{i}") for i in range(4)]
        vp_ready, v_evac = sem("vp_ready"), sem("v_evac")
        v_stored = [sem(f"v_stored{i}") for i in range(2)]
        stack_loaded = sem("stack_loaded")
        v_loaded = [sem(f"v_loaded{i}") for i in range(2)]
        st_ready, exp_done, pv_done, o_copied = sem("st_ready"), sem("exp_done"), sem("pv_done"), sem("o_copied")
        sm_ready, sm_free, dve_own = sem("sm_ready"), sem("sm_free"), sem("dve_own")
        pool_own, parts_done = sem("pool_own"), sem("parts_done")
        rows_stored = sem("rows_stored")
        rows_loaded = [sem(f"rows_loaded{i}") for i in range(2)]
        x_biased = sem("x_biased")
        yt_ready, yt_evac, pj_ready, added, ln_done, xt_ready, xt_evac = (
            sem(n) for n in ("yt_ready", "yt_evac", "pj_ready", "added", "ln_done", "xt_ready", "xt_evac"))
        ld_ctx, c_ready, c_evac, kv_done = sem("ld_ctx"), sem("c_ready"), sem("c_evac"), sem("kv_done")
        q2_ready, q2_evac = sem("q2_ready"), sem("q2_evac")
        s2_ready, sc_done, mx_done, sub_done, exp2_done, ptr_ready, ptr_evac = (
            sem(n) for n in ("s2_ready", "sc_done", "mx_done", "sub_done", "exp2_done", "ptr_ready", "ptr_evac"))
        pv2_ready, o2_copied, ot_ready, y2_done = (sem(n) for n in ("pv2_ready", "o2_copied", "ot_ready", "y2_done"))
        mask_scaled, v2_ones = sem("mask_scaled"), sem("v2_ones")
        ld_w1, ld_w2 = sem("ld_w1"), sem("ld_w2")
        lg_ready, lg_sub, lg_exp, routed, st_t, st_c, b2_ready, b2_added = (
            sem(n) for n in ("lg_ready", "lg_sub", "lg_exp", "routed", "st_t", "st_c", "b2_ready", "b2_added"))
        h_ready, h_done, y_ready, y_added = sem("h_ready"), sem("h_done"), sem("y_ready"), sem("y_added")
        out_stored, stats_done, sqrt_done = sem("out_stored"), sem("stats_done"), sem("sqrt_done")

        x_tok = x.rearrange("b (t p) c -> p (b t) c", p=P)
        out_tok = out.rearrange("b (t p) c -> p (b t) c", p=P)

        SM_UNIT = G * QT + 2
        SM_FIRST = 2 * G * QT
        OT_POS, MT_POS = 4, 5

        def max_pos(i):
            return i if i < 4 else i + 2

        def sm_index(u, pos_, first):
            return u * SM_UNIT + (SM_FIRST + pos_ + (1 if first and pos_ < OT_POS else 0))

        def sm_slot(pos_, first):
            return (pos_ + (1 if first and pos_ < OT_POS else 0)) % 2

        ST_BANK, O_BANK = 4, 7

        def sm_tile(slot):
            return psum[:, 2 * slot:2 * slot + 2, :].rearrange("p a q -> p (a q)")

        def stack_ap(stack, n, rows, h, start, size):
            return stack[rows, bass.ds(n * BLOCK_COLS + (h * T + start), size)]

        block = scope.enter_context(nc.Block())

        @block.sync
        def _(sp):
            for g in range(4):
                sp.dma_start(x_sb[:, 4 * g:4 * g + 4, :], x_tok[:, 4 * g:4 * g + 4, :]).then_inc(ld_x, 16)
            for m, w in enumerate(attn_w + cross_w):
                sp.dma_start(w_raw[:, m], w.rearrange("(a p) c -> p a c", p=P)).then_inc(ld_w, 16)
            for i, b in enumerate((attn_b[0], attn_b[1], cross_b[0], cross_b[1])):
                sp.dma_start(bias_col[:, i, :], b.rearrange("(a p) -> p a", p=P),
                             allow_slow_non_contiguous=True).then_inc(ld_bias, 16)
            for i, b in enumerate((attn_b[2], attn_b[3])):
                sp.dma_start(bias_row[:, i, :], b.rearrange("(o c) -> o c", o=1).broadcast_to([P, C])).then_inc(ld_bias, 16)

            def store_parts(j):
                b, m, a, ch = j // 8, j // 4 % 2, j // 2 % 2, j % 2
                sp.wait_ge(lo_done, j + 1)
                t0 = b * T + ch * HALF
                sp.dma_start(qk_parts[m, :, a * P:(a + 1) * P, t0:t0 + HALF].rearrange("j o t -> o j t"),
                             split[:, j % 4]).then_inc(part_stored[j % 4], 16)

            def store_v(j):
                sp.wait_ge(v_evac, j + 1)
                b, t0 = j // 4, j % 4 * 2 * P
                for k in range(2):
                    sp.dma_start(
                        v_heads[b * NG:(b + 1) * NG, t0 + k * P:t0 + (k + 1) * P, :].rearrange("g p c -> p g c"),
                        v_stage[:, j % 2, k].rearrange("p (g h) d -> p g (h d)", g=NG)).then_inc(v_stored[j % 2], 16)

            def load_stacks(b):
                for s in range(4):
                    sp.wait_ge(part_stored[s], 32 * (b + 1))
                for m, stack, parts in ((0, q_stack, (0, 0, 0, 1, 1, 2)), (1, k_stack, (0, 1, 2, 0, 1, 0))):
                    for j, part in enumerate(parts):
                        dst = stack[DH * j:DH * (j + 1), b * NG * BLOCK_COLS:(b + 1) * NG * BLOCK_COLS]
                        sp.dma_start(dst.rearrange("d (h t) -> d h t", h=H),
                                     qk_parts[m, part, :, b * T:(b + 1) * T].rearrange("(h d) t -> d h t", d=DH)
                                     ).then_inc(stack_loaded, 16)

            for b in range(B):
                for j in range(8 * b, 8 * b + 8):
                    store_parts(j)
                load_stacks(b)
                for j in range(4 * b, 4 * b + 4):
                    store_v(j)

            def load_v(n, q):
                sp.dma_start(v_ring[:, q], v_heads[bass.ds(n, 1)].rearrange("o (k p) c -> p (o k) c", p=P)
                             ).then_inc(v_loaded[q], 16)

            def move_rows(n, q, u, pos_=MT_POS):
                sp.wait_ge(sm_free, sm_index(u - 1, pos_, False) + 1)
                sp.dma_start(shift_rows[q], m_rows[0:3 * G * QT, q]).then_inc(rows_stored, 16)
                sp.wait_ge(rows_stored, u * 16 + 16)
                dst = q_stack[STACK:STACK + 3, bass.ds(n * BLOCK_COLS, BLOCK_COLS)].rearrange("p (h t) -> p h t", h=G)
                sp.dma_start(dst[:, :, q * HALF:(q + 1) * HALF],
                             shift_rows[q].rearrange("(j h t) c -> j h (t c)", j=3, h=G)).then_inc(rows_loaded[q], 16)

            for s in range(2):
                sp.wait_ge(v_stored[s], 2 * 16 * 4)
            load_v(0, 0)
            sp.wait_ge(sm_free, SM_FIRST + 1)
            sp.dma_start(shift_rows[0], m_rows[0:3 * G * QT, 0]).then_inc(rows_stored, 16)
            sp.wait_ge(rows_stored, 16)
            sp.dma_start(q_stack[STACK:STACK + 3, 0:BLOCK_COLS].rearrange("p (h t) -> p h t", h=G)[:, :, 0:HALF],
                         shift_rows[0].rearrange("(j h t) c -> j h (t c)", j=3, h=G)).then_inc(rows_loaded[0], 16)

            def units(n, first=False, last=False):
                if not first:
                    sp.wait_ge(pv_done, n * 16)
                load_v(n, 1)
                move_rows(n, 1, n * 2 + 1, 1 if last else MT_POS)
                if not last:
                    sp.wait_ge(pv_done, n * 16 + 8)
                    load_v(n + 1, 0)
                    move_rows(n + 1, 0, n * 2 + 2)

            units(0, first=True)
            with sp.Fori(1, BLOCKS - 1) as n:
                units(n)
            units(BLOCKS - 1, last=True)

            sp.wait_ge(pv_done, 8 * UNITS)
            for b in range(B):
                sp.dma_start(ctx_sb[0:S2, b, :], ctx_in[b]).then_inc(ld_ctx, 16)
            sp.dma_start(mask_sb[:, :, :], mask.rearrange("b o (t p) k -> p (b o t) k", p=P)).then_inc(ld_ctx, 16)
            for i, b in enumerate((cross_b[2], cross_b[3])):
                sp.dma_start(bias2_row[:, i, :], b.rearrange("(o c) -> o c", o=1).broadcast_to([P, C])).then_inc(ld_ctx, 16)
            for e in range(E):
                sp.dma_start(w1_sb[:, e], W1[e].rearrange("(a p) h -> p a h", p=P)).then_inc(ld_w1, 16)
            sp.wait_ge(pj_ready, 2 * NT)
            sp.wait_ge(y2_done, NT)
            sp.wait_ge(yt_evac, 2 * NT)
            sp.dma_start(wg_sb, Wg.rearrange("(a p) e -> p a e", p=P)).then_inc(ld_w2, 16)
            sp.dma_start(b1_col, b1.rearrange("e (a p) -> p e a", p=P), allow_slow_non_contiguous=True).then_inc(ld_w2, 16)
            sp.dma_start(b2_sb[0:E, :], b2).then_inc(ld_w2, 16)
            for e in range(E):
                sp.dma_start(w2_sb[:, e], W2[e].rearrange("(a p) c -> p a c", p=P)).then_inc(ld_w2, 16)
            for g in range(NT):
                sp.wait_ge(ln_done, 2 * NT + g + 1)
                sp.dma_start(out_tok[:, g:g + 1, :], x_sb[:, g:g + 1, :]).then_inc(out_stored, 16)
            sp.wait_ge(out_stored, 16 * NT)

        @block.gpsimd
        def _(pool):
            own = [0]

            def link(ins):
                own[0] += 1
                ins.then_inc(pool_own, 1)
                pool.wait_ge(pool_own, own[0])

            link(nc.gpsimd.memset(ident[:], 0.0))
            nc.gpsimd.affine_select(out=ident[:], in_=ident[:], compare_op=ALU.not_equal, fill=1.0, base=0,
                                    pattern=[[-1, P]], channel_multiplier=1).then_inc(s_ident, 1)
            pool.wait_ge(s_ident, 1)
            nc.gpsimd.tensor_copy(ident_b[:], ident[:]).then_inc(s_identb, 1)
            link(nc.gpsimd.memset(head_mask[:], SCALE))
            link(nc.gpsimd.affine_select(out=head_mask[:], in_=head_mask[:], compare_op=ALU.is_ge, fill=0.0, base=0,
                                         pattern=[[-DH, P // DH]], channel_multiplier=1))
            nc.gpsimd.affine_select(out=head_mask[:], in_=head_mask[:], compare_op=ALU.is_ge, fill=0.0, base=DH - 1,
                                    pattern=[[DH, P // DH]], channel_multiplier=-1).then_inc(s_hm, 1)
            link(nc.gpsimd.memset(minus_one[:], -1.0))
            link(nc.gpsimd.memset(mparts[:], 0.0))
            nc.gpsimd.memset(k_stack[STACK:STACK + 3, :], 1.0).then_inc(s_ones, 1)
            pool.wait_ge(s_ones, 1)
            pool.wait_ge(t_ready, 8)
            pool.wait_ge(ld_bias, 6 * 16)
            for t in range(NT):
                nc.gpsimd.tensor_tensor(x_sb[:, t, :], x_sb[:, t, :], bias_row[:, 1, :], ALU.add).then_inc(x_biased, 1)

            def shifts(q, u, rounds, mt_done=None):
                pool.wait_ge(sm_free, mt_done)
                base = own[0]
                m, a, r = stat[:, q], mparts[:, q], mres[:, q]
                nc.gpsimd.tensor_tensor(a[:, 0], m, minus_one[:], ALU.mult).then_inc(pool_own, 1)
                pool.wait_ge(pool_own, rounds + 1)
                nc.gpsimd.tensor_tensor(r, m, a[:, 0], ALU.add).then_inc(pool_own, 1)
                pool.wait_ge(pool_own, rounds + 2)
                nc.gpsimd.tensor_tensor(a[:, 1], r, minus_one[:], ALU.mult).then_inc(pool_own, 1)
                pool.wait_ge(pool_own, rounds + 3)
                nc.gpsimd.tensor_tensor(r, r, a[:, 1], ALU.add).then_inc(pool_own, 1)
                pool.wait_ge(pool_own, rounds + 4)
                nc.gpsimd.tensor_tensor(a[:, 2], r, minus_one[:], ALU.mult).then_inc(parts_done, 1)

            start = own[0]
            shifts(0, 0, start, mt_done=G * QT)
            shifts(1, 1, start + 4, mt_done=2 * G * QT)

            def block_shifts(n, first=False):
                for q in range(2):
                    u = n * 2 + q
                    shifts(q, u + 2, n * 8 + (start + 8 + 4 * q),
                           mt_done=sm_index(u, max_pos(G * QT - 1), first and q == 0) + 1)

            block_shifts(0, first=True)
            with pool.Fori(1, BLOCKS - 1) as n:
                block_shifts(n)
            own[0] = start + 8 + 8 * (BLOCKS - 1)

            pool.wait_ge(ld_ctx, 16 * (B + 3))
            pool.wait_ge(pv_done, 8 * UNITS)
            nc.gpsimd.tensor_scalar(mask_sb[:, :, :], mask_sb[:, :, :], -MASK_WEIGHT, None, ALU.mult).then_inc(mask_scaled, 1)
            nc.gpsimd.memset(v2[:, :, :, DH:32], 1.0).then_inc(v2_ones, 1)
            for t in range(NT):
                pool.wait_ge(xt_ready, t + 1)
                nc.gpsimd.tensor_tensor(x_sb[:, t, :], x_sb[:, t, :], bias2_row[:, 1, :], ALU.add).then_inc(x_biased, 1)
            for j in range(2 * NT):
                pool.wait_ge(mx_done, j + 1)
                if j >= 2:
                    pool.wait_ge(exp2_done, j - 1)
                nc.gpsimd.tensor_tensor(pc[:, j % 2], sc[:, j % 2],
                                        mx2[:, j % 2, :].unsqueeze(2).broadcast_to([P, HB, S2]), ALU.subtract).then_inc(sub_done, 1)

        @block.scalar
        def _(act):
            act.wait_ge(ld_w, 16 * 8)
            nc.scalar.activation(w_bin[:, :, :, :], w_raw[:, 0:4], ACT.Sign).then_inc(s_sign, 1)
            act.wait_ge(ld_bias, 6 * 16)
            for k in range(16):
                act.wait_ge(t_ready, k + 1)
                if k < 8:
                    a, g = k // 4, k % 4
                    dst = xt[:, a, 512 * g:512 * (g + 1)]
                    src = psum[:, k % 4, :]
                else:
                    m = (k - 8 + 4) % 8
                    dst = wt[:, m]
                    src = psum[:, k % 4, :].rearrange("p (a o) -> p a o", a=CT)
                nc.scalar.copy(dst, src).then_inc(t_evac, 1)

            def mid(j):
                act.wait_ge(r_done, j + 1)
                nc.scalar.copy(split[:, j % 4, 1], resid[:, j % 2]).then_inc(mid_done, 1)

            for j in range(16):
                m, a = j // 4 % 2, j // 2 % 2
                act.wait_ge(qk_ready, j + 1)
                if j >= 4:
                    act.wait_ge(part_stored[j % 4], 16 * (j // 4))
                nc.scalar.activation(split[:, j % 4, 0], psum[:, 4 + j % 4, :], ACT.Identity,
                                     bias=bias_col[:, m, a:a + 1]).then_inc(hi_done, 1)
                if j >= 1:
                    mid(j - 1)
            mid(15)

            def copy_o(u):
                act.wait_ge(pv_done, u * 8 + 8)
                nc.scalar.copy(o_sb[:], psum[:, O_BANK, :]).then_inc(o_copied, 1)

            def exps(n, q, first=False, pos_=OT_POS):
                u = n * 2 + q
                for kt in range(TB):
                    for h in range(G):
                        i = kt * G + h
                        act.wait_ge(st_ready, u * 32 + (i + 1))
                        if h == 0 and not (first and kt < 2):
                            act.wait_ge(pv_done, u * 8 + (kt - 1))
                        nc.scalar.activation(probs[:, kt % 2 * G + h, :], psum[:, ST_BANK + i % 3, :], ACT.Exp,
                                             scale=SCALE).then_inc(exp_done, 1)
                    if kt == 0 and not first:
                        if not (isinstance(n, int) and n == 0):
                            act.wait_ge(sm_ready, sm_index(u - 1, pos_, False) + 1)
                        copy_o(u - 1)

            exps(0, 0, first=True)
            exps(0, 1)
            with act.Fori(1, BLOCKS - 1) as n:
                exps(n, 0)
                exps(n, 1)
            exps(BLOCKS - 1, 0)
            exps(BLOCKS - 1, 1, pos_=0)
            act.wait_ge(sm_ready, sm_index(UNITS - 2, 2, False) + 1)
            copy_o(UNITS - 1)

            def norm_sqrt(k):
                act.wait_ge(stats_done, k + 1)
                nc.scalar.activation(std[:, k % 4:k % 4 + 1], mv[:, k % 4, 1:2], ACT.Sqrt, bias=EPS).then_inc(sqrt_done, 1)

            def proj_copies(stage):
                base = stage * NT
                for t in range(NT + 2):
                    if t < NT:
                        act.wait_ge(yt_ready, base + t + 1)
                        if base + t >= 2:
                            act.wait_ge(pj_ready, base + t - 1)
                        nc.scalar.copy(yt[:, t % 2], psum[:, t % 2, 0:C].rearrange("p (a q) -> p a q", a=CT)).then_inc(yt_evac, 1)
                    if 1 <= t <= NT:
                        norm_sqrt(base + t - 1)
                    if t >= 2:
                        act.wait_ge(xt_ready, base + t - 1)
                        nc.scalar.copy(xt[:, :, (t - 2) * P:(t - 1) * P],
                                       psum[:, 4 + t % 2, 0:C].rearrange("p (a q) -> p a q", a=CT)).then_inc(xt_evac, 1)

            proj_copies(0)

            act.wait_ge(c_ready, 1)
            nc.scalar.copy(ctx_t[:, :, :, :], psum[:, 6, 0:CT * B * S2].rearrange("p (a b k) -> p a b k", a=CT, b=B)).then_inc(c_evac, 1)
            for a in range(CT):
                act.wait_ge(c_ready, 2 + a)
                nc.scalar.activation(k2t[:, a], psum[:, 7 if a else 6, 0:B * S2].rearrange("p (b k) -> p b k", b=B),
                                     ACT.Identity, bias=bias_col[:, 3, a:a + 1]).then_inc(c_evac, 1)
            for j in range(8):
                a, ch = j // 4, j % 4
                act.wait_ge(q2_ready, j + 1)
                nc.scalar.activation(q2t[:, a, 512 * ch:512 * (ch + 1)], psum[:, j % 4, :], ACT.Identity,
                                     bias=bias_col[:, 2, a:a + 1]).then_inc(q2_evac, 1)

            def cross_exp(j):
                act.wait_ge(sub_done, j + 1)
                nc.scalar.activation(pc[:, j % 2], pc[:, j % 2], ACT.Exp).then_inc(exp2_done, 1)

            def pt_copies(j):
                c, tq, a = j // 8, j % 8 // 2, j % 2
                for s in range(2):
                    act.wait_ge(ptr_ready, 2 * j + s + 1)
                    if tq == 0 and a == 0 and c >= 1:
                        act.wait_ge(pv2_ready, 4 * c)
                    nc.scalar.copy(pt[0:S2, a * HB + 4 * s:a * HB + 4 * s + 4, tq * P:(tq + 1) * P],
                                   psum[0:S2, 4 + s, :].rearrange("k (h q) -> k h q", h=4)).then_inc(ptr_evac, 1)

            def cross_out(c):
                for g in range(NG):
                    k = NG * c + g
                    act.wait_ge(pv2_ready, k + 1)
                    if k >= 2:
                        act.wait_ge(ot_ready, k - 1)
                    nc.scalar.copy(o2_sb[:, g % 2], psum[:, 6 + g % 2, :]).then_inc(o2_copied, 1)

            for j in range(2 * NT + 1):
                if j < 2 * NT:
                    cross_exp(j)
                if j >= 1:
                    pt_copies(j - 1)
                    if j % 8 == 0:
                        cross_out(j // 8 - 1)

            proj_copies(1)

            act.wait_ge(lg_sub, 1)
            nc.scalar.activation(route[:, 1], route[:, 0], ACT.Exp).then_inc(lg_exp, 1)
            act.wait_ge(ld_w2, 16 * (3 + E))
            k = 0
            for c in range(4):
                for e in range(E):
                    if e == 1 and c >= 1:
                        for t in range(4 * c - 4, 4 * c):
                            norm_sqrt(2 * NT + t)
                    for a in range(HT):
                        act.wait_ge(h_ready, k * HT + a + 1)
                        if k >= 2:
                            act.wait_ge(y_ready, 4 * (k - 1))
                        nc.scalar.activation(h_ring[:, k % 2, a, :], psum[:, a, :], ACT.Relu,
                                             bias=b1_col[:, e, a:a + 1]).then_inc(h_done, 1)
                    k += 1
            for t in range(NT - 4, NT):
                norm_sqrt(2 * NT + t)

        @block.vector
        def _(dve):
            own = [0]

            def link(ins):
                own[0] += 1
                ins.then_inc(dve_own, 1)
                dve.wait_ge(dve_own, own[0])

            dve.wait_ge(ld_w, 16 * 8)
            link(nc.vector.tensor_reduce(alpha[:], w_raw[:, 0:4].rearrange("p m a c -> p (m a) c"), AX, ALU.add,
                                         apply_absolute_value=True))
            link(nc.vector.tensor_scalar(alpha[:], alpha[:], 1.0 / C, None, ALU.mult))
            dve.wait_ge(s_sign, 1)
            link(nc.vector.tensor_tensor(w_bin[:, :, :, :], w_bin[:, :, :, :], w_raw[:, 0:4], ALU.subtract))
            link(nc.vector.tensor_tensor(w_bin[:, :, :, :], w_bin[:, :, :, :], w_raw[:, 0:4], ALU.add))
            nc.vector.tensor_tensor(v_flat.rearrange("p (m c) -> p m c", c=C), v_flat.rearrange("p (m c) -> p m c", c=C),
                                    alpha[:].unsqueeze(2).broadcast_to([P, 8, C]), ALU.mult).then_inc(s_bin, 1)
            dve.wait_ge(ld_bias, 6 * 16)

            def lo(j):
                dve.wait_ge(mid_done, j + 1)
                nc.vector.tensor_tensor(split[:, j % 4, 2], resid[:, j % 2], split[:, j % 4, 1], ALU.subtract).then_inc(lo_done, 1)

            def v_out(j):
                if j == 0:
                    dve.wait_ge(t_ready, 16)
                    link(nc.vector.memset(v_stage[:, :, :, :, DH:32], 1.0))
                dve.wait_ge(vp_ready, j + 1)
                if j >= 2:
                    dve.wait_ge(v_stored[j % 2], 32 * (j // 2))
                nc.vector.tensor_tensor(
                    v_stage[:, j % 2, :, :, 0:DH], psum[:, j % 4, :].rearrange("p (k h d) -> p k h d", k=2, h=H),
                    bias_row[:, 0, :].rearrange("p (h d) -> p h d", h=H).unsqueeze(1).broadcast_to([P, 2, H, DH]),
                    ALU.add).then_inc(v_evac, 1)

            for b in range(B):
                for j in range(8 * b, 8 * b + 8):
                    m, a = j // 4 % 2, j // 2 % 2
                    dve.wait_ge(hi_done, j + 1)
                    if j >= 2:
                        dve.wait_ge(lo_done, j - 1)
                    nc.vector.scalar_tensor_tensor(out=resid[:, j % 2], in0=psum[:, 4 + j % 4, :], scalar=bias_col[:, m, a:a + 1],
                                                   in1=split[:, j % 4, 0], op0=ALU.add, op1=ALU.subtract).then_inc(r_done, 1)
                    if j >= 8 * b + 1:
                        lo(j - 1)
                lo(8 * b + 7)
                for j in range(4 * b, 4 * b + 4):
                    v_out(j)

            def row_max(q, i, k, slot, parts, last=None):
                dve.wait_ge(sm_ready, k + 1)
                if parts is not None:
                    dve.wait_ge(parts_done, parts)
                nc.vector.reduce_max(stat[:, q, i:i + 1], sm_tile(slot), AX).then_inc(sm_free, 1)

            def shift_row(q, k, slot):
                dve.wait_ge(sm_ready, k + 1)
                rows = psum[0:3 * G * QT, 2 * slot, :].bitcast(BF16)[:, 0:P]
                nc.vector.tensor_copy(m_rows[0:3 * G * QT, q], rows).then_inc(sm_free, 1)

            def normalise(n, q, k, slot, own_value):
                dve.wait_ge(sm_ready, k + 1)
                o = psum[:, 2 * slot, :].rearrange("p (t h d) -> p t h d", t=QT, h=G)
                nc.vector.reciprocal(rsum[:], o[:, :, :, DH]).then_inc(dve_own, 1)
                dve.wait_ge(dve_own, own_value + 1)
                dst = y[:, q * QT:(q + 1) * QT, bass.ds(n, 1), :]
                nc.vector.tensor_tensor(dst.rearrange("p t n (h d) -> p t (n h) d", h=G), o[:, :, :, 0:DH],
                                        rsum[:].unsqueeze(3).broadcast_to([P, QT, G, DH]), ALU.mult).then_inc(sm_free, 1)

            for u in range(2):
                for i in range(G * QT):
                    row_max(u, i, u * G * QT + i, i % 2, None)
            shift_row(0, SM_FIRST, 0)
            start = own[0]

            def unit_dve(n, q, first=False, maxima=True, rows=True):
                u = n * 2 + q
                for kt in range(TB):
                    if kt == 2:
                        if not first:
                            normalise(n if q else n - 1, 1 - q, sm_index(u, OT_POS, False), sm_slot(OT_POS, False), u + (start - 1))
                        if rows:
                            if not first:
                                dve.wait_ge(rows_stored, u * 16)
                            shift_row(1 - q, sm_index(u, MT_POS, first), sm_slot(MT_POS, first))
                    if maxima:
                        for i in (2 * kt, 2 * kt + 1):
                            row_max(q, i, sm_index(u, max_pos(i), first), sm_slot(max_pos(i), first), u + 1)

            unit_dve(0, 0, first=True)
            unit_dve(0, 1)
            with dve.Fori(1, BLOCKS - 1) as n:
                unit_dve(n, 0)
                unit_dve(n, 1)
            k0 = sm_index(UNITS - 2, 0, False)
            normalise(BLOCKS - 2, 1, k0, 0, start + UNITS - 3)
            dve.wait_ge(rows_stored, 16 * (UNITS - 2))
            shift_row(1, k0 + 1, 1)
            normalise(BLOCKS - 1, 0, k0 + 2, 0, start + UNITS - 2)
            dve.wait_ge(sm_free, k0 + 3)
            normalise(BLOCKS - 1, 1, k0 + 3, 1, start + UNITS - 1)
            own[0] = start + UNITS

            def norm_stats(t, k):
                if k >= 4:
                    dve.wait_ge(ln_done, k - 3)
                link(nc.vector.bn_stats(bn[:, k % 4], x_sb[:, t, :]))
                nc.vector.bn_aggr(mv[:, k % 4], bn[:, k % 4]).then_inc(stats_done, 1)

            def norm_apply(t, k):
                dve.wait_ge(sqrt_done, k + 1)
                link(nc.vector.reciprocal(std[:, k % 4:k % 4 + 1], std[:, k % 4:k % 4 + 1]))
                nc.vector.tensor_scalar(x_sb[:, t, :], x_sb[:, t, :], mv[:, k % 4, 0:1], std[:, k % 4:k % 4 + 1],
                                        ALU.subtract, ALU.mult).then_inc(ln_done, 1)

            def residual(stage):
                for t in range(NT + 1):
                    k = stage * NT + t
                    if t < NT:
                        dve.wait_ge(pj_ready, k + 1)
                        dve.wait_ge(x_biased, k + 1)
                        nc.vector.tensor_tensor(x_sb[:, t, :], x_sb[:, t, :], psum[:, 2 + t % 2, 0:C], ALU.add).then_inc(added, 1)
                        dve.wait_ge(added, k + 1)
                        norm_stats(t, k)
                    if t >= 1:
                        norm_apply(t - 1, k - 1)

            residual(0)

            dve.wait_ge(s_hm, 1)
            for b in range(B):
                for a in range(CT):
                    dve.wait_ge(c_evac, 2 + a)
                    nc.vector.tensor_tensor(k2bd[:, b, a].rearrange("p (h k) -> p h k", h=HB),
                                            k2t[:, a, b].unsqueeze(1).broadcast_to([P, HB, S2]),
                                            head_mask[:].unsqueeze(2).broadcast_to([P, HB, S2]), ALU.mult).then_inc(kv_done, 1)
            dve.wait_ge(ld_ctx, 16 * (B + 3))
            for b in range(B):
                dve.wait_ge(c_ready, 2 + CT + b)
                nc.vector.tensor_tensor(v2[0:S2, b, :, 0:DH], psum[0:S2, 4 + b, 0:C].rearrange("p (h d) -> p h d", h=H),
                                        bias2_row[0:S2, 0, :].rearrange("p (h d) -> p h d", h=H), ALU.add).then_inc(kv_done, 1)
            dve.wait_ge(mask_scaled, 1)

            def cross_scores(j):
                t = j // 2
                dve.wait_ge(s2_ready, j + 1)
                if j >= 2:
                    dve.wait_ge(sub_done, j - 1)
                nc.vector.tensor_tensor(
                    out=sc[:, j % 2].rearrange("p (b h) k -> p b h k", b=2),
                    in0=psum[:, 2 * (j % 2):2 * (j % 2) + 2, 0:HB // 2 * S2].rearrange("p b (h k) -> p b h k", k=S2),
                    in1=mask_sb[:, t, :].unsqueeze(1).unsqueeze(1).broadcast_to([P, 2, HB // 2, S2]),
                    op=ALU.add).then_inc(sc_done, 1)
                dve.wait_ge(sc_done, j + 1)
                nc.vector.reduce_max(mx2[:, j % 2, :], sc[:, j % 2], AX).then_inc(mx_done, 1)

            def cross_norm(c):
                for g in range(NG):
                    k = NG * c + g
                    dve.wait_ge(ot_ready, k + 1)
                    if k >= 1:
                        dve.wait_ge(y2_done, k)
                    o = psum[:, 4 + g % 2, :].rearrange("p (t h d) -> p t h d", t=QT, h=G)
                    link(nc.vector.reciprocal(rsum[:], o[:, :, :, DH]))
                    b, half = c // 2, c % 2
                    nc.vector.tensor_tensor(y[:, half * QT:(half + 1) * QT, b * NG + g, :].rearrange("p t (h d) -> p t h d", h=G),
                                            o[:, :, :, 0:DH], rsum[:].unsqueeze(3).broadcast_to([P, QT, G, DH]), ALU.mult).then_inc(y2_done, 1)

            for j in range(2 * NT + 1):
                if j < 2 * NT:
                    cross_scores(j)
                if j >= 1 and j % 8 == 0:
                    cross_norm(j // 8 - 1)

            residual(1)

            dve.wait_ge(lg_ready, 1)
            lg = psum[:, 6, 0:NT * E].rearrange("p (t e) -> p t e", e=E)

            def bc(v):
                return v.unsqueeze(2).broadcast_to([P, NT, E])

            rank = route[:, 9]
            for e in range(E):
                link(nc.vector.memset(rank[:, :, e:e + 1], float(E - e)))
            link(nc.vector.reduce_max(rowst[:, 0], lg, AX))
            nc.vector.tensor_tensor(route[:, 0], lg, bc(rowst[:, 0]), ALU.subtract).then_inc(lg_sub, 1)
            dve.wait_ge(lg_exp, 1)
            link(nc.vector.reduce_sum(rowst[:, 1], route[:, 1], AX))
            link(nc.vector.reciprocal(rowst[:, 2], rowst[:, 1]))
            link(nc.vector.tensor_tensor(route[:, 2], route[:, 1], bc(rowst[:, 2]), ALU.mult))
            for i in range(2):
                pr = route[:, 2 if i == 0 else 5]
                one = route[:, 3 if i == 0 else 6]
                link(nc.vector.reduce_max(rowst[:, 3 + i], pr, AX))
                link(nc.vector.tensor_tensor(one, pr, bc(rowst[:, 3 + i]), ALU.is_equal))
                link(nc.vector.tensor_tensor(one, one, rank, ALU.mult))
                link(nc.vector.reduce_max(rowst[:, 5], one, AX))
                link(nc.vector.tensor_tensor(one, one, bc(rowst[:, 5]), ALU.is_equal))
                if i == 0:
                    link(nc.vector.scalar_tensor_tensor(out=route[:, 5], in0=one, scalar=-2.0, in1=pr, op0=ALU.mult, op1=ALU.add))
            link(nc.vector.tensor_tensor(rowst[:, 6], rowst[:, 3], rowst[:, 4], ALU.add))
            link(nc.vector.reciprocal(rowst[:, 7], rowst[:, 6]))
            link(nc.vector.tensor_tensor(route[:, 3], route[:, 3], bc(rowst[:, 3]), ALU.mult))
            link(nc.vector.tensor_tensor(route[:, 6], route[:, 6], bc(rowst[:, 4]), ALU.mult))
            link(nc.vector.tensor_tensor(route[:, 3], route[:, 3], route[:, 6], ALU.add))
            nc.vector.tensor_tensor(route[:, 8], route[:, 3], bc(rowst[:, 7]), ALU.mult).then_inc(routed, 1)
            dve.wait_ge(routed, 1)
            score = route[:, 8]
            for t in range(NT):
                dve.wait_ge(st_t, t + 1)
                nc.vector.tensor_copy(score_t[0:E, t % 2, :], psum[0:E, 4 + t % 2, 0:P]).then_inc(st_c, 1)
                dve.wait_ge(b2_ready, t + 1)
                nc.vector.tensor_tensor(x_sb[:, t, :], x_sb[:, t, :], psum[:, 6 + t % 2, 0:C], ALU.add).then_inc(b2_added, 1)
            dve.wait_ge(b2_added, NT)
            k = 0
            for c in range(4):
                for e in range(E):
                    for tq in range(4):
                        t = 4 * c + tq
                        dve.wait_ge(y_ready, k + 1)
                        if e >= 1:
                            dve.wait_ge(y_added, k - 3)
                        nc.vector.scalar_tensor_tensor(out=x_sb[:, t, :], in0=psum[:, 4 + k % 4, 0:C], scalar=score[:, t, e:e + 1],
                                                       in1=x_sb[:, t, :], op0=ALU.mult, op1=ALU.add).then_inc(y_added, 1)
                        k += 1
                    if e == 0 and c >= 1:
                        for tq in range(4):
                            norm_apply(4 * c - 4 + tq, 2 * NT + 4 * c - 4 + tq)
                for tq in range(4):
                    t = 4 * c + tq
                    dve.wait_ge(y_added, k)
                    norm_stats(t, 2 * NT + t)
            for t in range(NT - 4, NT):
                norm_apply(t, 2 * NT + t)

        @block.tensor
        def _(pe):
            pe.wait_ge(s_ident, 1)
            pe.wait_ge(s_identb, 1)
            for k in range(16):
                if k >= 4:
                    pe.wait_ge(t_evac, k - 3)
                if k < 8:
                    a, g = k // 4, k % 4
                    pe.wait_ge(ld_x, 16 * 4)
                    for i in range(4):
                        mm = pe.transpose(psum[:, k % 4, i * P:(i + 1) * P], x_sb[:, 4 * g + i, a * P:(a + 1) * P], ident[:])
                else:
                    m = (k - 8 + 4) % 8
                    pe.wait_ge(ld_w, 16 * 8)
                    if m < 4:
                        pe.wait_ge(s_bin, 1)
                    src = w_bin[:, m] if m < 4 else w_raw[:, m]
                    for a in range(CT):
                        for o in range(CT):
                            mm = pe.transpose(psum[:, k % 4, (a * CT + o) * P:(a * CT + o + 1) * P],
                                              src[:, o, a * P:(a + 1) * P], ident[:])
                mm.then_inc(t_ready, 1)
            pe.wait_ge(t_evac, 16)
            for b in range(B):
                for j in range(8 * b, 8 * b + 8):
                    m, o, ch = j // 4 % 2, j // 2 % 2, j % 2
                    if j >= 4:
                        pe.wait_ge(r_done, j - 3)
                    t0 = b * T + ch * HALF
                    for a in range(CT):
                        mm = pe.matmul(psum[:, 4 + j % 4, :], wt[:, m, a, o * P:(o + 1) * P], xt[:, a, t0:t0 + HALF],
                                       start=(a == 0), stop=(a == CT - 1))
                    mm.then_inc(qk_ready, 1)
                for j in range(4 * b, 4 * b + 4):
                    if j >= 4:
                        pe.wait_ge(v_evac, j - 3)
                    for k in range(2):
                        t0 = (2 * j + k) * P
                        for a in range(CT):
                            mm = pe.matmul(psum[:, j % 4, k * C:(k + 1) * C], xt[:, a, t0:t0 + P], wt[:, 2, a, :],
                                           start=(a == 0), stop=(a == CT - 1))
                    mm.then_inc(vp_ready, 1)

            def max_tile(n, i, k, slot, free):
                h, t = i // QT, i % QT
                if free is not None:
                    pe.wait_ge(sm_free, free)
                q = max_q[0]
                for c in range(T // 512):
                    mm = pe.matmul(psum[:, 2 * slot + c, :], stack_ap(q_stack, n, slice(0, STACK), h, q * HALF + t * P, P),
                                   stack_ap(k_stack, n, slice(0, STACK), h, c * 512, 512), start=True, stop=True)
                mm.then_inc(sm_ready, 1)

            max_q = [0]

            def shift_tile(q, k, slot, parts):
                pe.wait_ge(parts_done, parts)
                pe.wait_ge(sm_free, k - 1)
                dst = psum[:, 2 * slot, :].bitcast(BF16)[:, 0:P]
                pe.transpose(dst, mparts[:, q].rearrange("p j c -> p (j c)"), ident_b[:]).then_inc(sm_ready, 1)

            def out_tile(k, slot, copied):
                pe.wait_ge(o_copied, copied)
                pe.wait_ge(sm_free, k - 1)
                for t in range(QT):
                    mm = pe.transpose(psum[:, 2 * slot, t * P:(t + 1) * P], o_sb[:, t * P:(t + 1) * P], ident[:])
                mm.then_inc(sm_ready, 1)

            def scores(n, q, kt, first):
                u = n * 2 + q
                if kt == 0:
                    pe.wait_ge(rows_loaded[q], n * 16 + 16)
                for h in range(G):
                    i = kt * G + h
                    if i >= 3:
                        pe.wait_ge(exp_done, u * 32 + (i - 2))
                    elif not first:
                        pe.wait_ge(exp_done, u * 32 + (-1, 0, -2)[i])
                    pe.matmul(psum[:, ST_BANK + i % 3, :], stack_ap(k_stack, n, slice(0, STACK + 3), h, kt * P, P),
                              stack_ap(q_stack, n, slice(0, STACK + 3), h, q * HALF, HALF), start=True, stop=True).then_inc(st_ready, 1)

            def values(n, q, kt, first):
                u = n * 2 + q
                pe.wait_ge(exp_done, u * 32 + (4 * kt + 4))
                if kt == 0:
                    pe.wait_ge(v_loaded[q], n * 16 + 16)
                    if not first:
                        pe.wait_ge(o_copied, u)
                for h in range(G):
                    mm = pe.matmul(psum[32 * h:32 * h + 32, O_BANK, :], v_ring[:, q, kt, 32 * h:32 * h + 32],
                                   probs[:, kt % 2 * G + h, :], start=(kt == 0), stop=(kt == TB - 1))
                mm.then_inc(pv_done, 1)

            pe.wait_ge(r_done, 16)
            pe.wait_ge(v_evac, 8)
            pe.wait_ge(stack_loaded, 16 * 12 * B)
            pe.wait_ge(s_ones, 1)
            for u in range(2):
                max_q[0] = u
                for i in range(G * QT):
                    k = u * G * QT + i
                    max_tile(0, i, k, i % 2, k - 1 if k >= 2 else None)
            shift_tile(0, SM_FIRST, 0, 1)

            def unit_pe(n, q, first=False, maxima=True, rows=True, k0=None):
                u = n * 2 + q
                for kt in range(TB):
                    scores(n, q, kt, first)
                    if kt == 2:
                        k = sm_index(u, OT_POS, first) if k0 is None else k0
                        if not first:
                            out_tile(k, sm_slot(OT_POS, first) if k0 is None else k0 % 2, u)
                        if rows:
                            k = k + 1
                            shift_tile(1 - q, k, sm_slot(MT_POS, first) if k0 is None else (k0 + 1) % 2, u + 2)
                    if maxima:
                        max_q[0] = q
                        for i in (2 * kt, 2 * kt + 1):
                            k = sm_index(u, max_pos(i), first)
                            max_tile(n + 1, i, k, sm_slot(max_pos(i), first), k - 1)
                    if kt >= 1:
                        values(n, q, kt - 1, first)
                    elif not first:
                        values(n if q else n - 1, 1 - q, TB - 1, False)

            unit_pe(0, 0, first=True)
            unit_pe(0, 1)
            with pe.Fori(1, BLOCKS - 1) as n:
                unit_pe(n, 0)
                unit_pe(n, 1)
            k0 = sm_index(UNITS - 2, 0, False)
            unit_pe(BLOCKS - 1, 0, maxima=False, k0=k0)
            unit_pe(BLOCKS - 1, 1, maxima=False, rows=False, k0=k0 + 2)
            values(BLOCKS - 1, 1, TB - 1, False)
            out_tile(k0 + 3, 1, UNITS)

            def project(stage):
                base, m = stage * NT, 3 + 4 * stage
                if stage == 0:
                    pe.wait_ge(sm_free, k0 + 4)
                    pe.wait_ge(exp_done, 32 * UNITS)
                else:
                    pe.wait_ge(y2_done, 4 * NG)
                for t in range(NT + 2):
                    k = base + t
                    b, tt = t // TB, t % TB
                    if t < NT:
                        if k >= 2:
                            pe.wait_ge(yt_evac, k - 1)
                        for a in range(CT):
                            mm = pe.transpose(psum[:, t % 2, a * P:(a + 1) * P],
                                              y[:, tt, b * NG + 2 * a:b * NG + 2 * a + 2, :].rearrange("p n c -> p (n c)"), ident[:])
                        mm.then_inc(yt_ready, 1)
                        pe.wait_ge(yt_evac, k + 1)
                        if k >= 2:
                            pe.wait_ge(added, k - 1)
                        for a in range(CT):
                            mm = pe.matmul(psum[:, 2 + t % 2, 0:C], yt[:, t % 2, a, :], wt[:, m, a, :], start=(a == 0), stop=(a == CT - 1))
                        mm.then_inc(pj_ready, 1)
                    if t >= 2:
                        pe.wait_ge(ln_done, k - 1)
                        if k >= 4:
                            pe.wait_ge(xt_evac, k - 3)
                        for a in range(CT):
                            mm = pe.transpose(psum[:, 4 + t % 2, a * P:(a + 1) * P], x_sb[:, t - 2, a * P:(a + 1) * P], ident[:])
                        mm.then_inc(xt_ready, 1)

            project(0)

            pe.wait_ge(ld_ctx, 16 * (B + 3))
            for a in range(CT):
                for b in range(B):
                    mm = pe.transpose(psum[:, 6, (a * B + b) * S2:(a * B + b + 1) * S2], ctx_sb[0:S2, b, a * P:(a + 1) * P], ident[0:S2, 0:S2])
            mm.then_inc(c_ready, 1)
            pe.wait_ge(c_evac, 1)
            for o in range(CT):
                for a in range(CT):
                    mm = pe.matmul(psum[:, 7 if o else 6, 0:B * S2], wt[:, 5, a, o * P:(o + 1) * P],
                                   ctx_t[:, a].rearrange("p b k -> p (b k)"), start=(a == 0), stop=(a == CT - 1))
                mm.then_inc(c_ready, 1)
            pe.wait_ge(xt_evac, NT)
            for b in range(B):
                for a in range(CT):
                    mm = pe.matmul(psum[0:S2, 4 + b, 0:C], ctx_t[:, a, b, :], wt[:, 6, a, :], start=(a == 0), stop=(a == CT - 1))
                mm.then_inc(c_ready, 1)
            for j in range(8):
                o, ch = j // 4, j % 4
                if j >= 4:
                    pe.wait_ge(q2_evac, j - 3)
                for a in range(CT):
                    mm = pe.matmul(psum[:, j % 4, :], wt[:, 4, a, o * P:(o + 1) * P], xt[:, a, 512 * ch:512 * (ch + 1)],
                                   start=(a == 0), stop=(a == CT - 1))
                mm.then_inc(q2_ready, 1)
            pe.wait_ge(q2_evac, 8)
            pe.wait_ge(c_evac, 1 + CT)
            pe.wait_ge(kv_done, B * CT + B)
            pe.wait_ge(v2_ones, 1)

            def cross_s(j):
                t, a = j // 2, j % 2
                if j >= 2:
                    pe.wait_ge(sc_done, j - 1)
                n_ = HB // 2 * S2
                for s in range(2):
                    mm = pe.matmul(psum[:, 2 * (j % 2) + s, 0:n_], q2t[:, a, t * P:(t + 1) * P],
                                   k2bd[:, t // TB, a, s * n_:(s + 1) * n_], start=True, stop=True)
                mm.then_inc(s2_ready, 1)

            def cross_t(j):
                c, a = j // 8, j % 2
                pe.wait_ge(exp2_done, j + 1)
                for s in range(2):
                    if j >= 1:
                        pe.wait_ge(ptr_evac, 2 * j + s - 1)
                    if j % 8 == 0 and c >= 1:
                        pe.wait_ge(y2_done, 4 * c)
                    for h in range(4):
                        mm = pe.transpose(psum[0:S2, 4 + s, h * P:(h + 1) * P], pc[:, j % 2, 4 * s + h, :], ident[:])
                    mm.then_inc(ptr_ready, 1)

            def cross_pv(c):
                b = c // 2
                pe.wait_ge(ptr_evac, 16 * (c + 1))
                for g in range(NG):
                    k = NG * c + g
                    if k >= 2:
                        pe.wait_ge(o2_copied, k - 1)
                    for h in range(G):
                        mm = pe.matmul(psum[32 * h:32 * h + 32, 6 + g % 2, :], v2[0:S2, b, G * g + h, :],
                                       pt[0:S2, G * g + h, :], start=True, stop=True)
                    mm.then_inc(pv2_ready, 1)
                    if g >= 1:
                        cross_o(k - 1)
                cross_o(NG * c + NG - 1)

            def cross_o(k):
                pe.wait_ge(o2_copied, k + 1)
                if k >= 2:
                    pe.wait_ge(y2_done, k - 1)
                for t in range(QT):
                    mm = pe.transpose(psum[:, 4 + k % 2, t * P:(t + 1) * P], o2_sb[:, k % 2, t * P:(t + 1) * P], ident[:])
                mm.then_inc(ot_ready, 1)

            for j in range(2 * NT + 1):
                if j < 2 * NT:
                    cross_s(j)
                if j >= 1:
                    cross_t(j - 1)
                    if j % 8 == 0:
                        cross_pv(j // 8 - 1)

            project(1)

            pe.wait_ge(xt_evac, 2 * NT)
            pe.wait_ge(ld_w2, 16 * (3 + E))
            pe.wait_ge(ld_w1, 16 * E)
            for t in range(NT):
                for a in range(CT):
                    mm = pe.matmul(psum[:, 6, t * E:(t + 1) * E], xt[:, a, t * P:(t + 1) * P], wg_sb[:, a, :], start=(a == 0), stop=(a == CT - 1))
            mm.then_inc(lg_ready, 1)
            pe.wait_ge(routed, 1)
            for t in range(NT):
                if t >= 2:
                    pe.wait_ge(b2_added, t - 1)
                pe.transpose(psum[0:E, 4 + t % 2, 0:P], route[:, 8, t, :], ident[:]).then_inc(st_t, 1)
                pe.wait_ge(st_c, t + 1)
                pe.matmul(psum[:, 6 + t % 2, 0:C], score_t[0:E, t % 2, :], b2_sb[0:E, :], start=True, stop=True).then_inc(b2_ready, 1)
            pe.wait_ge(b2_added, NT)

            def hidden(k):
                c, e = k // E, k % E
                for a in range(HT):
                    if k >= 1:
                        pe.wait_ge(h_done, (k - 1) * HT + a + 1)
                    for i in range(CT):
                        mm = pe.matmul(psum[:, a, :], w1_sb[:, e, i, a * P:(a + 1) * P], xt[:, i, 512 * c:512 * (c + 1)],
                                       start=(i == 0), stop=(i == CT - 1))
                    mm.then_inc(h_ready, 1)

            def down(k):
                e = k % E
                pe.wait_ge(h_done, HT * (k + 1))
                for tq in range(4):
                    j = 4 * k + tq
                    if j >= 4:
                        pe.wait_ge(y_added, j - 3)
                    for a in range(HT):
                        mm = pe.matmul(psum[:, 4 + j % 4, 0:C], h_ring[:, k % 2, a, tq * P:(tq + 1) * P], w2_sb[:, e, a, :],
                                       start=(a == 0), stop=(a == HT - 1))
                    mm.then_inc(y_ready, 1)

            for k in range(4 * E + 1):
                if k < 4 * E:
                    hidden(k)
                if k >= 1:
                    down(k - 1)


_INS = ["x", "ctx_1024", "mask_Bx1xSxS2_fk0",
        "L0_attn_Wq", "L0_attn_Wk", "L0_attn_Wv", "L0_attn_Wp", "L0_attn_bq", "L0_attn_bk", "L0_attn_bv", "L0_attn_bp",
        "L0_xattn_Wq", "L0_xattn_Wk", "L0_xattn_Wv", "L0_xattn_Wo", "L0_xattn_bq", "L0_xattn_bk", "L0_xattn_bv", "L0_xattn_bo",
        "L0_ffn_Wg", "L0_ffn_W1", "L0_ffn_b1", "L0_ffn_W2", "L0_ffn_b2"]


def kernel(**inputs):
    import numpy as np
    import concourse.bacc as bacc
    from concourse.bass_utils import run_bass_kernel_spmd

    nc = bacc.Bacc("TRN2", target_bir_lowering=False, num_devices=1)
    arrays, a = {}, {}
    for name in _INS:
        arrays[f"in_{name}"] = np.ascontiguousarray(inputs[name])
        a[name] = nc.dram_tensor(f"in_{name}", arrays[f"in_{name}"].shape, F32, kind="ExternalInput").ap()
    out = nc.dram_tensor("out", a["x"].shape, F32, kind="ExternalOutput").ap()

    def group(prefix, names):
        return [a[f"L0_{prefix}_{n}"] for n in names]

    decoder_layer(nc, a["x"], a["ctx_1024"], a["mask_Bx1xSxS2_fk0"],
                  group("attn", ("Wq", "Wk", "Wv", "Wp")), group("attn", ("bq", "bk", "bv", "bp")),
                  group("xattn", ("Wq", "Wk", "Wv", "Wo")), group("xattn", ("bq", "bk", "bv", "bo")),
                  *group("ffn", ("Wg", "W1", "b1", "W2", "b2")), out)
    r = run_bass_kernel_spmd(nc, [arrays], core_ids=[0])
    return r.results[0]["out"]
```

```python
from contextlib import ExitStack

import concourse.bass as bass
from concourse import mybir

F32 = mybir.dt.float32
BF16 = mybir.dt.bfloat16
ALU = mybir.AluOpType
ACT = mybir.ActivationFunctionType
AX = mybir.AxisListType.X

P = 128
EPS = 1e-5
MASK_WEIGHT = 1000000.0


def decoder_layer(nc, x, ctx_in, mask, attn_w, attn_b, cross_w, cross_b, Wg, W1, b1, W2, b2, out):
    B, T, C = x.shape
    S2 = ctx_in.shape[1]
    H = 16
    DH = C // H
    CT = C // P
    NT = B * T // P
    TB = T // P
    E, _, HID = W1.shape
    HT = HID // P
    G = 4
    NG = H // G
    BLOCKS = B * NG
    HALF = 512
    UNITS = BLOCKS * (T // HALF)
    QT = HALF // P
    STACK = 6 * DH
    SCALE = float(DH) ** -0.5
    BLOCK_COLS = G * T

    with ExitStack() as scope:
        def sb(name, shape, dt=F32):
            return scope.enter_context(nc.sbuf_tensor(name, shape, dt))

        def sem(name):
            return scope.enter_context(nc.semaphore(name))

        def dram(name, shape, dt):
            return nc.dram_tensor(name, shape, dt).ap()

        qk_parts = dram("qk_parts", (2, 3, B, C, T), BF16)
        v_heads = dram("v_heads", (BLOCKS, T, G * 32), F32)
        shift_rows = dram("shift_rows", (2, 3 * G * QT, P), BF16)

        x_sorted = dram("x_sorted", ((2 * B * T + E * (P - 1)) // P, P, C), F32)
        y_sorted = dram("y_sorted", ((2 * B * T + E * (P - 1)) // P, P, C), F32)

        big = sb("big", [P, 2 * BLOCKS * BLOCK_COLS], BF16)
        q_stack = big[:, 0:BLOCKS * BLOCK_COLS]
        k_stack = big[:, BLOCKS * BLOCK_COLS:]
        big_f = big[:].bitcast(F32)
        xt = sb("xt", [P, CT, B * T])
        probs = xt[:].rearrange("p a t -> p (a t)").rearrange("p (s q) -> p s q", q=HALF)
        v_ring = sb("v_ring", [P, 2, T // P, G * 32])
        y = sb("y", [P, TB, BLOCKS, G * DH])
        x_sb = sb("x_sb", [P, NT, C])
        wt = sb("wt", [P, 8, CT, C])
        ident = sb("ident", [P, P])
        ident_b = sb("ident_b", [P, P], BF16)
        bias_col = sb("bias_col", [P, 4, CT])
        bias_row = sb("bias_row", [P, 2, C])
        o_sb = sb("o_sb", [P, HALF])
        alpha = sb("alpha", [P, 8])
        stat = sb("stat", [P, 2, G * QT])
        mparts = sb("mparts", [P, 2, P // (G * QT), G * QT], BF16)
        minus_one = sb("minus_one", [P, G * QT])
        mres = sb("mres", [P, 2, G * QT])
        m_rows = sb("m_rows", [P, 2, P], BF16)
        rsum = sb("rsum", [P, QT, G])
        head_mask = sb("head_mask", [P, P // DH])
        bn = sb("bn", [P, 4, 6])
        mv = sb("mv", [P, 4, 2])
        std = sb("std", [P, 4])

        y_flat = y[:].rearrange("p t n c -> p (t n c)")
        w_raw = y_flat.rearrange("p (m a c) -> p m a c", m=8, a=CT)
        resid = y_flat[:, 0:1024].rearrange("p (s q) -> p s q", s=2)
        split = y_flat[:, 1024:4096].bitcast(BF16).rearrange("p (s j q) -> p s j q", s=4, j=3)
        v_flat = v_ring[:].rearrange("p s k c -> p (s k c)")
        w_bin = v_flat.rearrange("p (m a c) -> p m a c", m=4, a=CT)
        v_stage = v_flat.rearrange("p (s k h d) -> p s k h d", s=2, k=2, h=H)

        zeros = q_stack[:, (BLOCKS - 1) * BLOCK_COLS:].bitcast(F32)
        ZERO_STORES = -(-((2 * B * T + E * (P - 1)) // P) // 8)

        psum = scope.enter_context(nc.psum_tensor("psum", [P, 8, 512], F32))

        pos = [0]

        def carve(n):
            pos[0] += n
            return big_f[:, pos[0] - n:pos[0]]

        w1_sb = carve(E * CT * HID).rearrange("p (e a h) -> p e a h", e=E, a=CT)
        q2t = carve(CT * B * T).rearrange("p (a t) -> p a t", a=CT)
        pt = carve(H * HALF).rearrange("p (h q) -> p h q", h=H)
        HB = P // DH
        k2bd = carve(B * CT * HB * S2).rearrange("p (b a k) -> p b a k", b=B, a=CT)
        v2 = carve(B * H * 32).rearrange("p (b h d) -> p b h d", b=B, h=H)
        ctx_sb = carve(B * C).rearrange("p (b c) -> p b c", b=B)
        ctx_t = carve(CT * B * S2).rearrange("p (a b k) -> p a b k", a=CT, b=B)
        k2t = carve(CT * B * S2).rearrange("p (a b k) -> p a b k", a=CT, b=B)
        bias2_row = carve(2 * C).rearrange("p (i c) -> p i c", i=2)
        mask_sb = carve(NT * S2).rearrange("p (t k) -> p t k", t=NT)
        sc = carve(4 * HB * S2).rearrange("p (s h k) -> p s h k", s=4, h=HB)
        mx2 = carve(4 * HB).rearrange("p (s h) -> p s h", s=4)
        o2_sb = carve(2 * HALF).rearrange("p (g q) -> p g q", g=2)
        YT_AT = pos[0]
        yt = carve(2 * C).rearrange("p (s a q) -> p s a q", s=2, a=CT)
        assert pos[0] <= big_f.shape[1]
        pos[0] = E * CT * HID
        SLOT_TILES = (2 * B * T + E * (P - 1)) // P
        w2_sb = carve(E * HT * C).rearrange("p (e a c) -> p e a c", e=E, a=HT)
        b1_rows = carve(E * HID)
        b2_rows = carve(E * C)
        wg_sb = carve(CT * E).rearrange("p (a e) -> p a e", a=CT)
        route = carve(10 * NT * E).rearrange("p (n t e) -> p n t e", n=10, t=NT)
        prob, prob2, first, second, chosen, before, scan_a, scan_b, weigh, counts = (route[:, i] for i in range(10))
        rows = carve(10 * NT).rearrange("p (n t) -> p n t", n=10)
        row_a, top1, top2, share1, share2, place1, place2, row_b, row_c, row_d = (rows[:, i] for i in range(10))
        upto = carve(48)
        upto_i = carve(48).bitcast(mybir.dt.int32)
        earlier = carve(P)
        ones = carve(P)
        many = carve(E * 48).rearrange("p (a b) -> p a b", b=48)
        e_rows = carve(4 * E).rearrange("p (n e) -> p n e", n=4)
        tile_e = carve(48)
        tile_expert = carve(48).bitcast(mybir.dt.int32)
        places = carve(2 * NT).bitcast(mybir.dt.uint32).rearrange("p (k t) -> p k t", k=2)
        xs_in = carve(2 * C).rearrange("p (s c) -> p s c", s=2)
        xst = carve(2 * C).rearrange("p (s a q) -> p s a q", s=2, a=CT)
        hid = carve(2 * HID).rearrange("p (s h) -> p s h", s=2)
        hid_t = carve(2 * HID).rearrange("p (s a q) -> p s a q", s=2, a=HT)
        y_out = carve(2 * C).rearrange("p (s c) -> p s c", s=2)
        assert pos[0] <= YT_AT
        pos[0] = E * CT * HID + 8 * C
        gathered = big_f[:, E * CT * HID:E * CT * HID + 8 * C].rearrange("p (s k c) -> p s k c", s=4, k=2)

        s_ident, s_identb = sem("s_ident"), sem("s_identb")
        s_hm = sem("s_hm")
        ld_x, ld_w, ld_bias = sem("ld_x"), sem("ld_w"), sem("ld_bias")
        s_sign, s_bin = sem("s_sign"), sem("s_bin")
        s_ones = sem("s_ones")
        t_ready, t_evac = sem("t_ready"), sem("t_evac")
        qk_ready, hi_done, r_done, mid_done, lo_done = (sem(n) for n in ("qk_ready", "hi_done", "r_done", "mid_done", "lo_done"))
        part_stored = [sem(f"part_stored{i}") for i in range(4)]
        vp_ready, v_evac = sem("vp_ready"), sem("v_evac")
        v_stored = [sem(f"v_stored{i}") for i in range(2)]
        stack_loaded = sem("stack_loaded")
        v_loaded = [sem(f"v_loaded{i}") for i in range(2)]
        st_ready, exp_done, pv_done, o_copied = sem("st_ready"), sem("exp_done"), sem("pv_done"), sem("o_copied")
        sm_ready, sm_free, dve_own = sem("sm_ready"), sem("sm_free"), sem("dve_own")
        pool_own, parts_done = sem("pool_own"), sem("parts_done")
        rows_stored = sem("rows_stored")
        rows_loaded = [sem(f"rows_loaded{i}") for i in range(2)]
        x_biased = sem("x_biased")
        yt_ready, yt_evac, pj_ready, added, ln_done, xt_ready, xt_evac = (
            sem(n) for n in ("yt_ready", "yt_evac", "pj_ready", "added", "ln_done", "xt_ready", "xt_evac"))
        ld_ctx, c_ready, c_evac, kv_done = sem("ld_ctx"), sem("c_ready"), sem("c_evac"), sem("kv_done")
        q2_ready, q2_evac = sem("q2_ready"), sem("q2_evac")
        s2_ready, sc_done, mx_done, sub_done, exp2_done, ptr_ready, ptr_evac = (
            sem(n) for n in ("s2_ready", "sc_done", "mx_done", "sub_done", "exp2_done", "ptr_ready", "ptr_evac"))
        pv2_ready, o2_copied, ot_ready, y2_done = (sem(n) for n in ("pv2_ready", "o2_copied", "ot_ready", "y2_done"))
        mask_scaled, v2_ones = sem("mask_scaled"), sem("v2_ones")
        ld_w1, ld_w2, ld_wg = sem("ld_w1"), sem("ld_w2"), sem("ld_wg")
        zeros_set, zeros_stored, s_upto, s_tri = (sem(n) for n in ("zeros_set", "zeros_stored", "s_upto", "s_tri"))
        lg_ready, lg_sub, lg_exp, mask_ready, ranks_ready, placed, scattered = (
            sem(n) for n in ("lg_ready", "lg_sub", "lg_exp", "mask_ready", "ranks_ready", "placed", "scattered"))
        xs_loaded = [sem(f"xs_loaded{i}") for i in range(2)]
        xs_t, xst_evac, up_ready, hid_done, hid_tr, relu_done, down_ready, y_biased = (
            sem(n) for n in ("xs_t", "xst_evac", "up_ready", "hid_done", "hid_tr", "relu_done", "down_ready", "y_biased"))
        ys_stored = [sem(f"ys_stored{i}") for i in range(2)]
        got = [sem(f"got{i}") for i in range(4)]
        mixed = sem("mixed")
        out_stored, stats_done, sqrt_done = sem("out_stored"), sem("stats_done"), sem("sqrt_done")

        x_tok = x.rearrange("b (t p) c -> p (b t) c", p=P)
        out_tok = out.rearrange("b (t p) c -> p (b t) c", p=P)

        SM_UNIT = G * QT + 2
        SM_FIRST = 2 * G * QT
        OT_POS, MT_POS = 4, 5

        def max_pos(i):
            return i if i < 4 else i + 2

        def sm_index(u, pos_, first):
            return u * SM_UNIT + (SM_FIRST + pos_ + (1 if first and pos_ < OT_POS else 0))

        def sm_slot(pos_, first):
            return (pos_ + (1 if first and pos_ < OT_POS else 0)) % 2

        ST_BANK, O_BANK = 4, 7

        def sm_tile(slot):
            return psum[:, 2 * slot:2 * slot + 2, :].rearrange("p a q -> p (a q)")

        def stack_ap(stack, n, rows, h, start, size):
            return stack[rows, bass.ds(n * BLOCK_COLS + (h * T + start), size)]

        def stack_block(rows, n):
            return rows[:, bass.ds(n * BLOCK_COLS, BLOCK_COLS)]

        LAG = 3
        STACK_LOADS = 2 * 6 * 16

        block = scope.enter_context(nc.Block())

        @block.sync
        def _(sp):
            for g in range(4):
                sp.dma_start(x_sb[:, 4 * g:4 * g + 4, :], x_tok[:, 4 * g:4 * g + 4, :]).then_inc(ld_x, 16)
            for m, w in enumerate(attn_w + cross_w):
                sp.dma_start(w_raw[:, m], w.rearrange("(a p) c -> p a c", p=P)).then_inc(ld_w, 16)
            for i, b in enumerate((attn_b[0], attn_b[1], cross_b[0], cross_b[1])):
                sp.dma_start(bias_col[:, i, :], b.rearrange("(a p) -> p a", p=P),
                             allow_slow_non_contiguous=True).then_inc(ld_bias, 16)
            for i, b in enumerate((attn_b[2], attn_b[3])):
                sp.dma_start(bias_row[:, i, :], b.rearrange("(o c) -> o c", o=1).broadcast_to([P, C])).then_inc(ld_bias, 16)

            def store_parts(j):
                b, m, a, ch = j // 8, j // 4 % 2, j // 2 % 2, j % 2
                sp.wait_ge(lo_done, j + 1)
                sp.dma_start(qk_parts[m, :, b, a * P:(a + 1) * P, ch * HALF:(ch + 1) * HALF].rearrange("j o t -> o j t"),
                             split[:, j % 4]).then_inc(part_stored[j % 4], 16)

            def store_v(j):
                sp.wait_ge(v_evac, j + 1)
                b, t0 = j // 4, j % 4 * 2 * P
                for k in range(2):
                    sp.dma_start(
                        v_heads[b * NG:(b + 1) * NG, t0 + k * P:t0 + (k + 1) * P, :].rearrange("g p c -> p g c"),
                        v_stage[:, j % 2, k].rearrange("p (g h) d -> p g (h d)", g=NG)).then_inc(v_stored[j % 2], 16)

            by_block = qk_parts.rearrange("m j b (g h d) t -> m j (b g) d h t", g=NG, d=DH)

            def load_stacks(n):
                for m, stack, parts in ((0, q_stack, (0, 0, 0, 1, 1, 2)), (1, k_stack, (0, 1, 2, 0, 1, 0))):
                    for j, part in enumerate(parts):
                        sp.dma_start(stack_block(stack[DH * j:DH * (j + 1)], n).rearrange("d (h t) -> d h t", h=G),
                                     by_block[m, part, bass.ds(n, 1)].rearrange("o d h t -> (o d) h t")).then_inc(stack_loaded, 16)

            sp.wait_ge(zeros_set, 1)
            for i in range(0, SLOT_TILES, 8):
                k = min(8, SLOT_TILES - i)
                sp.dma_start(x_sorted[i:i + k].rearrange("k p c -> p k c"),
                             zeros[:, 0:k * C].rearrange("p (k c) -> p k c", k=k)).then_inc(zeros_stored, 16)

            for b in range(B):
                for j in range(8 * b, 8 * b + 8):
                    store_parts(j)
                if b == 0:
                    for s in range(4):
                        sp.wait_ge(part_stored[s], 32)
                    load_stacks(0)
                for j in range(4 * b, 4 * b + 4):
                    store_v(j)
            for s in range(4):
                sp.wait_ge(part_stored[s], 64)
            sp.wait_ge(zeros_stored, 16 * ZERO_STORES)
            sp.wait_ge(stack_loaded, STACK_LOADS)
            load_stacks(1)

            def load_v(n, q):
                sp.dma_start(v_ring[:, q], v_heads[bass.ds(n, 1)].rearrange("o (k p) c -> p (o k) c", p=P)
                             ).then_inc(v_loaded[q], 16)

            def move_rows(n, q, u, pos_=MT_POS):
                sp.wait_ge(sm_free, sm_index(u - 1, pos_, False) + 1)
                sp.dma_start(shift_rows[q], m_rows[0:3 * G * QT, q]).then_inc(rows_stored, 16)
                sp.wait_ge(rows_stored, u * 16 + 16)
                dst = q_stack[STACK:STACK + 3, bass.ds(n * BLOCK_COLS, BLOCK_COLS)].rearrange("p (h t) -> p h t", h=G)
                sp.dma_start(dst[:, :, q * HALF:(q + 1) * HALF],
                             shift_rows[q].rearrange("(j h t) c -> j h (t c)", j=3, h=G)).then_inc(rows_loaded[q], 16)

            for s in range(2):
                sp.wait_ge(v_stored[s], 2 * 16 * 4)
            load_v(0, 0)
            sp.wait_ge(sm_free, SM_FIRST + 1)
            sp.dma_start(shift_rows[0], m_rows[0:3 * G * QT, 0]).then_inc(rows_stored, 16)
            sp.wait_ge(rows_stored, 16)
            sp.dma_start(q_stack[STACK:STACK + 3, 0:BLOCK_COLS].rearrange("p (h t) -> p h t", h=G)[:, :, 0:HALF],
                         shift_rows[0].rearrange("(j h t) c -> j h (t c)", j=3, h=G)).then_inc(rows_loaded[0], 16)

            def units(n, first=False, last=False, stacks=True):
                if stacks:
                    sp.wait_ge(stack_loaded, n * STACK_LOADS + 2 * STACK_LOADS)
                    load_stacks(n + 2)
                if not first:
                    sp.wait_ge(pv_done, n * 16)
                load_v(n, 1)
                move_rows(n, 1, n * 2 + 1, 1 if last else MT_POS)
                if not last:
                    sp.wait_ge(pv_done, n * 16 + 8)
                    load_v(n + 1, 0)
                    move_rows(n + 1, 0, n * 2 + 2)

            units(0, first=True)
            with sp.Fori(1, BLOCKS - 2) as n:
                units(n)
            units(BLOCKS - 2, stacks=False)
            units(BLOCKS - 1, last=True, stacks=False)

            sp.wait_ge(pv_done, 8 * UNITS)
            for b in range(B):
                sp.dma_start(ctx_sb[0:S2, b, :], ctx_in[b]).then_inc(ld_ctx, 16)
            sp.dma_start(mask_sb[:, :, :], mask.rearrange("b o (t p) k -> p (b o t) k", p=P)).then_inc(ld_ctx, 16)
            for i, b in enumerate((cross_b[2], cross_b[3])):
                sp.dma_start(bias2_row[:, i, :], b.rearrange("(o c) -> o c", o=1).broadcast_to([P, C])).then_inc(ld_ctx, 16)
            for e in range(E):
                sp.dma_start(w1_sb[:, e], W1[e].rearrange("(a p) h -> p a h", p=P)).then_inc(ld_w1, 16)
            sp.wait_ge(y2_done, 4 * NG)
            sp.wait_ge(x_biased, 2 * NT)
            sp.dma_start(wg_sb, Wg.rearrange("(a p) e -> p a e", p=P)).then_inc(ld_wg, 16)
            sp.dma_start(b1_rows, b1.rearrange("(o e) h -> o (e h)", o=1).broadcast_to([P, E * HID])).then_inc(ld_w2, 16)
            for e in range(E):
                sp.dma_start(w2_sb[:, e], W2[e].rearrange("(a p) c -> p a c", p=P)).then_inc(ld_w2, 16)
            sp.dma_start(b2_rows, b2.rearrange("(o e) c -> o (e c)", o=1).broadcast_to([P, E * C])).then_inc(ld_w2, 16)

            sp.wait_ge(scattered, 2 * NT * 16)
            for i in range(2):
                sp.dma_start(xs_in[:, i], x_sorted[i]).then_inc(xs_loaded[i], 16)

            def expert_io(i, s, load=True):
                if load:
                    sp.wait_ge(xs_t, i + 1)
                    sp.dma_start(xs_in[:, s], x_sorted[bass.ds(i + 2, 1)].rearrange("o p c -> p (o c)")).then_inc(xs_loaded[s], 16)
                if not (isinstance(i, int) and i == 0):
                    sp.wait_ge(y_biased, i)
                    sp.dma_start(y_sorted[bass.ds(i - 1, 1)].rearrange("o p c -> p (o c)"), y_out[:, 1 - s]).then_inc(ys_stored[1 - s], 16)

            expert_io(0, 0)
            with sp.Fori(0, (SLOT_TILES - 3) // 2) as m:
                expert_io(m * 2 + 1, 1)
                expert_io(m * 2 + 2, 0)
            for i in range(SLOT_TILES - 2, SLOT_TILES + 1):
                expert_io(i, i % 2, load=False)

            for g in range(NT):
                sp.wait_ge(ln_done, 2 * NT + g + 1)
                sp.dma_start(out_tok[:, g:g + 1, :], x_sb[:, g:g + 1, :]).then_inc(out_stored, 16)
            sp.wait_ge(out_stored, 16 * NT)

        @block.gpsimd
        def _(pool):
            own = [0]

            def link(ins):
                own[0] += 1
                ins.then_inc(pool_own, 1)
                pool.wait_ge(pool_own, own[0])

            nc.gpsimd.memset(zeros, 0.0).then_inc(zeros_set, 1)
            pool.wait_ge(zeros_set, 1)
            link(nc.gpsimd.memset(ident[:], 0.0))
            nc.gpsimd.affine_select(out=ident[:], in_=ident[:], compare_op=ALU.not_equal, fill=1.0, base=0,
                                    pattern=[[-1, P]], channel_multiplier=1).then_inc(s_ident, 1)
            pool.wait_ge(s_ident, 1)
            nc.gpsimd.tensor_copy(ident_b[:], ident[:]).then_inc(s_identb, 1)
            link(nc.gpsimd.memset(head_mask[:], SCALE))
            link(nc.gpsimd.affine_select(out=head_mask[:], in_=head_mask[:], compare_op=ALU.is_ge, fill=0.0, base=0,
                                         pattern=[[-DH, P // DH]], channel_multiplier=1))
            nc.gpsimd.affine_select(out=head_mask[:], in_=head_mask[:], compare_op=ALU.is_ge, fill=0.0, base=DH - 1,
                                    pattern=[[DH, P // DH]], channel_multiplier=-1).then_inc(s_hm, 1)
            link(nc.gpsimd.memset(minus_one[:], -1.0))
            link(nc.gpsimd.memset(mparts[:], 0.0))
            nc.gpsimd.memset(k_stack[STACK:STACK + 3, :], 1.0).then_inc(s_ones, 1)
            pool.wait_ge(s_ones, 1)
            pool.wait_ge(t_ready, 8)
            pool.wait_ge(ld_bias, 6 * 16)
            for t in range(NT):
                nc.gpsimd.tensor_tensor(x_sb[:, t, :], x_sb[:, t, :], bias_row[:, 1, :], ALU.add).then_inc(x_biased, 1)

            def shifts(q, u, rounds, mt_done=None):
                pool.wait_ge(sm_free, mt_done)
                base = own[0]
                m, a, r = stat[:, q], mparts[:, q], mres[:, q]
                nc.gpsimd.tensor_tensor(a[:, 0], m, minus_one[:], ALU.mult).then_inc(pool_own, 1)
                pool.wait_ge(pool_own, rounds + 1)
                nc.gpsimd.tensor_tensor(r, m, a[:, 0], ALU.add).then_inc(pool_own, 1)
                pool.wait_ge(pool_own, rounds + 2)
                nc.gpsimd.tensor_tensor(a[:, 1], r, minus_one[:], ALU.mult).then_inc(pool_own, 1)
                pool.wait_ge(pool_own, rounds + 3)
                nc.gpsimd.tensor_tensor(r, r, a[:, 1], ALU.add).then_inc(pool_own, 1)
                pool.wait_ge(pool_own, rounds + 4)
                nc.gpsimd.tensor_tensor(a[:, 2], r, minus_one[:], ALU.mult).then_inc(parts_done, 1)

            start = own[0]
            shifts(0, 0, start, mt_done=G * QT)
            shifts(1, 1, start + 4, mt_done=2 * G * QT)

            def block_shifts(n, first=False):
                for q in range(2):
                    u = n * 2 + q
                    shifts(q, u + 2, n * 8 + (start + 8 + 4 * q),
                           mt_done=sm_index(u, max_pos(G * QT - 1), first and q == 0) + 1)

            block_shifts(0, first=True)
            with pool.Fori(1, BLOCKS - 1) as n:
                block_shifts(n)
            own[0] = start + 8 + 8 * (BLOCKS - 1)

            pool.wait_ge(ld_ctx, 16 * (B + 3))
            pool.wait_ge(pv_done, 8 * UNITS)
            nc.gpsimd.tensor_scalar(mask_sb[:, :, :], mask_sb[:, :, :], -MASK_WEIGHT, None, ALU.mult).then_inc(mask_scaled, 1)
            nc.gpsimd.memset(v2[:, :, :, DH:32], 1.0).then_inc(v2_ones, 1)
            for t in range(NT):
                pool.wait_ge(xt_ready, t + 1)
                nc.gpsimd.tensor_tensor(x_sb[:, t, :], x_sb[:, t, :], bias2_row[:, 1, :], ALU.add).then_inc(x_biased, 1)
            for j in range(2 * NT):
                pool.wait_ge(mx_done, j + 1)
                nc.gpsimd.tensor_tensor(sc[:, j % 4], sc[:, j % 4],
                                        mx2[:, j % 4, :].unsqueeze(2).broadcast_to([P, HB, S2]), ALU.subtract).then_inc(sub_done, 1)

            pool.wait_ge(y2_done, 4 * NG)
            link(nc.gpsimd.iota(upto_i, [[1, 48]], base=0, channel_multiplier=0))
            nc.gpsimd.tensor_copy(upto, upto_i).then_inc(s_upto, 1)
            link(nc.gpsimd.memset(ones, 1.0))
            nc.gpsimd.affine_select(out=earlier, in_=ones, compare_op=ALU.is_ge, fill=0.0, base=-1,
                                    pattern=[[1, P]], channel_multiplier=-1).then_inc(s_tri, 1)
            pool.wait_ge(placed, 1)
            pool.wait_ge(zeros_stored, 16 * ZERO_STORES)
            pool.wait_ge(ln_done, 2 * NT)
            for t in range(NT):
                for k in range(2):
                    pool.indirect_dma_start(out=x_sorted.rearrange("n p c -> (n p) c"),
                                            out_offset=bass.IndirectOffsetOnAxis(ap=places[:, k, t:t + 1], axis=0),
                                            in_=x_sb[:, t, :], in_offset=None).then_inc(scattered, 16)
            for s in range(2):
                pool.wait_ge(ys_stored[s], 16 * ((SLOT_TILES + 1 - s) // 2))
            for t in range(NT):
                if t >= 4:
                    pool.wait_ge(mixed, 2 * (t - 3))
                for k in range(2):
                    pool.indirect_dma_start(out=gathered[:, t % 4, k], out_offset=None,
                                            in_=y_sorted.rearrange("n p c -> (n p) c"),
                                            in_offset=bass.IndirectOffsetOnAxis(ap=places[:, k, t:t + 1], axis=0)).then_inc(got[t % 4], 16)

        @block.scalar
        def _(act):
            act.wait_ge(ld_w, 16 * 8)
            nc.scalar.activation(w_bin[:, :, :, :], w_raw[:, 0:4], ACT.Sign).then_inc(s_sign, 1)
            act.wait_ge(ld_bias, 6 * 16)
            for k in range(16):
                act.wait_ge(t_ready, k + 1)
                if k < 8:
                    a, g = k // 4, k % 4
                    dst = xt[:, a, 512 * g:512 * (g + 1)]
                    src = psum[:, k % 4, :]
                else:
                    m = (k - 8 + 4) % 8
                    dst = wt[:, m]
                    src = psum[:, k % 4, :].rearrange("p (a o) -> p a o", a=CT)
                nc.scalar.copy(dst, src).then_inc(t_evac, 1)

            def mid(j):
                act.wait_ge(r_done, j + 1)
                nc.scalar.copy(split[:, j % 4, 1], resid[:, j % 2]).then_inc(mid_done, 1)

            for j in range(16):
                m, a = j // 4 % 2, j // 2 % 2
                act.wait_ge(qk_ready, j + 1)
                if j >= 4:
                    act.wait_ge(part_stored[j % 4], 16 * (j // 4))
                nc.scalar.activation(split[:, j % 4, 0], psum[:, 4 + j % 4, :], ACT.Identity,
                                     bias=bias_col[:, m, a:a + 1]).then_inc(hi_done, 1)
                if j >= 1:
                    mid(j - 1)
            mid(15)

            def copy_o(u):
                act.wait_ge(pv_done, u * 8 + 8)
                nc.scalar.copy(o_sb[:], psum[:, O_BANK, :]).then_inc(o_copied, 1)

            def exps(n, q, first=False, pos_=OT_POS):
                u = n * 2 + q
                for kt in range(TB):
                    for h in range(G):
                        i = kt * G + h
                        act.wait_ge(st_ready, u * 32 + (i + 1))
                        if h == 0 and not (first and kt < 2):
                            act.wait_ge(pv_done, u * 8 + (kt - 1))
                        nc.scalar.activation(probs[:, kt % 2 * G + h, :], psum[:, ST_BANK + i % 3, :], ACT.Exp,
                                             scale=SCALE).then_inc(exp_done, 1)
                    if kt == 0 and not first:
                        if not (isinstance(n, int) and n == 0):
                            act.wait_ge(sm_ready, sm_index(u - 1, pos_, False) + 1)
                        copy_o(u - 1)

            exps(0, 0, first=True)
            exps(0, 1)
            with act.Fori(1, BLOCKS - 1) as n:
                exps(n, 0)
                exps(n, 1)
            exps(BLOCKS - 1, 0)
            exps(BLOCKS - 1, 1, pos_=0)
            act.wait_ge(sm_ready, sm_index(UNITS - 2, 2, False) + 1)
            copy_o(UNITS - 1)

            def norm_sqrt(k):
                act.wait_ge(stats_done, k + 1)
                nc.scalar.activation(std[:, k % 4:k % 4 + 1], mv[:, k % 4, 1:2], ACT.Sqrt, bias=EPS).then_inc(sqrt_done, 1)

            def proj_copies(stage):
                base = stage * NT
                for t in range(NT + 2):
                    if t < NT:
                        act.wait_ge(yt_ready, base + t + 1)
                        if base + t >= 2:
                            act.wait_ge(pj_ready, base + t - 1)
                        nc.scalar.copy(yt[:, t % 2], psum[:, t % 2, 0:C].rearrange("p (a q) -> p a q", a=CT)).then_inc(yt_evac, 1)
                    if 1 <= t <= NT:
                        norm_sqrt(base + t - 1)
                    if t >= 2:
                        act.wait_ge(xt_ready, base + t - 1)
                        nc.scalar.copy(xt[:, :, (t - 2) * P:(t - 1) * P],
                                       psum[:, 4 + t % 2, 0:C].rearrange("p (a q) -> p a q", a=CT)).then_inc(xt_evac, 1)

            proj_copies(0)

            act.wait_ge(c_ready, 1)
            nc.scalar.copy(ctx_t[:, :, :, :], psum[:, 6, 0:CT * B * S2].rearrange("p (a b k) -> p a b k", a=CT, b=B)).then_inc(c_evac, 1)
            for a in range(CT):
                act.wait_ge(c_ready, 2 + a)
                nc.scalar.activation(k2t[:, a], psum[:, 7 if a else 6, 0:B * S2].rearrange("p (b k) -> p b k", b=B),
                                     ACT.Identity, bias=bias_col[:, 3, a:a + 1]).then_inc(c_evac, 1)
            for j in range(8):
                a, ch = j // 4, j % 4
                act.wait_ge(q2_ready, j + 1)
                nc.scalar.activation(q2t[:, a, 512 * ch:512 * (ch + 1)], psum[:, j % 4, :], ACT.Identity,
                                     bias=bias_col[:, 2, a:a + 1]).then_inc(q2_evac, 1)

            def cross_exp(j):
                act.wait_ge(sub_done, j + 1)
                nc.scalar.activation(sc[:, j % 4], sc[:, j % 4], ACT.Exp).then_inc(exp2_done, 1)

            def pt_copies(j):
                c, tq, a = j // 8, j % 8 // 2, j % 2
                for s in range(2):
                    act.wait_ge(ptr_ready, 2 * j + s + 1)
                    if tq == 0 and a == 0 and c >= 1:
                        act.wait_ge(pv2_ready, 4 * c)
                    nc.scalar.copy(pt[0:S2, a * HB + 4 * s:a * HB + 4 * s + 4, tq * P:(tq + 1) * P],
                                   psum[0:S2, 4 + s, :].rearrange("k (h q) -> k h q", h=4)).then_inc(ptr_evac, 1)

            def cross_out(c):
                for g in range(NG):
                    k = NG * c + g
                    act.wait_ge(pv2_ready, k + 1)
                    if k >= 2:
                        act.wait_ge(ot_ready, k - 1)
                    nc.scalar.copy(o2_sb[:, g % 2], psum[:, 6 + g % 2, :]).then_inc(o2_copied, 1)

            for j in range(2 * NT + LAG - 1):
                if j < 2 * NT:
                    cross_exp(j)
                if j >= LAG - 1:
                    pt_copies(j - LAG + 1)
                    if (j - LAG + 1) % 8 == 7:
                        cross_out((j - LAG + 1) // 8)

            proj_copies(1)

            act.wait_ge(lg_sub, 1)
            nc.scalar.activation(prob, prob, ACT.Exp).then_inc(lg_exp, 1)

            def xst_copy(i, s):
                act.wait_ge(xs_t, i + 1)
                if not (isinstance(i, int) and i < 2):
                    act.wait_ge(up_ready, i - 1)
                nc.scalar.copy(xst[:, s], psum[:, 6 + s, 0:C].rearrange("p (a q) -> p a q", a=CT)).then_inc(xst_evac, 1)

            def relu(i, s):
                act.wait_ge(hid_tr, i + 1)
                if not (isinstance(i, int) and i < 2):
                    act.wait_ge(down_ready, i - 1)
                nc.scalar.activation(hid_t[:, s], psum[:, 2 + s, :].rearrange("p (a q) -> p a q", a=HT), ACT.Relu).then_inc(relu_done, 1)

            xst_copy(0, 0)
            xst_copy(1, 1)
            relu(0, 0)
            xst_copy(2, 0)
            relu(1, 1)
            xst_copy(3, 1)
            relu(2, 0)
            with act.Fori(1, (SLOT_TILES - 3) // 2) as m:
                xst_copy(m * 2 + 2, 0)
                relu(m * 2 + 1, 1)
                xst_copy(m * 2 + 3, 1)
                relu(m * 2 + 2, 0)
            xst_copy(SLOT_TILES - 1, (SLOT_TILES - 1) % 2)
            relu(SLOT_TILES - 2, SLOT_TILES % 2)
            relu(SLOT_TILES - 1, (SLOT_TILES - 1) % 2)
            for t in range(NT):
                norm_sqrt(2 * NT + t)

        @block.vector
        def _(dve):
            own = [0]

            def link(ins):
                own[0] += 1
                ins.then_inc(dve_own, 1)
                dve.wait_ge(dve_own, own[0])

            dve.wait_ge(ld_w, 16 * 8)
            link(nc.vector.tensor_reduce(alpha[:], w_raw[:, 0:4].rearrange("p m a c -> p (m a) c"), AX, ALU.add,
                                         apply_absolute_value=True))
            link(nc.vector.tensor_scalar(alpha[:], alpha[:], 1.0 / C, None, ALU.mult))
            dve.wait_ge(s_sign, 1)
            link(nc.vector.tensor_tensor(w_bin[:, :, :, :], w_bin[:, :, :, :], w_raw[:, 0:4], ALU.subtract))
            link(nc.vector.tensor_tensor(w_bin[:, :, :, :], w_bin[:, :, :, :], w_raw[:, 0:4], ALU.add))
            nc.vector.tensor_tensor(v_flat.rearrange("p (m c) -> p m c", c=C), v_flat.rearrange("p (m c) -> p m c", c=C),
                                    alpha[:].unsqueeze(2).broadcast_to([P, 8, C]), ALU.mult).then_inc(s_bin, 1)
            dve.wait_ge(ld_bias, 6 * 16)

            def lo(j):
                dve.wait_ge(mid_done, j + 1)
                nc.vector.tensor_tensor(split[:, j % 4, 2], resid[:, j % 2], split[:, j % 4, 1], ALU.subtract).then_inc(lo_done, 1)

            def v_out(j):
                if j == 0:
                    dve.wait_ge(t_ready, 16)
                    link(nc.vector.memset(v_stage[:, :, :, :, DH:32], 1.0))
                dve.wait_ge(vp_ready, j + 1)
                if j >= 2:
                    dve.wait_ge(v_stored[j % 2], 32 * (j // 2))
                nc.vector.tensor_tensor(
                    v_stage[:, j % 2, :, :, 0:DH], psum[:, j % 4, :].rearrange("p (k h d) -> p k h d", k=2, h=H),
                    bias_row[:, 0, :].rearrange("p (h d) -> p h d", h=H).unsqueeze(1).broadcast_to([P, 2, H, DH]),
                    ALU.add).then_inc(v_evac, 1)

            for b in range(B):
                for j in range(8 * b, 8 * b + 8):
                    m, a = j // 4 % 2, j // 2 % 2
                    dve.wait_ge(hi_done, j + 1)
                    if j >= 2:
                        dve.wait_ge(lo_done, j - 1)
                    nc.vector.scalar_tensor_tensor(out=resid[:, j % 2], in0=psum[:, 4 + j % 4, :], scalar=bias_col[:, m, a:a + 1],
                                                   in1=split[:, j % 4, 0], op0=ALU.add, op1=ALU.subtract).then_inc(r_done, 1)
                    if j >= 8 * b + 1:
                        lo(j - 1)
                lo(8 * b + 7)
                for j in range(4 * b, 4 * b + 4):
                    v_out(j)

            def row_max(q, i, k, slot, parts, last=None):
                dve.wait_ge(sm_ready, k + 1)
                if parts is not None:
                    dve.wait_ge(parts_done, parts)
                nc.vector.reduce_max(stat[:, q, i:i + 1], sm_tile(slot), AX).then_inc(sm_free, 1)

            def shift_row(q, k, slot):
                dve.wait_ge(sm_ready, k + 1)
                rows = psum[0:3 * G * QT, 2 * slot, :].bitcast(BF16)[:, 0:P]
                nc.vector.tensor_copy(m_rows[0:3 * G * QT, q], rows).then_inc(sm_free, 1)

            def normalise(n, q, k, slot, own_value):
                dve.wait_ge(sm_ready, k + 1)
                o = psum[:, 2 * slot, :].rearrange("p (t h d) -> p t h d", t=QT, h=G)
                nc.vector.reciprocal(rsum[:], o[:, :, :, DH]).then_inc(dve_own, 1)
                dve.wait_ge(dve_own, own_value + 1)
                dst = y[:, q * QT:(q + 1) * QT, bass.ds(n, 1), :]
                nc.vector.tensor_tensor(dst.rearrange("p t n (h d) -> p t (n h) d", h=G), o[:, :, :, 0:DH],
                                        rsum[:].unsqueeze(3).broadcast_to([P, QT, G, DH]), ALU.mult).then_inc(sm_free, 1)

            for u in range(2):
                for i in range(G * QT):
                    row_max(u, i, u * G * QT + i, i % 2, None)
            shift_row(0, SM_FIRST, 0)
            start = own[0]

            def unit_dve(n, q, first=False, maxima=True, rows=True):
                u = n * 2 + q
                for kt in range(TB):
                    if kt == 2:
                        if not first:
                            normalise(n if q else n - 1, 1 - q, sm_index(u, OT_POS, False), sm_slot(OT_POS, False), u + (start - 1))
                        if rows:
                            if not first:
                                dve.wait_ge(rows_stored, u * 16)
                            shift_row(1 - q, sm_index(u, MT_POS, first), sm_slot(MT_POS, first))
                    if maxima:
                        for i in (2 * kt, 2 * kt + 1):
                            row_max(q, i, sm_index(u, max_pos(i), first), sm_slot(max_pos(i), first), u + 1)

            unit_dve(0, 0, first=True)
            unit_dve(0, 1)
            with dve.Fori(1, BLOCKS - 1) as n:
                unit_dve(n, 0)
                unit_dve(n, 1)
            k0 = sm_index(UNITS - 2, 0, False)
            normalise(BLOCKS - 2, 1, k0, 0, start + UNITS - 3)
            dve.wait_ge(rows_stored, 16 * (UNITS - 2))
            shift_row(1, k0 + 1, 1)
            normalise(BLOCKS - 1, 0, k0 + 2, 0, start + UNITS - 2)
            dve.wait_ge(sm_free, k0 + 3)
            normalise(BLOCKS - 1, 1, k0 + 3, 1, start + UNITS - 1)
            own[0] = start + UNITS

            def norm_stats(t, k):
                if k >= 4:
                    dve.wait_ge(ln_done, k - 3)
                link(nc.vector.bn_stats(bn[:, k % 4], x_sb[:, t, :]))
                nc.vector.bn_aggr(mv[:, k % 4], bn[:, k % 4]).then_inc(stats_done, 1)

            def norm_apply(t, k):
                dve.wait_ge(sqrt_done, k + 1)
                link(nc.vector.reciprocal(std[:, k % 4:k % 4 + 1], std[:, k % 4:k % 4 + 1]))
                nc.vector.tensor_scalar(x_sb[:, t, :], x_sb[:, t, :], mv[:, k % 4, 0:1], std[:, k % 4:k % 4 + 1],
                                        ALU.subtract, ALU.mult).then_inc(ln_done, 1)

            def residual(stage):
                for t in range(NT + 1):
                    k = stage * NT + t
                    if t < NT:
                        dve.wait_ge(pj_ready, k + 1)
                        dve.wait_ge(x_biased, k + 1)
                        nc.vector.tensor_tensor(x_sb[:, t, :], x_sb[:, t, :], psum[:, 2 + t % 2, 0:C], ALU.add).then_inc(added, 1)
                        dve.wait_ge(added, k + 1)
                        norm_stats(t, k)
                    if t >= 1:
                        norm_apply(t - 1, k - 1)

            residual(0)

            dve.wait_ge(s_hm, 1)
            for b in range(B):
                for a in range(CT):
                    dve.wait_ge(c_evac, 2 + a)
                    nc.vector.tensor_tensor(k2bd[:, b, a].rearrange("p (h k) -> p h k", h=HB),
                                            k2t[:, a, b].unsqueeze(1).broadcast_to([P, HB, S2]),
                                            head_mask[:].unsqueeze(2).broadcast_to([P, HB, S2]), ALU.mult).then_inc(kv_done, 1)
            dve.wait_ge(ld_ctx, 16 * (B + 3))
            for b in range(B):
                dve.wait_ge(c_ready, 2 + CT + b)
                nc.vector.tensor_tensor(v2[0:S2, b, :, 0:DH], psum[0:S2, 4 + b, 0:C].rearrange("p (h d) -> p h d", h=H),
                                        bias2_row[0:S2, 0, :].rearrange("p (h d) -> p h d", h=H), ALU.add).then_inc(kv_done, 1)
            dve.wait_ge(mask_scaled, 1)

            def cross_scores(j):
                t = j // 2
                dve.wait_ge(s2_ready, j + 1)
                if j >= 4:
                    dve.wait_ge(ptr_ready, 2 * (j - 3))
                nc.vector.tensor_tensor(
                    out=sc[:, j % 4].rearrange("p (b h) k -> p b h k", b=2),
                    in0=psum[:, 2 * (j % 2):2 * (j % 2) + 2, 0:HB // 2 * S2].rearrange("p b (h k) -> p b h k", k=S2),
                    in1=mask_sb[:, t, :].unsqueeze(1).unsqueeze(1).broadcast_to([P, 2, HB // 2, S2]),
                    op=ALU.add).then_inc(sc_done, 1)
                dve.wait_ge(sc_done, j + 1)
                nc.vector.reduce_max(mx2[:, j % 4, :], sc[:, j % 4], AX).then_inc(mx_done, 1)

            def cross_norm(c):
                for g in range(NG):
                    k = NG * c + g
                    dve.wait_ge(ot_ready, k + 1)
                    if k >= 1:
                        dve.wait_ge(y2_done, k)
                    o = psum[:, 4 + g % 2, :].rearrange("p (t h d) -> p t h d", t=QT, h=G)
                    link(nc.vector.reciprocal(rsum[:], o[:, :, :, DH]))
                    b, half = c // 2, c % 2
                    nc.vector.tensor_tensor(y[:, half * QT:(half + 1) * QT, b * NG + g, :].rearrange("p t (h d) -> p t h d", h=G),
                                            o[:, :, :, 0:DH], rsum[:].unsqueeze(3).broadcast_to([P, QT, G, DH]), ALU.mult).then_inc(y2_done, 1)

            for j in range(2 * NT + LAG):
                if j < 2 * NT:
                    cross_scores(j)
                if j >= LAG and (j - LAG) % 8 == 7:
                    cross_norm((j - LAG) // 8)

            residual(1)

            dve.wait_ge(lg_ready, 1)
            dve.wait_ge(s_upto, 1)
            lg = psum[:, 6, 0:NT * E].rearrange("p (t e) -> p t e", e=E)

            def bc(v, n=E):
                return v.unsqueeze(2).broadcast_to([P, v.shape[1], n])

            link(nc.vector.tensor_scalar(e_rows[:, 0], upto[:, 0:E], -1.0, float(E), ALU.mult, ALU.add))
            rank = e_rows[:, 0].unsqueeze(1).broadcast_to([P, NT, E])
            link(nc.vector.reduce_max(row_a, lg, AX))
            nc.vector.tensor_tensor(prob, lg, bc(row_a), ALU.subtract).then_inc(lg_sub, 1)
            dve.wait_ge(lg_exp, 1)
            link(nc.vector.reduce_sum(row_a, prob, AX))
            link(nc.vector.reciprocal(row_a, row_a))
            link(nc.vector.tensor_tensor(prob, prob, bc(row_a), ALU.mult))
            for pr, one, top in ((prob, first, top1), (prob2, second, top2)):
                link(nc.vector.reduce_max(top, pr, AX))
                link(nc.vector.tensor_tensor(one, pr, bc(top), ALU.is_equal))
                link(nc.vector.tensor_tensor(one, one, rank, ALU.mult))
                link(nc.vector.reduce_max(row_a, one, AX))
                link(nc.vector.tensor_tensor(one, one, bc(row_a), ALU.is_equal))
                if one is first:
                    link(nc.vector.scalar_tensor_tensor(out=prob2, in0=one, scalar=-2.0, in1=pr, op0=ALU.mult, op1=ALU.add))
            nc.vector.tensor_tensor(chosen, first, second, ALU.add).then_inc(mask_ready, 1)
            link(nc.vector.tensor_tensor(row_a, top1, top2, ALU.add))
            link(nc.vector.reciprocal(row_a, row_a))
            link(nc.vector.tensor_tensor(share1, top1, row_a, ALU.mult))
            link(nc.vector.tensor_tensor(share2, top2, row_a, ALU.mult))
            dve.wait_ge(ranks_ready, 1)
            link(nc.vector.tensor_copy(counts, psum[:, 5, 0:NT * E].rearrange("p (t e) -> p t e", e=E)))
            src, dst = counts, scan_a
            shift = 1
            while shift < NT:
                link(nc.vector.tensor_copy(dst[:, 0:shift], src[:, 0:shift]))
                link(nc.vector.tensor_tensor(dst[:, shift:], src[:, shift:], src[:, 0:NT - shift], ALU.add))
                src, dst = dst, (scan_b if dst is scan_a else scan_a)
                shift *= 2
            total, tiles, ends, other = (e_rows[:, i] for i in range(4))
            link(nc.vector.tensor_scalar(total, src[:, NT - 1], 1.0 / P, None, ALU.mult))
            begun = many[:, :, 0:NT]
            link(nc.vector.tensor_tensor(begun, bc(total, NT), upto[:, 0:NT].unsqueeze(1).broadcast_to([P, E, NT]), ALU.is_gt))
            link(nc.vector.reduce_sum(tiles, begun, AX))
            a, z = tiles, ends
            shift = 1
            while shift < E:
                link(nc.vector.tensor_copy(z[:, 0:shift], a[:, 0:shift]))
                link(nc.vector.tensor_tensor(z[:, shift:], a[:, shift:], a[:, 0:E - shift], ALU.add))
                a, z = z, (other if z is ends else ends)
                shift *= 2
            of_tile = many.rearrange("p a b -> p (a b)")[:, 0:SLOT_TILES * (E - 1)].rearrange("p (i e) -> p i e", e=E - 1)
            link(nc.vector.tensor_tensor(of_tile, a[:, 0:E - 1].unsqueeze(1).broadcast_to([P, SLOT_TILES, E - 1]),
                                         bc(upto[:, 0:SLOT_TILES], E - 1), ALU.is_le))
            link(nc.vector.reduce_sum(tile_e[:, 0:SLOT_TILES], of_tile, AX))
            link(nc.vector.tensor_copy(tile_expert[:, 0:SLOT_TILES], tile_e[:, 0:SLOT_TILES]))
            link(nc.vector.tensor_tensor(z, a, tiles, ALU.subtract))
            link(nc.vector.tensor_scalar(z, z, float(P), None, ALU.mult))
            link(nc.vector.tensor_tensor(before, src, counts, ALU.subtract))
            link(nc.vector.tensor_tensor(before, before, z.unsqueeze(1).broadcast_to([P, NT, E]), ALU.add))
            link(nc.vector.tensor_tensor(before, before, psum[:, 4, 0:NT * E].rearrange("p (t e) -> p t e", e=E), ALU.add))
            for one, place in ((first, place1), (second, place2)):
                link(nc.vector.tensor_tensor(weigh, one, before, ALU.mult))
                link(nc.vector.reduce_sum(place, weigh, AX))
            nc.vector.tensor_copy(places[:, :, :], rows[:, 5:7]).then_inc(placed, 1)

            def up_bias(i, s):
                e = dve.value_load(tile_expert[0:1, bass.ds(i, 1)], min_val=0, max_val=E - 1)
                dve.wait_ge(up_ready, i + 1)
                if not (isinstance(i, int) and i < 2):
                    dve.wait_ge(hid_tr, i - 1)
                nc.vector.tensor_tensor(hid[:, s], psum[:, s, :], b1_rows[:, bass.ds(e * HID, HID)], ALU.add).then_inc(hid_done, 1)

            def down_bias(i, s):
                e = dve.value_load(tile_expert[0:1, bass.ds(i, 1)], min_val=0, max_val=E - 1)
                dve.wait_ge(down_ready, i + 1)
                if not (isinstance(i, int) and i < 2):
                    dve.wait_ge(ys_stored[s], ys_turn(i, s))
                nc.vector.tensor_tensor(y_out[:, s], psum[:, 4 + s, 0:C], b2_rows[:, bass.ds(e * C, C)], ALU.add).then_inc(y_biased, 1)

            def ys_turn(i, s):
                return (i - s) * 8

            dve.wait_ge(placed, 1)
            dve.wait_ge(ld_w2, 16 * (2 + E))
            up_bias(0, 0)
            up_bias(1, 1)
            down_bias(0, 0)
            up_bias(2, 0)
            down_bias(1, 1)
            with dve.Fori(1, (SLOT_TILES - 1) // 2) as m:
                up_bias(m * 2 + 1, 1)
                down_bias(m * 2, 0)
                up_bias(m * 2 + 2, 0)
                down_bias(m * 2 + 1, 1)
            down_bias(SLOT_TILES - 1, 0)

            for t in range(NT + 1):
                if t < NT:
                    dve.wait_ge(got[t % 4], 32 * (t // 4 + 1))
                    for k, share in enumerate((share1, share2)):
                        nc.vector.scalar_tensor_tensor(out=x_sb[:, t, :], in0=gathered[:, t % 4, k], scalar=share[:, t:t + 1],
                                                       in1=x_sb[:, t, :], op0=ALU.mult, op1=ALU.add).then_inc(mixed, 1)
                        dve.wait_ge(mixed, 2 * t + k + 1)
                    norm_stats(t, 2 * NT + t)
                if t >= 1:
                    norm_apply(t - 1, 2 * NT + t - 1)

        @block.tensor
        def _(pe):
            pe.wait_ge(s_ident, 1)
            pe.wait_ge(s_identb, 1)
            for k in range(16):
                if k >= 4:
                    pe.wait_ge(t_evac, k - 3)
                if k < 8:
                    a, g = k // 4, k % 4
                    pe.wait_ge(ld_x, 16 * 4)
                    for i in range(4):
                        mm = pe.transpose(psum[:, k % 4, i * P:(i + 1) * P], x_sb[:, 4 * g + i, a * P:(a + 1) * P], ident[:])
                else:
                    m = (k - 8 + 4) % 8
                    pe.wait_ge(ld_w, 16 * 8)
                    if m < 4:
                        pe.wait_ge(s_bin, 1)
                    src = w_bin[:, m] if m < 4 else w_raw[:, m]
                    for a in range(CT):
                        for o in range(CT):
                            mm = pe.transpose(psum[:, k % 4, (a * CT + o) * P:(a * CT + o + 1) * P],
                                              src[:, o, a * P:(a + 1) * P], ident[:])
                mm.then_inc(t_ready, 1)
            pe.wait_ge(t_evac, 16)
            for b in range(B):
                for j in range(8 * b, 8 * b + 8):
                    m, o, ch = j // 4 % 2, j // 2 % 2, j % 2
                    if j >= 4:
                        pe.wait_ge(r_done, j - 3)
                    t0 = b * T + ch * HALF
                    for a in range(CT):
                        mm = pe.matmul(psum[:, 4 + j % 4, :], wt[:, m, a, o * P:(o + 1) * P], xt[:, a, t0:t0 + HALF],
                                       start=(a == 0), stop=(a == CT - 1))
                    mm.then_inc(qk_ready, 1)
                for j in range(4 * b, 4 * b + 4):
                    if j >= 4:
                        pe.wait_ge(v_evac, j - 3)
                    for k in range(2):
                        t0 = (2 * j + k) * P
                        for a in range(CT):
                            mm = pe.matmul(psum[:, j % 4, k * C:(k + 1) * C], xt[:, a, t0:t0 + P], wt[:, 2, a, :],
                                           start=(a == 0), stop=(a == CT - 1))
                    mm.then_inc(vp_ready, 1)

            def max_tile(n, i, k, slot, free):
                h, t = i // QT, i % QT
                if free is not None:
                    pe.wait_ge(sm_free, free)
                q = max_q[0]
                for c in range(T // 512):
                    mm = pe.matmul(psum[:, 2 * slot + c, :], stack_ap(q_stack, n, slice(0, STACK), h, q * HALF + t * P, P),
                                   stack_ap(k_stack, n, slice(0, STACK), h, c * 512, 512), start=True, stop=True)
                mm.then_inc(sm_ready, 1)

            max_q = [0]

            def shift_tile(q, k, slot, parts):
                pe.wait_ge(parts_done, parts)
                pe.wait_ge(sm_free, k - 1)
                dst = psum[:, 2 * slot, :].bitcast(BF16)[:, 0:P]
                pe.transpose(dst, mparts[:, q].rearrange("p j c -> p (j c)"), ident_b[:]).then_inc(sm_ready, 1)

            def out_tile(k, slot, copied):
                pe.wait_ge(o_copied, copied)
                pe.wait_ge(sm_free, k - 1)
                for t in range(QT):
                    mm = pe.transpose(psum[:, 2 * slot, t * P:(t + 1) * P], o_sb[:, t * P:(t + 1) * P], ident[:])
                mm.then_inc(sm_ready, 1)

            def scores(n, q, kt, first, heads):
                u = n * 2 + q
                if kt == 0 and 0 in heads:
                    pe.wait_ge(rows_loaded[q], n * 16 + 16)
                for h in heads:
                    i = kt * G + h
                    if i >= 3:
                        pe.wait_ge(exp_done, u * 32 + (i - 2))
                    elif not first:
                        pe.wait_ge(exp_done, u * 32 + (-1, 0, -2)[i])
                    pe.matmul(psum[:, ST_BANK + i % 3, :], stack_ap(k_stack, n, slice(0, STACK + 3), h, kt * P, P),
                              stack_ap(q_stack, n, slice(0, STACK + 3), h, q * HALF, HALF), start=True, stop=True).then_inc(st_ready, 1)

            def values(n, q, kt, first):
                u = n * 2 + q
                pe.wait_ge(exp_done, u * 32 + (4 * kt + 4))
                if kt == 0:
                    pe.wait_ge(v_loaded[q], n * 16 + 16)
                    if not first:
                        pe.wait_ge(o_copied, u)
                for h in range(G):
                    mm = pe.matmul(psum[32 * h:32 * h + 32, O_BANK, :], v_ring[:, q, kt, 32 * h:32 * h + 32],
                                   probs[:, kt % 2 * G + h, :], start=(kt == 0), stop=(kt == TB - 1))
                mm.then_inc(pv_done, 1)

            pe.wait_ge(r_done, 16)
            pe.wait_ge(v_evac, 8)
            pe.wait_ge(stack_loaded, STACK_LOADS)
            pe.wait_ge(s_ones, 1)
            for u in range(2):
                max_q[0] = u
                for i in range(G * QT):
                    k = u * G * QT + i
                    max_tile(0, i, k, i % 2, k - 1 if k >= 2 else None)
            shift_tile(0, SM_FIRST, 0, 1)

            def unit_pe(n, q, first=False, maxima=True, rows=True, k0=None):
                u = n * 2 + q
                max_q[0] = q

                def maxima_of(i):
                    if maxima:
                        max_tile(n + 1, i, sm_index(u, max_pos(i), first), sm_slot(max_pos(i), first), sm_index(u, max_pos(i), first) - 1)

                if maxima and q == 0:
                    pe.wait_ge(stack_loaded, n * STACK_LOADS + 2 * STACK_LOADS)
                for kt in range(TB):
                    if kt == 2:
                        k = sm_index(u, OT_POS, first) if k0 is None else k0
                        if not first:
                            out_tile(k, sm_slot(OT_POS, first) if k0 is None else k0 % 2, u)
                        if rows:
                            k = k + 1
                            shift_tile(1 - q, k, sm_slot(MT_POS, first) if k0 is None else (k0 + 1) % 2, u + 2)
                    maxima_of(2 * kt)
                    scores(n, q, kt, first, (0, 1))
                    maxima_of(2 * kt + 1)
                    scores(n, q, kt, first, (2, 3))
                    if kt >= 1:
                        values(n, q, kt - 1, first)
                    elif not first:
                        values(n if q else n - 1, 1 - q, TB - 1, False)

            unit_pe(0, 0, first=True)
            unit_pe(0, 1)
            with pe.Fori(1, BLOCKS - 1) as n:
                unit_pe(n, 0)
                unit_pe(n, 1)
            k0 = sm_index(UNITS - 2, 0, False)
            unit_pe(BLOCKS - 1, 0, maxima=False, k0=k0)
            unit_pe(BLOCKS - 1, 1, maxima=False, rows=False, k0=k0 + 2)
            values(BLOCKS - 1, 1, TB - 1, False)
            out_tile(k0 + 3, 1, UNITS)

            def project(stage):
                base, m = stage * NT, 3 + 4 * stage
                if stage == 0:
                    pe.wait_ge(sm_free, k0 + 4)
                    pe.wait_ge(exp_done, 32 * UNITS)
                else:
                    pe.wait_ge(y2_done, 4 * NG)
                for t in range(NT + 2):
                    k = base + t
                    b, tt = t // TB, t % TB
                    if t < NT:
                        if k >= 2:
                            pe.wait_ge(yt_evac, k - 1)
                        for a in range(CT):
                            mm = pe.transpose(psum[:, t % 2, a * P:(a + 1) * P],
                                              y[:, tt, b * NG + 2 * a:b * NG + 2 * a + 2, :].rearrange("p n c -> p (n c)"), ident[:])
                        mm.then_inc(yt_ready, 1)
                        pe.wait_ge(yt_evac, k + 1)
                        if k >= 2:
                            pe.wait_ge(added, k - 1)
                        for a in range(CT):
                            mm = pe.matmul(psum[:, 2 + t % 2, 0:C], yt[:, t % 2, a, :], wt[:, m, a, :], start=(a == 0), stop=(a == CT - 1))
                        mm.then_inc(pj_ready, 1)
                    if t >= 2:
                        pe.wait_ge(ln_done, k - 1)
                        if k >= 4:
                            pe.wait_ge(xt_evac, k - 3)
                        for a in range(CT):
                            mm = pe.transpose(psum[:, 4 + t % 2, a * P:(a + 1) * P], x_sb[:, t - 2, a * P:(a + 1) * P], ident[:])
                        mm.then_inc(xt_ready, 1)

            project(0)

            pe.wait_ge(ld_ctx, 16 * (B + 3))
            for a in range(CT):
                for b in range(B):
                    mm = pe.transpose(psum[:, 6, (a * B + b) * S2:(a * B + b + 1) * S2], ctx_sb[0:S2, b, a * P:(a + 1) * P], ident[0:S2, 0:S2])
            mm.then_inc(c_ready, 1)
            pe.wait_ge(c_evac, 1)
            for o in range(CT):
                for a in range(CT):
                    mm = pe.matmul(psum[:, 7 if o else 6, 0:B * S2], wt[:, 5, a, o * P:(o + 1) * P],
                                   ctx_t[:, a].rearrange("p b k -> p (b k)"), start=(a == 0), stop=(a == CT - 1))
                mm.then_inc(c_ready, 1)
            pe.wait_ge(xt_evac, NT)
            for b in range(B):
                for a in range(CT):
                    mm = pe.matmul(psum[0:S2, 4 + b, 0:C], ctx_t[:, a, b, :], wt[:, 6, a, :], start=(a == 0), stop=(a == CT - 1))
                mm.then_inc(c_ready, 1)
            for j in range(8):
                o, ch = j // 4, j % 4
                if j >= 4:
                    pe.wait_ge(q2_evac, j - 3)
                for a in range(CT):
                    mm = pe.matmul(psum[:, j % 4, :], wt[:, 4, a, o * P:(o + 1) * P], xt[:, a, 512 * ch:512 * (ch + 1)],
                                   start=(a == 0), stop=(a == CT - 1))
                mm.then_inc(q2_ready, 1)
            pe.wait_ge(q2_evac, 8)
            pe.wait_ge(c_evac, 1 + CT)
            pe.wait_ge(kv_done, B * CT + B)
            pe.wait_ge(v2_ones, 1)

            def cross_s(j):
                t, a = j // 2, j % 2
                if j >= 2:
                    pe.wait_ge(sc_done, j - 1)
                n_ = HB // 2 * S2
                for s in range(2):
                    mm = pe.matmul(psum[:, 2 * (j % 2) + s, 0:n_], q2t[:, a, t * P:(t + 1) * P],
                                   k2bd[:, t // TB, a, s * n_:(s + 1) * n_], start=True, stop=True)
                mm.then_inc(s2_ready, 1)

            def cross_t(j):
                c, a = j // 8, j % 2
                pe.wait_ge(exp2_done, j + 1)
                for s in range(2):
                    if j >= 1:
                        pe.wait_ge(ptr_evac, 2 * j + s - 1)
                    if j % 8 == 0 and c >= 1:
                        pe.wait_ge(y2_done, 4 * c)
                    for h in range(4):
                        mm = pe.transpose(psum[0:S2, 4 + s, h * P:(h + 1) * P], sc[:, j % 4, 4 * s + h, :], ident[:])
                    mm.then_inc(ptr_ready, 1)

            def cross_pv(c):
                b = c // 2
                pe.wait_ge(ptr_evac, 16 * (c + 1))
                for g in range(NG):
                    k = NG * c + g
                    if k >= 2:
                        pe.wait_ge(o2_copied, k - 1)
                    for h in range(G):
                        mm = pe.matmul(psum[32 * h:32 * h + 32, 6 + g % 2, :], v2[0:S2, b, G * g + h, :],
                                       pt[0:S2, G * g + h, :], start=True, stop=True)
                    mm.then_inc(pv2_ready, 1)
                    if g >= 1:
                        cross_o(k - 1)
                cross_o(NG * c + NG - 1)

            def cross_o(k):
                pe.wait_ge(o2_copied, k + 1)
                if k >= 2:
                    pe.wait_ge(y2_done, k - 1)
                for t in range(QT):
                    mm = pe.transpose(psum[:, 4 + k % 2, t * P:(t + 1) * P], o2_sb[:, k % 2, t * P:(t + 1) * P], ident[:])
                mm.then_inc(ot_ready, 1)

            for j in range(2 * NT + LAG):
                if j < 2 * NT:
                    cross_s(j)
                if j >= LAG:
                    cross_t(j - LAG)
                    if (j - LAG) % 8 == 7:
                        cross_pv((j - LAG) // 8)

            project(1)

            pe.wait_ge(xt_evac, 2 * NT)
            pe.wait_ge(ld_wg, 16)
            for t in range(NT):
                for a in range(CT):
                    mm = pe.matmul(psum[:, 6, t * E:(t + 1) * E], xt[:, a, t * P:(t + 1) * P], wg_sb[:, a, :], start=(a == 0), stop=(a == CT - 1))
            mm.then_inc(lg_ready, 1)
            pe.wait_ge(mask_ready, 1)
            pe.wait_ge(s_tri, 1)
            flat = chosen.rearrange("p t e -> p (t e)")
            pe.matmul(psum[:, 4, 0:NT * E], earlier, flat, start=True, stop=True)
            pe.matmul(psum[:, 5, 0:NT * E], ones, flat, start=True, stop=True).then_inc(ranks_ready, 1)
            pe.wait_ge(placed, 1)

            def tokens_in(i, s, loaded):
                pe.wait_ge(xs_loaded[s], loaded)
                if not (isinstance(i, int) and i < 2):
                    pe.wait_ge(xst_evac, i - 1)
                for a in range(CT):
                    mm = pe.transpose(psum[:, 6 + s, a * P:(a + 1) * P], xs_in[:, s, a * P:(a + 1) * P], ident[:])
                mm.then_inc(xs_t, 1)

            def up(i, s):
                e = pe.value_load(tile_expert[0:1, bass.ds(i, 1)], min_val=0, max_val=E - 1)
                pe.wait_ge(xst_evac, i + 1)
                if not (isinstance(i, int) and i < 2):
                    pe.wait_ge(hid_done, i - 1)
                for a in range(CT):
                    mm = pe.matmul(psum[:, s, :], xst[:, s, a, :], w1_sb[:, bass.ds(e, 1), a, :],
                                   start=(a == 0), stop=(a == CT - 1))
                mm.then_inc(up_ready, 1)

            def turn(i, s):
                pe.wait_ge(hid_done, i + 1)
                if not (isinstance(i, int) and i < 2):
                    pe.wait_ge(relu_done, i - 1)
                for a in range(HT):
                    mm = pe.transpose(psum[:, 2 + s, a * P:(a + 1) * P], hid[:, s, a * P:(a + 1) * P], ident[:])
                mm.then_inc(hid_tr, 1)

            def down(i, s):
                e = pe.value_load(tile_expert[0:1, bass.ds(i, 1)], min_val=0, max_val=E - 1)
                pe.wait_ge(relu_done, i + 1)
                if not (isinstance(i, int) and i < 2):
                    pe.wait_ge(y_biased, i - 1)
                for a in range(HT):
                    mm = pe.matmul(psum[:, 4 + s, 0:C], hid_t[:, s, a, :], w2_sb[:, bass.ds(e, 1), a, :],
                                   start=(a == 0), stop=(a == HT - 1))
                mm.then_inc(down_ready, 1)

            def expert_step(i, s, loaded):
                up(i, s)
                if loaded is not None:
                    tokens_in(i + 1, 1 - s, loaded)
                if not (isinstance(i, int) and i == 0):
                    down(i - 1, 1 - s)
                turn(i, s)

            pe.wait_ge(ld_w2, 16 * (2 + E))
            pe.wait_ge(ld_w1, 16 * E)
            tokens_in(0, 0, 16)
            expert_step(0, 0, 16)
            expert_step(1, 1, 32)
            expert_step(2, 0, 32)
            with pe.Fori(1, (SLOT_TILES - 3) // 2) as m:
                expert_step(m * 2 + 1, 1, m * 16 + 32)
                expert_step(m * 2 + 2, 0, m * 16 + 32)
            expert_step(SLOT_TILES - 2, 1, 16 * ((SLOT_TILES + 1) // 2))
            expert_step(SLOT_TILES - 1, 0, None)
            down(SLOT_TILES - 1, 0)


_INS = ["x", "ctx_1024", "mask_Bx1xSxS2_fk0",
        "L0_attn_Wq", "L0_attn_Wk", "L0_attn_Wv", "L0_attn_Wp", "L0_attn_bq", "L0_attn_bk", "L0_attn_bv", "L0_attn_bp",
        "L0_xattn_Wq", "L0_xattn_Wk", "L0_xattn_Wv", "L0_xattn_Wo", "L0_xattn_bq", "L0_xattn_bk", "L0_xattn_bv", "L0_xattn_bo",
        "L0_ffn_Wg", "L0_ffn_W1", "L0_ffn_b1", "L0_ffn_W2", "L0_ffn_b2"]


def kernel(**inputs):
    import numpy as np
    import concourse.bacc as bacc
    from concourse.bass_utils import run_bass_kernel_spmd

    nc = bacc.Bacc("TRN2", target_bir_lowering=False, num_devices=1)
    arrays, a = {}, {}
    for name in _INS:
        arrays[f"in_{name}"] = np.ascontiguousarray(inputs[name])
        a[name] = nc.dram_tensor(f"in_{name}", arrays[f"in_{name}"].shape, F32, kind="ExternalInput").ap()
    out = nc.dram_tensor("out", a["x"].shape, F32, kind="ExternalOutput").ap()

    def group(prefix, names):
        return [a[f"L0_{prefix}_{n}"] for n in names]

    decoder_layer(nc, a["x"], a["ctx_1024"], a["mask_Bx1xSxS2_fk0"],
                  group("attn", ("Wq", "Wk", "Wv", "Wp")), group("attn", ("bq", "bk", "bv", "bp")),
                  group("xattn", ("Wq", "Wk", "Wv", "Wo")), group("xattn", ("bq", "bk", "bv", "bo")),
                  *group("ffn", ("Wg", "W1", "b1", "W2", "b2")), out)
    r = run_bass_kernel_spmd(nc, [arrays], core_ids=[0])
    return r.results[0]["out"]
```

```python
from contextlib import ExitStack

import concourse.bass as bass
from concourse import mybir

F32 = mybir.dt.float32
BF16 = mybir.dt.bfloat16
ALU = mybir.AluOpType
ACT = mybir.ActivationFunctionType
AX = mybir.AxisListType.X

P = 128
EPS = 1e-5
MASK_WEIGHT = 1000000.0


def decoder_layer(nc, x, ctx_in, mask, attn_w, attn_b, cross_w, cross_b, Wg, W1, b1, W2, b2, out):
    B, T, C = x.shape
    S2 = ctx_in.shape[1]
    H = 16
    DH = C // H
    CT = C // P
    NT = B * T // P
    TB = T // P
    E, _, HID = W1.shape
    HT = HID // P
    G = 4
    NG = H // G
    BLOCKS = B * NG
    HALF = 512
    UNITS = BLOCKS * (T // HALF)
    QT = HALF // P
    STACK = 6 * DH
    SCALE = float(DH) ** -0.5
    BLOCK_COLS = G * T

    with ExitStack() as scope:
        def sb(name, shape, dt=F32):
            return scope.enter_context(nc.sbuf_tensor(name, shape, dt))

        def sem(name):
            return scope.enter_context(nc.semaphore(name))

        def dram(name, shape, dt):
            return nc.dram_tensor(name, shape, dt).ap()

        qk_parts = dram("qk_parts", (2, 3, B, C, T), BF16)
        v_heads = dram("v_heads", (BLOCKS, T, G * 32), F32)
        shift_rows = dram("shift_rows", (2, 3 * G * QT, P), BF16)

        ROOM = B * T + P
        x_sorted = dram("x_sorted", (E * ROOM, C + 2), F32)
        y_token = dram("y_token", (2 * B * T + E * P, C), F32)

        big = sb("big", [P, 2 * BLOCKS * BLOCK_COLS], BF16)
        q_stack = big[:, 0:BLOCKS * BLOCK_COLS]
        k_stack = big[:, BLOCKS * BLOCK_COLS:]
        big_f = big[:].bitcast(F32)
        xt = sb("xt", [P, CT, B * T])
        probs = xt[:].rearrange("p a t -> p (a t)").rearrange("p (s q) -> p s q", q=HALF)
        v_ring = sb("v_ring", [P, 2, T // P, G * 32])
        number = sb("number", [P, NT], mybir.dt.int32)
        y = sb("y", [P, TB, BLOCKS, G * DH])
        x_ext = sb("x_ext", [P, NT, C + 2])
        x_sb = x_ext[:, :, 0:C]
        wt = sb("wt", [P, 8, CT, C])
        ident = sb("ident", [P, P])
        ident_b = sb("ident_b", [P, P], BF16)
        bias_col = sb("bias_col", [P, 4, CT])
        bias_row = sb("bias_row", [P, 2, C])
        o_sb = sb("o_sb", [P, HALF])
        alpha = sb("alpha", [P, 8])
        stat = sb("stat", [P, 2, G * QT])
        mparts = sb("mparts", [P, 2, P // (G * QT), G * QT], BF16)
        minus_one = sb("minus_one", [P, G * QT])
        mres = sb("mres", [P, 2, G * QT])
        m_rows = sb("m_rows", [P, 2, P], BF16)
        rsum = sb("rsum", [P, QT, G])
        head_mask = sb("head_mask", [P, P // DH])
        NS = 8
        bn = sb("bn", [P, NS, 6])
        mv = sb("mv", [P, NS, 2])
        std = sb("std", [P, NS])
        waited = sb("waited", [P, 2])
        shift = sb("shift", [P, NS])

        y_flat = y[:].rearrange("p t n c -> p (t n c)")
        w_raw = y_flat.rearrange("p (m a c) -> p m a c", m=8, a=CT)
        resid = y_flat[:, 0:1024].rearrange("p (s q) -> p s q", s=2)
        split_y = y_flat[:, 1024:4096].bitcast(BF16).rearrange("p (s j q) -> p s j q", s=4, j=3)
        split_k = k_stack[:, BLOCKS // 2 * BLOCK_COLS:][:, 0:10 * 3 * 512].rearrange("p (s j q) -> p s j q", s=10, j=3)

        def split(j):
            return split_y[:, j % 14] if j % 14 < 4 else split_k[:, j - 4]

        v_flat = v_ring[:].rearrange("p s k c -> p (s k c)")
        w_bin = v_flat.rearrange("p (m a c) -> p m a c", m=4, a=CT)
        v_stage = q_stack[:, BLOCKS // 2 * BLOCK_COLS:].bitcast(F32).rearrange("p (s k h d) -> p s k h d", s=NT // 2, k=2, h=H)

        psum = scope.enter_context(nc.psum_tensor("psum", [P, 8, 512], F32))

        pos = [0]

        def carve(n):
            pos[0] += n
            return big_f[:, pos[0] - n:pos[0]]

        w1_sb = carve(E * CT * HID).rearrange("p (e a h) -> p e a h", e=E, a=CT)
        q2t = carve(CT * B * T).rearrange("p (a t) -> p a t", a=CT)
        pt = carve(H * HALF).rearrange("p (h q) -> p h q", h=H)
        HB = P // DH
        k2bd = carve(B * CT * HB * S2).rearrange("p (b a k) -> p b a k", b=B, a=CT)
        v2 = carve(B * H * 32).rearrange("p (b h d) -> p b h d", b=B, h=H)
        ctx_sb = carve(B * C).rearrange("p (b c) -> p b c", b=B)
        ctx_t = carve(CT * B * S2).rearrange("p (a b k) -> p a b k", a=CT, b=B)
        k2t = carve(CT * B * S2).rearrange("p (a b k) -> p a b k", a=CT, b=B)
        bias2_row = carve(2 * C).rearrange("p (i c) -> p i c", i=2)
        mask_sb = carve(NT * S2).rearrange("p (t k) -> p t k", t=NT)
        FILLED = pos[0]
        sc = carve(4 * HB * S2).rearrange("p (s h k) -> p s h k", s=4, h=HB)
        mx2 = carve(4 * HB).rearrange("p (s h) -> p s h", s=4)
        o2_sb = carve(2 * HALF).rearrange("p (g q) -> p g q", g=2)
        YT_AT = pos[0]
        yt = carve(2 * C).rearrange("p (s a q) -> p s a q", s=2, a=CT)
        assert pos[0] <= big_f.shape[1]
        last_q, last_k = (BLOCKS - 1) * BLOCK_COLS // 2, (2 * BLOCKS - 1) * BLOCK_COLS // 2
        assert E * CT * HID + CT * B * T <= last_q and FILLED <= last_k
        pos[0] = E * CT * HID
        SLOT_TILES = (2 * B * T + E * (P - 1)) // P
        w2_sb = carve(E * HT * C).rearrange("p (e a c) -> p e a c", e=E, a=HT)
        b1_in = carve(P)[0:E * HT]
        b1_col = carve(E * HT).rearrange("p (e a) -> p e a", e=E)
        b2_rows = carve(E * C)
        wg_sb = carve(CT * E).rearrange("p (a e) -> p a e", a=CT)
        route = carve(8 * NT * E).rearrange("p (n t e) -> p n t e", n=8, t=NT)
        prob, others, first, second, chosen, before, weigh, logits = (route[:, i] for i in range(8))
        rows = carve(10 * NT).rearrange("p (n t) -> p n t", n=10)
        row_a, top1, top2, share1, share2, place1, place2, best, row_b, row_c = (rows[:, i] for i in range(10))
        upto_row = carve((NT + 1) * E).rearrange("p (t e) -> p t e", e=E)
        upto = carve(48)
        upto_i = carve(48).bitcast(mybir.dt.int32)
        earlier = carve(P)
        ones = carve(P)
        many = carve(E * 48).rearrange("p (a b) -> p a b", b=48)
        e_rows = carve(4 * E).rearrange("p (n e) -> p n e", n=4)
        tile_e = carve(48)
        tile_expert = carve(48).bitcast(mybir.dt.int32)
        tile_row = carve(48)
        tile_place = carve(48).bitcast(mybir.dt.int32)
        real = carve(48)
        fill_row = carve(E).bitcast(mybir.dt.int32)
        fill = carve(E * (C + 2)).rearrange("p (e c) -> p e c", e=E)
        fill_id = carve(E).bitcast(mybir.dt.int32)
        of_two, noted = carve(2), carve(2)
        dest = carve(2).bitcast(mybir.dt.uint32)
        places = carve(2 * NT).bitcast(mybir.dt.uint32).rearrange("p (k t) -> p k t", k=2)
        assert pos[0] <= YT_AT
        xt_flat = xt[:].rearrange("p a t -> p (a t)")
        pos[0] = 0

        def carve_xt(n):
            pos[0] += n
            return xt_flat[:, pos[0] - n:pos[0]]

        w1_now = v_flat.rearrange("p (s a h) -> p s a h", s=2, a=CT)
        xs_in = carve_xt(2 * (C + 2)).rearrange("p (s c) -> p s c", s=2)
        xst = carve_xt(2 * C).rearrange("p (s a q) -> p s a q", s=2, a=CT)
        hid = carve_xt(2 * HID).rearrange("p (s a q) -> p s a q", s=2, a=HT)
        hid_t = carve_xt(2 * HID).rearrange("p (s a q) -> p s a q", s=2, a=HT)
        y_out = carve_xt(2 * C).rearrange("p (s c) -> p s c", s=2)
        assert pos[0] <= CT * B * T
        gathered = big_f[:, 0:2 * NT * C].rearrange("p (k t c) -> p t k c", k=2, t=NT)
        assert 2 * NT * C <= E * CT * HID

        s_ident, s_identb = sem("s_ident"), sem("s_identb")
        s_hm = sem("s_hm")
        ld_w, ld_cross_w, ld_bias = sem("ld_w"), sem("ld_cross_w"), sem("ld_bias")
        ld_x = [sem(f"ld_x{i}") for i in range(4)]
        s_sign, s_bin = sem("s_sign"), sem("s_bin")
        s_ones = sem("s_ones")
        t_ready, t_evac = sem("t_ready"), sem("t_evac")
        qk_ready, hi_done, r_done, mid_done, lo_done = (sem(n) for n in ("qk_ready", "hi_done", "r_done", "mid_done", "lo_done"))
        part_stored = [sem(f"part_stored{i}") for i in range(4)]
        vp_ready, v_evac = sem("vp_ready"), sem("v_evac")
        v_stored = [sem(f"v_stored{i}") for i in range(2)]
        stack_loaded = sem("stack_loaded")
        v_loaded = [sem(f"v_loaded{i}") for i in range(2)]
        st_ready, exp_done, pv_done, o_copied = sem("st_ready"), sem("exp_done"), sem("pv_done"), sem("o_copied")
        sm_ready, sm_free, dve_own = sem("sm_ready"), sem("sm_free"), sem("dve_own")
        pool_own, parts_done = sem("pool_own"), sem("parts_done")
        rows_stored = sem("rows_stored")
        rows_loaded = [sem(f"rows_loaded{i}") for i in range(2)]
        x_biased = sem("x_biased")
        yt_ready, yt_evac, pj_ready, added, ln_done, xt_ready, xt_evac = (
            sem(n) for n in ("yt_ready", "yt_evac", "pj_ready", "added", "ln_done", "xt_ready", "xt_evac"))
        ld_ctx, c_ready, c_evac, kv_done = sem("ld_ctx"), sem("c_ready"), sem("c_evac"), sem("kv_done")
        q2_ready, q2_evac = sem("q2_ready"), sem("q2_evac")
        s2_ready, sc_done, mx_done, sub_done, exp2_done, ptr_ready, ptr_evac = (
            sem(n) for n in ("s2_ready", "sc_done", "mx_done", "sub_done", "exp2_done", "ptr_ready", "ptr_evac"))
        pv2_ready, o2_copied, ot_ready, y2_done = (sem(n) for n in ("pv2_ready", "o2_copied", "ot_ready", "y2_done"))
        mask_scaled, v2_ones = sem("mask_scaled"), sem("v2_ones")
        ld_w1, ld_w2, ld_wg = sem("ld_w1"), sem("ld_w2"), sem("ld_wg")
        s_upto, s_tri, s_fill, fill_known, fill_stored, tiles_known = (
            sem(n) for n in ("s_upto", "s_tri", "s_fill", "fill_known", "fill_stored", "tiles_known"))
        lg_ready, lg_sub, lg_exp, mask_ready, ranks_ready, placed, scattered = (
            sem(n) for n in ("lg_ready", "lg_sub", "lg_exp", "mask_ready", "ranks_ready", "placed", "scattered"))
        xs_loaded = [sem(f"xs_loaded{i}") for i in range(2)]
        xs_t, xst_evac, up_ready, hid_done, relu_done, down_ready, y_biased = (
            sem(n) for n in ("xs_t", "xst_evac", "up_ready", "hid_done", "relu_done", "down_ready", "y_biased"))
        ys_stored = [sem(f"ys_stored{i}") for i in range(2)]
        RESULT_LOADS = [(0, 1), (1, 2), (2, 4), (4, 8), (8, 12), (12, NT)]
        got = [sem(f"got{i}") for i in range(len(RESULT_LOADS))]
        b1_turned, b1_there, w1_taken = sem("b1_turned"), sem("b1_there"), sem("w1_taken")
        turned, normed = sem("turned"), sem("normed")
        v_ones = sem("v_ones")
        more_ones = sem("more_ones")
        store_turn = sem("store_turn")
        scaled, first_added, rstd_ready, dest_noted, compared = (
            sem(n) for n in ("scaled", "first_added", "rstd_ready", "dest_noted", "compared"))
        dest_done, bn_done, recip_done = sem("dest_done"), sem("bn_done"), sem("recip_done")
        out_stored, stats_done, sqrt_done = sem("out_stored"), sem("stats_done"), sem("sqrt_done")

        x_tok = x.rearrange("b (t p) c -> p (b t) c", p=P)
        out_tok = out.rearrange("b (t p) c -> p (b t) c", p=P)

        SM_UNIT = G * QT + 1
        SM_FIRST = 2 * G * QT + 1
        AHEAD = 6
        FIRST_MT = G * QT + AHEAD
        MT_POS = 4

        def max_pos(i):
            return i if i < MT_POS else i + 1

        def sm_index(u, pos_):
            return u * SM_UNIT + (SM_FIRST + pos_)

        def sm_slot(q, pos_):
            return (SM_FIRST + q * SM_UNIT + pos_) % 2

        ST_BANK, O_BANK = 4, 7
        OT_ENTRY = 8

        LAST_RING = (ST_BANK, ST_BANK + 1, ST_BANK + 2, 0, 1)
        ENTRIES = G * TB + 1

        def last_bank(entry):
            return LAST_RING[entry % len(LAST_RING)]

        def st_bank(i, last_q=None):
            entry = i if i < OT_ENTRY else i + 1
            return ST_BANK + entry % 3 if last_q is None else last_bank(last_q * ENTRIES + entry)

        def ot_bank(last_q=None):
            return ST_BANK + OT_ENTRY % 3 if last_q is None else last_bank(last_q * ENTRIES + OT_ENTRY)


        def sm_tile(slot):
            return psum[:, 2 * slot:2 * slot + 2, :].rearrange("p a q -> p (a q)")

        def stack_ap(stack, n, rows, h, start, size):
            return stack[rows, bass.ds(n * BLOCK_COLS + (h * T + start), size)]

        def stack_block(rows, n):
            return rows[:, bass.ds(n * BLOCK_COLS, BLOCK_COLS)]

        LAG = 3
        GROUPS = [(0, 3), (3, 8), (8, 12), (12, NT)]

        def rank_step(g):
            return GROUPS[g][1] + 9

        STACK_LOADS = 2 * 6 * 16

        block = scope.enter_context(nc.Block())

        @block.sync
        def _(sp):
            for m, w in enumerate(attn_w):
                sp.dma_start(w_raw[:, m], w.rearrange("(a p) c -> p a c", p=P)).then_inc(ld_w, 16)
            for g in range(4):
                sp.dma_start(x_sb[:, 4 * g:4 * g + 4, :], x_tok[:, 4 * g:4 * g + 4, :]).then_inc(ld_x[g], 16)
            for m, w in enumerate(cross_w):
                sp.dma_start(w_raw[:, 4 + m], w.rearrange("(a p) c -> p a c", p=P)).then_inc(ld_cross_w, 16)
            for i, b in enumerate((attn_b[0], attn_b[1], cross_b[0], cross_b[1])):
                sp.dma_start(bias_col[:, i, :], b.rearrange("(a p) -> p a", p=P),
                             allow_slow_non_contiguous=True).then_inc(ld_bias, 16)
            for i, b in enumerate((attn_b[2], attn_b[3])):
                sp.dma_start(bias_row[:, i, :], b.rearrange("(o c) -> o c", o=1).broadcast_to([P, C])).then_inc(ld_bias, 16)

            def store_parts(j):
                b, m, a, ch = j // 8, j // 4 % 2, j // 2 % 2, j % 2
                sp.wait_ge(lo_done, j + 1)
                sp.dma_start(qk_parts[m, :, b, a * P:(a + 1) * P, ch * HALF:(ch + 1) * HALF].rearrange("j o t -> o j t"),
                             split(j)).then_inc(part_stored[j % 4], 16)

            def store_v(j):
                if j == 0:
                    sp.wait_ge(v_ones, 1)
                sp.wait_ge(v_evac, j + 1)
                b, t0 = j // 4, j % 4 * 2 * P
                for k in range(2):
                    sp.dma_start(
                        v_heads[b * NG:(b + 1) * NG, t0 + k * P:t0 + (k + 1) * P, :].rearrange("g p c -> p g c"),
                        v_stage[:, j, k].rearrange("p (g h) d -> p g (h d)", g=NG)).then_inc(v_stored[j % 2], 16)

            by_block = qk_parts.rearrange("m j b (g h d) t -> m j (b g) d h t", g=NG, d=DH)

            def load_stacks(n):
                for m, stack, parts in ((0, q_stack, (0, 0, 0, 1, 1, 2)), (1, k_stack, (0, 1, 2, 0, 1, 0))):
                    for j, part in enumerate(parts):
                        sp.dma_start(stack_block(stack[DH * j:DH * (j + 1)], n).rearrange("d (h t) -> d h t", h=G),
                                     by_block[m, part, bass.ds(n, 1)].rearrange("o d h t -> (o d) h t")).then_inc(stack_loaded, 16)

            for j in range(8):
                store_parts(j)
            for s in range(4):
                sp.wait_ge(part_stored[s], 32)
            load_stacks(0)
            for j in range(4):
                store_v(j)
            sp.wait_ge(stack_loaded, STACK_LOADS)
            load_stacks(1)
            for j in range(4, 4 * B):
                store_v(j)
            for j in range(8, 16):
                store_parts(j)
            for s in range(4):
                sp.wait_ge(part_stored[s], 64)

            def load_v(n, q):
                sp.dma_start(v_ring[:, q], v_heads[bass.ds(n, 1)].rearrange("o (k p) c -> p (o k) c", p=P)
                             ).then_inc(v_loaded[q], 16)

            def move_rows(n, q, u, pos_=MT_POS):
                sp.wait_ge(sm_free, sm_index(u - 1, pos_) + 1)
                sp.dma_start(shift_rows[q], m_rows[0:3 * G * QT, q]).then_inc(rows_stored, 16)
                sp.wait_ge(rows_stored, u * 16 + 16)
                dst = q_stack[STACK:STACK + 3, bass.ds(n * BLOCK_COLS, BLOCK_COLS)].rearrange("p (h t) -> p h t", h=G)
                sp.dma_start(dst[:, :, q * HALF:(q + 1) * HALF],
                             shift_rows[q].rearrange("(j h t) c -> j h (t c)", j=3, h=G)).then_inc(rows_loaded[q], 16)

            for s in range(2):
                sp.wait_ge(v_stored[s], 2 * 16 * 4)
            load_v(0, 0)
            sp.wait_ge(sm_free, FIRST_MT + 1)
            sp.dma_start(shift_rows[0], m_rows[0:3 * G * QT, 0]).then_inc(rows_stored, 16)
            sp.wait_ge(rows_stored, 16)
            sp.dma_start(q_stack[STACK:STACK + 3, 0:BLOCK_COLS].rearrange("p (h t) -> p h t", h=G)[:, :, 0:HALF],
                         shift_rows[0].rearrange("(j h t) c -> j h (t c)", j=3, h=G)).then_inc(rows_loaded[0], 16)

            def units(n, first=False, last=False, stacks=True):
                if stacks:
                    sp.wait_ge(stack_loaded, n * STACK_LOADS + 2 * STACK_LOADS)
                    load_stacks(n + 2)
                if not first:
                    sp.wait_ge(pv_done, n * 16)
                load_v(n, 1)
                move_rows(n, 1, n * 2 + 1, 0 if last else MT_POS)
                if not last:
                    sp.wait_ge(pv_done, n * 16 + 8)
                    load_v(n + 1, 0)
                    move_rows(n + 1, 0, n * 2 + 2)

            units(0, first=True)
            with sp.Fori(1, BLOCKS - 2) as n:
                units(n)
            units(BLOCKS - 2, stacks=False)
            units(BLOCKS - 1, last=True, stacks=False)

            sp.wait_ge(pv_done, 8 * (UNITS - 2))
            for b in range(B):
                sp.dma_start(ctx_sb[0:S2, b, :], ctx_in[b]).then_inc(ld_ctx, 16)
            sp.dma_start(mask_sb[:, :, :], mask.rearrange("b o (t p) k -> p (b o t) k", p=P)).then_inc(ld_ctx, 16)
            for i, b in enumerate((cross_b[2], cross_b[3])):
                sp.dma_start(bias2_row[:, i, :], b.rearrange("(o c) -> o c", o=1).broadcast_to([P, C])).then_inc(ld_ctx, 16)
            for e in range(E):
                sp.dma_start(w1_sb[:, e], W1[e].rearrange("(a p) h -> p a h", p=P)).then_inc(ld_w1, 16)
            sp.wait_ge(y2_done, 4 * NG)
            sp.wait_ge(x_biased, 2 * NT)
            sp.dma_start(wg_sb, Wg.rearrange("(a p) e -> p a e", p=P)).then_inc(ld_wg, 16)
            sp.dma_start(b1_in, b1.rearrange("e (a h) -> (e a) h", a=HT)).then_inc(ld_w2, 16)
            for e in range(E):
                sp.dma_start(w2_sb[:, e], W2[e].rearrange("(a p) c -> p a c", p=P)).then_inc(ld_w2, 16)
            sp.dma_start(b2_rows, b2.rearrange("(o e) c -> o (e c)", o=1).broadcast_to([P, E * C])).then_inc(ld_w2, 16)

            sp.wait_ge(s_fill, 1)
            sp.wait_ge(fill_known, 1)
            for e in range(E):
                row = sp.value_load(fill_row[0:1, e:e + 1], min_val=e * ROOM, max_val=e * ROOM + B * T)
                sp.dma_start(x_sorted[bass.ds(row, P)], fill[:, e]).then_inc(fill_stored, 16)
            sp.wait_ge(tiles_known, 1)
            sp.wait_ge(scattered, 2 * NT * 16)
            sp.wait_ge(fill_stored, E * 16)

            def load_tile(i, s):
                place = sp.value_load(tile_place[0:1, bass.ds(i, 1)], min_val=0, max_val=E * ROOM // P - 1)
                sp.dma_start(xs_in[:, s], x_sorted.rearrange("(n p) c -> n p c", p=P)[bass.ds(place, 1)].rearrange("o p c -> p (o c)")
                             ).then_inc(xs_loaded[s], 16)

            load_tile(0, 0)
            load_tile(1, 1)

            def next_tile(i, s):
                sp.wait_ge(xs_t, i + 1)
                sp.wait_ge(dest_noted, i + 1)
                load_tile(i + 2, s)

            next_tile(0, 0)
            with sp.Fori(0, (SLOT_TILES - 3) // 2) as m:
                next_tile(m * 2 + 1, 1)
                next_tile(m * 2 + 2, 0)

            for s in range(2):
                sp.wait_ge(ys_stored[s], 16 * ((SLOT_TILES + 1 - s) // 2))
            by_choice = y_token[0:2 * B * T].rearrange("(k t p) c -> k p t c", k=2, p=P)
            for g, (t0, t1) in enumerate(RESULT_LOADS):
                for k in range(2):
                    sp.dma_start(gathered[:, t0:t1, k], by_choice[k, :, t0:t1]).then_inc(got[g], 16)
            for g in range(NT):
                sp.wait_ge(ln_done, 2 * NT + g + 1)
                sp.dma_start(out_tok[:, g:g + 1, :], x_sb[:, g:g + 1, :]).then_inc(out_stored, 16)
            sp.wait_ge(out_stored, 16 * NT)

        @block.gpsimd
        def _(pool):
            own = [0]

            def link(ins):
                own[0] += 1
                ins.then_inc(pool_own, 1)
                pool.wait_ge(pool_own, own[0])

            link(nc.gpsimd.memset(ident[:], 0.0))
            nc.gpsimd.affine_select(out=ident[:], in_=ident[:], compare_op=ALU.not_equal, fill=1.0, base=0,
                                    pattern=[[-1, P]], channel_multiplier=1).then_inc(s_ident, 1)
            pool.wait_ge(s_ident, 1)
            nc.gpsimd.tensor_copy(ident_b[:], ident[:]).then_inc(s_identb, 1)
            nc.gpsimd.memset(v_stage[:, :, :, :, DH:32], 1.0).then_inc(v_ones, 1)
            link(nc.gpsimd.memset(head_mask[:], SCALE))
            link(nc.gpsimd.affine_select(out=head_mask[:], in_=head_mask[:], compare_op=ALU.is_ge, fill=0.0, base=0,
                                         pattern=[[-DH, P // DH]], channel_multiplier=1))
            nc.gpsimd.affine_select(out=head_mask[:], in_=head_mask[:], compare_op=ALU.is_ge, fill=0.0, base=DH - 1,
                                    pattern=[[DH, P // DH]], channel_multiplier=-1).then_inc(s_hm, 1)
            link(nc.gpsimd.memset(minus_one[:], -1.0))
            link(nc.gpsimd.memset(mparts[:], 0.0))
            link(nc.gpsimd.iota(number[:], [[P, NT]], base=B * T, channel_multiplier=1))
            link(nc.gpsimd.tensor_copy(x_ext[:, :, C], number[:]))
            nc.gpsimd.memset(k_stack[STACK:STACK + 3, 0:BLOCKS // 2 * BLOCK_COLS], 1.0).then_inc(s_ones, 1)
            pool.wait_ge(s_ones, 1)
            pool.wait_ge(t_ready, 8)
            pool.wait_ge(ld_bias, 6 * 16)
            for t in range(NT):
                nc.gpsimd.tensor_tensor(x_sb[:, t, :], x_sb[:, t, :], bias_row[:, 1, :], ALU.add).then_inc(x_biased, 1)

            def shifts(q, u, rounds, mt_done=None):
                pool.wait_ge(sm_free, mt_done)
                base = own[0]
                m, a, r = stat[:, q], mparts[:, q], mres[:, q]
                nc.gpsimd.tensor_tensor(a[:, 0], m, minus_one[:], ALU.mult).then_inc(pool_own, 1)
                pool.wait_ge(pool_own, rounds + 1)
                nc.gpsimd.tensor_tensor(r, m, a[:, 0], ALU.add).then_inc(pool_own, 1)
                pool.wait_ge(pool_own, rounds + 2)
                nc.gpsimd.tensor_tensor(a[:, 1], r, minus_one[:], ALU.mult).then_inc(pool_own, 1)
                pool.wait_ge(pool_own, rounds + 3)
                nc.gpsimd.tensor_tensor(r, r, a[:, 1], ALU.add).then_inc(pool_own, 1)
                pool.wait_ge(pool_own, rounds + 4)
                nc.gpsimd.tensor_tensor(a[:, 2], r, minus_one[:], ALU.mult).then_inc(parts_done, 1)

            start = own[0]
            shifts(0, 0, start, mt_done=G * QT)
            shifts(1, 1, start + 4, mt_done=SM_FIRST)
            for s in range(4):
                pool.wait_ge(part_stored[s], 64)
            pool.wait_ge(parts_done, 2)
            nc.gpsimd.memset(k_stack[STACK:STACK + 3, BLOCKS // 2 * BLOCK_COLS:BLOCKS * BLOCK_COLS], 1.0).then_inc(more_ones, 1)
            pool.wait_ge(more_ones, 1)

            def block_shifts(n):
                for q in range(2):
                    u = n * 2 + q
                    shifts(q, u + 2, n * 8 + (start + 8 + 4 * q),
                           mt_done=sm_index(u, max_pos(G * QT - 1)) + 1)

            block_shifts(0)
            with pool.Fori(1, BLOCKS - 1) as n:
                block_shifts(n)
            own[0] = start + 8 + 8 * (BLOCKS - 1)

            pool.wait_ge(ld_ctx, 16 * (B + 3))
            pool.wait_ge(pv_done, 8 * (UNITS - 2))
            nc.gpsimd.tensor_scalar(mask_sb[:, :, :], mask_sb[:, :, :], -MASK_WEIGHT, None, ALU.mult).then_inc(mask_scaled, 1)
            nc.gpsimd.memset(v2[:, :, :, DH:32], 1.0).then_inc(v2_ones, 1)
            for t in range(NT):
                pool.wait_ge(xt_ready, t + 1)
                nc.gpsimd.tensor_tensor(x_sb[:, t, :], x_sb[:, t, :], bias2_row[:, 1, :], ALU.add).then_inc(x_biased, 1)
            for j in range(2 * NT):
                pool.wait_ge(mx_done, j + 1)
                nc.gpsimd.tensor_tensor(sc[:, j % 4], sc[:, j % 4],
                                        mx2[:, j % 4, :].unsqueeze(2).broadcast_to([P, HB, S2]), ALU.subtract).then_inc(sub_done, 1)

            pool.wait_ge(y2_done, 4 * NG)
            link(nc.gpsimd.iota(upto_i, [[1, 48]], base=0, channel_multiplier=0))
            nc.gpsimd.tensor_copy(upto, upto_i).then_inc(s_upto, 1)
            link(nc.gpsimd.memset(ones, 1.0))
            nc.gpsimd.affine_select(out=earlier, in_=ones, compare_op=ALU.is_ge, fill=0.0, base=-1,
                                    pattern=[[1, P]], channel_multiplier=-1).then_inc(s_tri, 1)
            link(nc.gpsimd.memset(fill, 0.0))
            link(nc.gpsimd.iota(fill_id, [[P, E]], base=2 * B * T, channel_multiplier=1))
            link(nc.gpsimd.tensor_copy(fill[:, :, C], fill_id))
            nc.gpsimd.memset(fill[:, :, C + 1], -1.0).then_inc(s_fill, 1)
            for g, (t0, t1) in enumerate(GROUPS):
                pool.wait_ge(placed, g + 1)
                for t in range(t0, t1):
                    for k in range(2):
                        pool.indirect_dma_start(out=x_sorted[:, :],
                                                out_offset=bass.IndirectOffsetOnAxis(ap=places[:, k, t:t + 1], axis=0),
                                                in_=x_ext[:, t, :], in_offset=None).then_inc(scattered, 16)

            def store_results(i, s):
                pool.wait_ge(y_biased, i + 1)
                if not (isinstance(i, int) and i == 0):
                    pool.wait_ge(ys_stored[1 - s], (i + s) * 8)
                if not (isinstance(i, int) and i == 0):
                    pool.wait_ge(store_turn, i)
                nc.gpsimd.tensor_tensor(waited[:, s:s + 1], minus_one[:, 0:1], minus_one[:, 0:1], ALU.add).then_inc(store_turn, 1)
                pool.indirect_dma_start(out=y_token[:, :], out_offset=bass.IndirectOffsetOnAxis(ap=dest[:, s:s + 1], axis=0),
                                        in_=y_out[:, s], in_offset=None).then_inc(ys_stored[s], 16)

            store_results(0, 0)
            with pool.Fori(0, (SLOT_TILES - 1) // 2) as m:
                store_results(m * 2 + 1, 1)
                store_results(m * 2 + 2, 0)

            for t in range(NT):
                pool.wait_ge(scaled, t + 1)
                nc.gpsimd.tensor_tensor(x_sb[:, t, :], x_sb[:, t, :], gathered[:, t, 0], ALU.add).then_inc(first_added, 1)

        @block.scalar
        def _(act):
            act.wait_ge(ld_w, 16 * 4)
            nc.scalar.activation(w_bin[:, :, :, :], w_raw[:, 0:4], ACT.Sign).then_inc(s_sign, 1)
            act.wait_ge(ld_bias, 6 * 16)
            for k in range(16):
                act.wait_ge(t_ready, k + 1)
                if k < 8:
                    a, g = k // 4, k % 4
                    dst = xt[:, a, 512 * g:512 * (g + 1)]
                    src = psum[:, k % 4, :]
                else:
                    m = k - 8
                    dst = wt[:, m]
                    src = psum[:, k % 4, :].rearrange("p (a o) -> p a o", a=CT)
                nc.scalar.copy(dst, src).then_inc(t_evac, 1)

            def mid(j):
                act.wait_ge(r_done, j + 1)
                nc.scalar.copy(split(j)[:, 1], resid[:, j % 2]).then_inc(mid_done, 1)

            for j in range(16):
                m, a = j // 4 % 2, j // 2 % 2
                if j == 8:
                    mid(7)
                act.wait_ge(qk_ready, j + 1)
                if j >= 14:
                    act.wait_ge(part_stored[(j - 14) % 4], 32)
                nc.scalar.activation(split(j)[:, 0], psum[:, 4 + j % 4, :], ACT.Identity,
                                     bias=bias_col[:, m, a:a + 1]).then_inc(hi_done, 1)
                if j >= 1 and j != 8:
                    mid(j - 1)
            mid(15)
            def copy_o(u):
                act.wait_ge(pv_done, u * 8 + 8)
                nc.scalar.copy(o_sb[:], psum[:, O_BANK, :]).then_inc(o_copied, 1)

            def exps(n, q, first=False, last=False):
                u = n * 2 + q
                for kt in range(TB):
                    for h in range(G):
                        i = kt * G + h
                        act.wait_ge(st_ready, u * 32 + (i + 1))
                        if h == 0 and not (first and kt < 2):
                            act.wait_ge(pv_done, u * 8 + (kt - 1))
                        nc.scalar.activation(probs[:, kt % 2 * G + h, :], psum[:, st_bank(i, q if last else None), :], ACT.Exp,
                                             scale=SCALE).then_inc(exp_done, 1)
                    if kt == 0 and not first:
                        if not (isinstance(n, int) and n == 0):
                            act.wait_ge(turned, u - 1)
                        copy_o(u - 1)

            exps(0, 0, first=True)
            exps(0, 1)
            with act.Fori(1, BLOCKS - 1) as n:
                exps(n, 0)
                exps(n, 1)
            exps(BLOCKS - 1, 0, last=True)
            exps(BLOCKS - 1, 1, last=True)
            act.wait_ge(turned, UNITS - 1)
            copy_o(UNITS - 1)

            def norm_sqrt(k):
                act.wait_ge(stats_done, k + 1)
                s = k % NS
                nc.scalar.activation(std[:, s:s + 1], mv[:, s, 1:2], ACT.Sqrt, bias=EPS).then_inc(sqrt_done, 1)

            def norm_apply(t, k):
                act.wait_ge(rstd_ready, k + 1)
                s = k % NS
                nc.scalar.activation(x_sb[:, t, :], x_sb[:, t, :], ACT.Identity, bias=shift[:, s:s + 1],
                                     scale=std[:, s:s + 1]).then_inc(ln_done, 1)

            def query_copy(j):
                ch, a = j // 2, j % 2
                act.wait_ge(q2_ready, j + 1)
                nc.scalar.activation(q2t[:, a, 512 * ch:512 * (ch + 1)], psum[:, 6 + a, :], ACT.Identity,
                                     bias=bias_col[:, 2, a:a + 1]).then_inc(q2_evac, 1)

            def proj_copies(stage):
                base = stage * NT
                for t in range(NT + (7 if stage else 11)):
                    if t < NT:
                        act.wait_ge(yt_ready, base + t + 1)
                        if base + t >= 2:
                            act.wait_ge(pj_ready, base + t - 1)
                        nc.scalar.copy(yt[:, t % 2], psum[:, t % 2, 0:C].rearrange("p (a q) -> p a q", a=CT)).then_inc(yt_evac, 1)
                    if stage == 0 and t >= 12 and t % 2 == 0:
                        query_copy((t - 12) // 2)
                    if 7 <= t < NT + 7:
                        act.wait_ge(xt_ready, base + t - 6)
                        nc.scalar.copy(xt[:, :, (t - 7) * P:(t - 6) * P],
                                       psum[:, 4 + (t - 7) % 2, 0:C].rearrange("p (a q) -> p a q", a=CT)).then_inc(xt_evac, 1)
                    if 2 <= t < NT + 2:
                        norm_sqrt(base + t - 2)
                    if 4 <= t < NT + 4:
                        norm_apply(t - 4, base + t - 4)

            proj_copies(0)

            def cross_exp(j):
                act.wait_ge(sub_done, j + 1)
                nc.scalar.activation(sc[:, j % 4], sc[:, j % 4], ACT.Exp).then_inc(exp2_done, 1)

            def pt_copies(j):
                c, tq, a = j // 8, j % 8 // 2, j % 2
                for s in range(2):
                    act.wait_ge(ptr_ready, 2 * j + s + 1)
                    if tq == 0 and a == 0 and c >= 1:
                        act.wait_ge(pv2_ready, 4 * c)
                    nc.scalar.copy(pt[0:S2, a * HB + 4 * s:a * HB + 4 * s + 4, tq * P:(tq + 1) * P],
                                   psum[0:S2, 4 + s, :].rearrange("k (h q) -> k h q", h=4)).then_inc(ptr_evac, 1)

            def cross_out(c):
                for g in range(NG):
                    k = NG * c + g
                    act.wait_ge(pv2_ready, k + 1)
                    if k >= 2:
                        act.wait_ge(ot_ready, k - 1)
                    nc.scalar.copy(o2_sb[:, g % 2], psum[:, 6 + g % 2, :]).then_inc(o2_copied, 1)

            for j in range(2 * NT + LAG - 1):
                if j >= LAG - 1:
                    pt_copies(j - LAG + 1)
                if j < 2 * NT:
                    cross_exp(j)
                if j >= LAG - 1:
                    if (j - LAG + 1) % 8 == 7:
                        cross_out((j - LAG + 1) // 8)

            proj_copies(1)

            act.wait_ge(lg_sub, 1)
            nc.scalar.activation(prob, prob, ACT.Exp).then_inc(lg_exp, 1)

            def xst_copy(i, s):
                act.wait_ge(xs_t, i + 1)
                if not (isinstance(i, int) and i < 2):
                    act.wait_ge(up_ready, i - 1)
                nc.scalar.copy(xst[:, s], psum[:, 6 + s, 0:C].rearrange("p (a q) -> p a q", a=CT)).then_inc(xst_evac, 1)

            def relu(i, s):
                act.wait_ge(hid_done, i + 1)
                if not (isinstance(i, int) and i < 2):
                    act.wait_ge(down_ready, i - 1)
                nc.scalar.activation(hid_t[:, s], hid[:, s], ACT.Relu).then_inc(relu_done, 1)

            xst_copy(0, 0)
            xst_copy(1, 1)
            relu(0, 0)
            xst_copy(2, 0)
            relu(1, 1)
            xst_copy(3, 1)
            relu(2, 0)
            with act.Fori(1, (SLOT_TILES - 3) // 2) as m:
                xst_copy(m * 2 + 2, 0)
                relu(m * 2 + 1, 1)
                xst_copy(m * 2 + 3, 1)
                relu(m * 2 + 2, 0)
            xst_copy(SLOT_TILES - 1, (SLOT_TILES - 1) % 2)
            relu(SLOT_TILES - 2, SLOT_TILES % 2)
            relu(SLOT_TILES - 1, (SLOT_TILES - 1) % 2)
            for t in range(NT + 4):
                if t < NT:
                    for g, (t0, _) in enumerate(RESULT_LOADS):
                        if t == t0:
                            act.wait_ge(got[g], 32)
                    nc.scalar.activation(gathered[:, t, 0], gathered[:, t, 0], ACT.Identity, scale=share1[:, t:t + 1]).then_inc(scaled, 1)
                if 2 <= t < NT + 2:
                    norm_sqrt(2 * NT + t - 2)
                if t >= 4:
                    norm_apply(t - 4, 2 * NT + t - 4)

        @block.vector
        def _(dve):
            own = [0]

            def link(ins):
                own[0] += 1
                ins.then_inc(dve_own, 1)
                dve.wait_ge(dve_own, own[0])

            dve.wait_ge(ld_w, 16 * 4)
            link(nc.vector.tensor_reduce(alpha[:], w_raw[:, 0:4].rearrange("p m a c -> p (m a) c"), AX, ALU.add,
                                         apply_absolute_value=True))
            link(nc.vector.tensor_scalar(alpha[:], alpha[:], 1.0 / C, None, ALU.mult))
            dve.wait_ge(s_sign, 1)
            link(nc.vector.tensor_tensor(w_bin[:, :, :, :], w_bin[:, :, :, :], w_raw[:, 0:4], ALU.subtract))
            link(nc.vector.tensor_tensor(w_bin[:, :, :, :], w_bin[:, :, :, :], w_raw[:, 0:4], ALU.add))
            nc.vector.tensor_tensor(v_flat.rearrange("p (m c) -> p m c", c=C), v_flat.rearrange("p (m c) -> p m c", c=C),
                                    alpha[:].unsqueeze(2).broadcast_to([P, 8, C]), ALU.mult).then_inc(s_bin, 1)
            dve.wait_ge(ld_bias, 6 * 16)

            def lo(j):
                dve.wait_ge(mid_done, j + 1)
                nc.vector.tensor_tensor(split(j)[:, 2], resid[:, j % 2], split(j)[:, 1], ALU.subtract).then_inc(lo_done, 1)

            def v_out(j):
                dve.wait_ge(vp_ready, j + 1)
                nc.vector.tensor_tensor(
                    v_stage[:, j, :, :, 0:DH], psum[:, j % 4, :].rearrange("p (k h d) -> p k h d", k=2, h=H),
                    bias_row[:, 0, :].rearrange("p (h d) -> p h d", h=H).unsqueeze(1).broadcast_to([P, 2, H, DH]),
                    ALU.add).then_inc(v_evac, 1)

            def residue(j):
                m, a = j // 4 % 2, j // 2 % 2
                dve.wait_ge(hi_done, j + 1)
                if j >= 2:
                    dve.wait_ge(lo_done, j - 1)
                nc.vector.scalar_tensor_tensor(out=resid[:, j % 2], in0=psum[:, 4 + j % 4, :], scalar=bias_col[:, m, a:a + 1],
                                               in1=split(j)[:, 0], op0=ALU.add, op1=ALU.subtract).then_inc(r_done, 1)

            for j in range(8):
                residue(j)
                if j >= 1:
                    lo(j - 1)
            lo(7)
            for j in range(8):
                v_out(j)

            def row_max(q, i, k, slot, parts, last=None):
                dve.wait_ge(sm_ready, k + 1)
                if parts is not None:
                    dve.wait_ge(parts_done, parts)
                nc.vector.reduce_max(stat[:, q, i:i + 1], sm_tile(slot), AX).then_inc(sm_free, 1)

            def shift_row(q, k, slot):
                dve.wait_ge(sm_ready, k + 1)
                rows = psum[0:3 * G * QT, 2 * slot, :].bitcast(BF16)[:, 0:P]
                nc.vector.tensor_copy(m_rows[0:3 * G * QT, q], rows).then_inc(sm_free, 1)

            def normalise(n, q, u, bank, own_value):
                dve.wait_ge(turned, u + 1)
                o = psum[:, bank, :].rearrange("p (t h d) -> p t h d", t=QT, h=G)
                nc.vector.reciprocal(rsum[:], o[:, :, :, DH]).then_inc(dve_own, 1)
                dve.wait_ge(dve_own, own_value + 1)
                dst = y[:, q * QT:(q + 1) * QT, bass.ds(n, 1), :]
                nc.vector.tensor_tensor(dst.rearrange("p t n (h d) -> p t (n h) d", h=G), o[:, :, :, 0:DH],
                                        rsum[:].unsqueeze(3).broadcast_to([P, QT, G, DH]), ALU.mult).then_inc(normed, 1)

            for j in range(8, 16):
                i = 2 * (j - 8)
                residue(j)
                row_max(0, i, i, 0, None)
                if j > 8:
                    lo(j - 1)
                row_max(0, i + 1, i + 1, 1, None)
            lo(15)
            for i in range(G * QT):
                if i == AHEAD:
                    shift_row(0, FIRST_MT, FIRST_MT % 2)
                k = G * QT + i + (1 if i >= AHEAD else 0)
                row_max(1, i, k, k % 2, None)
            start = own[0]

            def unit_dve(n, q, first=False):
                u = n * 2 + q
                for kt in range(TB):
                    if kt == 2:
                        if not first:
                            if not (isinstance(n, int) and n == 0):
                                dve.wait_ge(normed, u - 1)
                            normalise(n if q else n - 1, 1 - q, u - 1, ot_bank(), u + (start - 1))
                            dve.wait_ge(rows_stored, u * 16)
                        shift_row(1 - q, sm_index(u, MT_POS), sm_slot(q, MT_POS))
                    for i in (2 * kt, 2 * kt + 1):
                        row_max(q, i, sm_index(u, max_pos(i)), sm_slot(q, max_pos(i)), u + 1)

            unit_dve(0, 0, first=True)
            unit_dve(0, 1)
            with dve.Fori(1, BLOCKS - 1) as n:
                unit_dve(n, 0)
                unit_dve(n, 1)
            dve.wait_ge(normed, UNITS - 3)
            normalise(BLOCKS - 2, 1, UNITS - 3, ot_bank(0), start + UNITS - 3)
            dve.wait_ge(rows_stored, 16 * (UNITS - 2))
            shift_row(1, sm_index(UNITS - 2, 0), sm_slot(0, 0))
            dve.wait_ge(normed, UNITS - 2)
            normalise(BLOCKS - 1, 0, UNITS - 2, ot_bank(1), start + UNITS - 2)
            dve.wait_ge(ld_ctx, 16 * (B + 3))
            dve.wait_ge(c_ready, 1)
            nc.vector.tensor_copy(ctx_t[:, :, :, :], psum[:, 2, 0:CT * B * S2].rearrange("p (a b k) -> p a b k", a=CT, b=B)).then_inc(c_evac, 1)
            for a in range(CT):
                dve.wait_ge(c_ready, 2 + a)
                nc.vector.tensor_scalar(k2t[:, a], psum[:, 3 - a, 0:B * S2].rearrange("p (b k) -> p b k", b=B),
                                        bias_col[:, 3, a:a + 1], None, ALU.add).then_inc(c_evac, 1)
            dve.wait_ge(c_evac, 1 + CT)
            dve.wait_ge(s_hm, 1)
            for b in range(B):
                for a in range(CT):
                    nc.vector.tensor_tensor(k2bd[:, b, a].rearrange("p (h k) -> p h k", h=HB),
                                            k2t[:, a, b].unsqueeze(1).broadcast_to([P, HB, S2]),
                                            head_mask[:].unsqueeze(2).broadcast_to([P, HB, S2]), ALU.mult).then_inc(kv_done, 1)
            for b in range(B):
                dve.wait_ge(c_ready, 2 + CT + b)
                nc.vector.tensor_tensor(v2[0:S2, b, :, 0:DH], psum[0:S2, 3 - b, 0:C].rearrange("p (h d) -> p h d", h=H),
                                        bias2_row[0:S2, 0, :].rearrange("p (h d) -> p h d", h=H), ALU.add).then_inc(kv_done, 1)

            dve.wait_ge(normed, UNITS - 1)
            normalise(BLOCKS - 1, 1, UNITS - 1, last_bank(2 * ENTRIES), start + UNITS - 1)
            own[0] = start + UNITS

            def norms(stage, last_step, add, also=None):
                base = stage * NT
                for t in range(last_step + 1):
                    if 1 <= t <= NT:
                        k = base + t - 1
                        dve.wait_ge(added, k + 1)
                        if k >= NS:
                            dve.wait_ge(ln_done, k - NS + 1)
                        nc.vector.bn_stats(bn[:, k % NS], x_sb[:, t - 1, :]).then_inc(bn_done, 1)
                    if 3 <= t < NT + 3:
                        k = base + t - 3
                        s = k % NS
                        dve.wait_ge(sqrt_done, k + 1)
                        nc.vector.reciprocal(std[:, s:s + 1], std[:, s:s + 1]).then_inc(recip_done, 1)
                    if t < NT:
                        add(t, base + t)
                    if 1 <= t <= NT:
                        k = base + t - 1
                        dve.wait_ge(bn_done, k + 1)
                        nc.vector.bn_aggr(mv[:, k % NS], bn[:, k % NS]).then_inc(stats_done, 1)
                    if 3 <= t < NT + 3:
                        k = base + t - 3
                        s = k % NS
                        dve.wait_ge(recip_done, k + 1)
                        nc.vector.scalar_tensor_tensor(out=shift[:, s:s + 1], in0=mv[:, s, 0:1], scalar=-1.0,
                                                       in1=std[:, s:s + 1], op0=ALU.mult, op1=ALU.mult).then_inc(rstd_ready, 1)
                    if also is not None:
                        also(t)

            def add_projected(t, k):
                dve.wait_ge(pj_ready, k + 1)
                dve.wait_ge(x_biased, k + 1)
                nc.vector.tensor_tensor(x_sb[:, t, :], x_sb[:, t, :], psum[:, 2 + t % 2, 0:C], ALU.add).then_inc(added, 1)

            norms(0, NT + 2, add_projected)

            dve.wait_ge(mask_scaled, 1)

            def cross_scores(j):
                t = j // 2
                dve.wait_ge(s2_ready, j + 1)
                if j >= 4:
                    dve.wait_ge(ptr_ready, 2 * (j - 3))
                nc.vector.tensor_tensor(
                    out=sc[:, j % 4].rearrange("p (b h) k -> p b h k", b=2),
                    in0=psum[:, 2 * (j % 2):2 * (j % 2) + 2, 0:HB // 2 * S2].rearrange("p b (h k) -> p b h k", k=S2),
                    in1=mask_sb[:, t, :].unsqueeze(1).unsqueeze(1).broadcast_to([P, 2, HB // 2, S2]),
                    op=ALU.add).then_inc(sc_done, 1)
                dve.wait_ge(sc_done, j + 1)
                nc.vector.reduce_max(mx2[:, j % 4, :], sc[:, j % 4], AX).then_inc(mx_done, 1)

            def cross_norm(c):
                for g in range(NG):
                    k = NG * c + g
                    dve.wait_ge(ot_ready, k + 1)
                    if k >= 1:
                        dve.wait_ge(y2_done, k)
                    o = psum[:, 4 + g % 2, :].rearrange("p (t h d) -> p t h d", t=QT, h=G)
                    link(nc.vector.reciprocal(rsum[:], o[:, :, :, DH]))
                    b, half = c // 2, c % 2
                    nc.vector.tensor_tensor(y[:, half * QT:(half + 1) * QT, b * NG + g, :].rearrange("p t (h d) -> p t h d", h=G),
                                            o[:, :, :, 0:DH], rsum[:].unsqueeze(3).broadcast_to([P, QT, G, DH]), ALU.mult).then_inc(y2_done, 1)

            for j in range(2 * NT + LAG):
                if j < 2 * NT:
                    cross_scores(j)
                if j >= LAG and (j - LAG) % 8 == 7:
                    cross_norm((j - LAG) // 8)

            number_of = e_rows[:, 0].unsqueeze(1)

            def bc(v, n=E):
                return v.unsqueeze(2).broadcast_to([P, v.shape[1], n])

            def choose(g):
                t0, t1 = GROUPS[g]
                ts, n = slice(t0, t1), t1 - t0
                if g == 0:
                    dve.wait_ge(s_upto, 1)
                    link(nc.vector.tensor_scalar(e_rows[:, 0], upto[:, 0:E], -1.0, float(E), ALU.mult, ALU.add))
                    link(nc.vector.tensor_scalar(upto_row[:, 0], upto[:, 0:E], float(ROOM), None, ALU.mult))
                dve.wait_ge(lg_ready, t1)
                link(nc.vector.tensor_copy(logits[:, ts], psum[:, 6 + g % 2, 0:n * E].rearrange("p (t e) -> p t e", e=E)))
                for values_, one, top in ((logits, first, best), (others, second, row_b)):
                    link(nc.vector.reduce_max(top[:, ts], values_[:, ts], AX))
                    link(nc.vector.tensor_tensor(one[:, ts], values_[:, ts], bc(top[:, ts]), ALU.is_equal))
                    link(nc.vector.tensor_tensor(one[:, ts], one[:, ts], number_of.broadcast_to([P, n, E]), ALU.mult))
                    link(nc.vector.reduce_max(row_a[:, ts], one[:, ts], AX))
                    link(nc.vector.tensor_tensor(one[:, ts], one[:, ts], bc(row_a[:, ts]), ALU.is_equal))
                    if one is first:
                        link(nc.vector.tensor_scalar(x_ext[:, ts, C + 1], row_a[:, ts], -1.0, float(E), ALU.mult, ALU.add))
                        link(nc.vector.scalar_tensor_tensor(out=others[:, ts], in0=one[:, ts], scalar=-3e38, in1=values_[:, ts],
                                                            op0=ALU.mult, op1=ALU.add))
                nc.vector.tensor_tensor(chosen[:, ts], first[:, ts], second[:, ts], ALU.add).then_inc(mask_ready, 1)

            def place(g):
                t0, t1 = GROUPS[g]
                ts, n = slice(t0, t1), t1 - t0
                dve.wait_ge(ranks_ready, g + 1)
                for t in range(t0, t1):
                    link(nc.vector.tensor_tensor(upto_row[:, t + 1], upto_row[:, t],
                                                 psum[:, 6 + g % 2, (16 + t - t0) * E:(17 + t - t0) * E], ALU.add))
                link(nc.vector.tensor_tensor(before[:, ts], upto_row[:, ts],
                                             psum[:, 6 + g % 2, 8 * E:(8 + n) * E].rearrange("p (t e) -> p t e", e=E), ALU.add))
                for one, where in ((first, place1), (second, place2)):
                    link(nc.vector.tensor_tensor(weigh[:, ts], one[:, ts], before[:, ts], ALU.mult))
                    link(nc.vector.reduce_sum(where[:, ts], weigh[:, ts], AX))
                nc.vector.tensor_copy(places[:, :, ts], rows[:, 5:7, ts]).then_inc(placed, 1)

            def router(t):
                for g, (_, t1) in enumerate(GROUPS):
                    if t == t1 + 7:
                        choose(g)
                    if t == rank_step(g):
                        place(g)

            norms(1, NT + 9, add_projected, router)

            nc.vector.tensor_copy(fill_row, upto_row[:, NT]).then_inc(fill_known, 1)
            nc.vector.tensor_tensor(prob, logits, bc(best), ALU.subtract).then_inc(lg_sub, 1)
            total, tiles, ends, other = (e_rows[:, i] for i in range(4))
            link(nc.vector.tensor_tensor(total, upto_row[:, NT], upto_row[:, 0], ALU.subtract))
            link(nc.vector.tensor_scalar(total, total, 1.0 / P, None, ALU.mult))
            begun = many[:, :, 0:NT]
            link(nc.vector.tensor_tensor(begun, bc(total, NT), upto[:, 0:NT].unsqueeze(1).broadcast_to([P, E, NT]), ALU.is_gt))
            link(nc.vector.reduce_sum(tiles, begun, AX))
            a, z = tiles, ends
            step = 1
            while step < E:
                link(nc.vector.tensor_copy(z[:, 0:step], a[:, 0:step]))
                link(nc.vector.tensor_tensor(z[:, step:], a[:, step:], a[:, 0:E - step], ALU.add))
                a, z = z, (other if z is ends else ends)
                step *= 2
            link(nc.vector.tensor_scalar(row_c[:, 0:1], a[:, E - 1:E], -1.0, None, ALU.add))
            tile_no = real[:, 0:SLOT_TILES]
            link(nc.vector.tensor_tensor(tile_no, upto[:, 0:SLOT_TILES], row_c[:, 0:1].broadcast_to([P, SLOT_TILES]), ALU.min))
            of_tile = many.rearrange("p a b -> p (a b)")[:, 0:SLOT_TILES * (E - 1)].rearrange("p (i e) -> p i e", e=E - 1)
            link(nc.vector.tensor_tensor(of_tile, a[:, 0:E - 1].unsqueeze(1).broadcast_to([P, SLOT_TILES, E - 1]),
                                         bc(tile_no, E - 1), ALU.is_le))
            link(nc.vector.reduce_sum(tile_e[:, 0:SLOT_TILES], of_tile, AX))
            starts = z
            link(nc.vector.tensor_scalar(starts, tiles, -1.0, float(ROOM // P), ALU.mult, ALU.add))
            link(nc.vector.tensor_tensor(of_tile, of_tile, starts[:, 0:E - 1].unsqueeze(1).broadcast_to([P, SLOT_TILES, E - 1]), ALU.mult))
            link(nc.vector.reduce_sum(tile_row[:, 0:SLOT_TILES], of_tile, AX))
            link(nc.vector.tensor_tensor(tile_row[:, 0:SLOT_TILES], tile_row[:, 0:SLOT_TILES], tile_no, ALU.add))
            link(nc.vector.tensor_copy(tile_place[:, 0:SLOT_TILES], tile_row[:, 0:SLOT_TILES]))
            nc.vector.tensor_copy(tile_expert[:, 0:SLOT_TILES], tile_e[:, 0:SLOT_TILES]).then_inc(tiles_known, 1)
            dve.wait_ge(lg_exp, 1)
            link(nc.vector.reduce_sum(row_a, prob, AX))
            link(nc.vector.reciprocal(row_a, row_a))
            link(nc.vector.tensor_tensor(prob, prob, bc(row_a), ALU.mult))
            for one, top in ((first, top1), (second, top2)):
                link(nc.vector.tensor_tensor(weigh, one, prob, ALU.mult))
                link(nc.vector.reduce_sum(top, weigh, AX))
            link(nc.vector.tensor_tensor(row_a, top1, top2, ALU.add))
            link(nc.vector.reciprocal(row_a, row_a))
            link(nc.vector.tensor_tensor(share1, top1, row_a, ALU.mult))
            link(nc.vector.tensor_tensor(share2, top2, row_a, ALU.mult))

            def up_bias(i, s):
                e = dve.value_load(tile_expert[0:1, bass.ds(i, 1)], min_val=0, max_val=E - 1)
                dve.wait_ge(up_ready, i + 1)
                if not (isinstance(i, int) and i < 2):
                    dve.wait_ge(relu_done, i - 1)
                nc.vector.tensor_tensor(hid[:, s], psum[:, s, :].rearrange("p (a q) -> p a q", a=HT),
                                        b1_col[:, bass.ds(e, 1), :].rearrange("p o a -> p (o a)").unsqueeze(2).broadcast_to([P, HT, P]),
                                        ALU.add).then_inc(hid_done, 1)

            def take_w1(i, s):
                e = dve.value_load(tile_expert[0:1, bass.ds(i, 1)], min_val=0, max_val=E - 1)
                if not (isinstance(i, int) and i < 2):
                    dve.wait_ge(up_ready, i - 1)
                nc.vector.tensor_copy(w1_now[:, s], w1_sb[:, bass.ds(e, 1)].rearrange("p o a h -> p (o a) h")).then_inc(w1_taken, 1)

            def note(i, s):
                dve.wait_ge(xs_loaded[s], (i - s) * 8 + 16)
                if not (isinstance(i, int) and i < 2):
                    dve.wait_ge(dest_done, i - 1)
                nc.vector.tensor_tensor(of_two[:, s:s + 1], xs_in[:, s, C + 1:C + 2], tile_e[:, bass.ds(i, 1)], ALU.is_equal).then_inc(compared, 1)
                dve.wait_ge(compared, i + 1)
                nc.vector.scalar_tensor_tensor(out=noted[:, s:s + 1], in0=of_two[:, s:s + 1], scalar=-float(B * T),
                                               in1=xs_in[:, s, C:C + 1], op0=ALU.mult, op1=ALU.add).then_inc(dest_noted, 1)

            def down_bias(i, s):
                e = dve.value_load(tile_expert[0:1, bass.ds(i, 1)], min_val=0, max_val=E - 1)
                dve.wait_ge(down_ready, i + 1)
                if not (isinstance(i, int) and i < 2):
                    dve.wait_ge(ys_stored[s], ys_turn(i, s))
                dve.wait_ge(dest_noted, i + 1)
                nc.vector.tensor_copy(dest[:, s:s + 1], noted[:, s:s + 1]).then_inc(dest_done, 1)
                nc.vector.tensor_tensor(y_out[:, s], psum[:, 4 + s, 0:C], b2_rows[:, bass.ds(e * C, C)], ALU.add).then_inc(y_biased, 1)

            def ys_turn(i, s):
                return (i - s) * 8

            dve.wait_ge(tiles_known, 1)
            dve.wait_ge(ld_w2, 16 * (2 + E))
            dve.wait_ge(ld_w1, 16 * E)
            take_w1(0, 0)
            take_w1(1, 1)
            def expert_biases(i, s, more=2):
                up_bias(i, s)
                if more >= 2:
                    take_w1(i + 2, s)
                down_bias(i - 1, 1 - s)
                if more >= 1:
                    note(i + 1, 1 - s)

            dve.wait_ge(b1_turned, 1)
            nc.vector.tensor_copy(b1_col, psum[:, 0, 0:E * HT].rearrange("p (e a) -> p e a", e=E)).then_inc(b1_there, 1)
            dve.wait_ge(b1_there, 1)
            note(0, 0)
            up_bias(0, 0)
            take_w1(2, 0)
            note(1, 1)
            expert_biases(1, 1)
            expert_biases(2, 0)
            with dve.Fori(1, (SLOT_TILES - 3) // 2) as m:
                expert_biases(m * 2 + 1, 1)
                expert_biases(m * 2 + 2, 0)
            expert_biases(SLOT_TILES - 2, 1, more=1)
            expert_biases(SLOT_TILES - 1, 0, more=0)
            down_bias(SLOT_TILES - 1, 0)

            def add_second(t, k):
                dve.wait_ge(first_added, t + 1)
                nc.vector.scalar_tensor_tensor(out=x_sb[:, t, :], in0=gathered[:, t, 1], scalar=share2[:, t:t + 1],
                                               in1=x_sb[:, t, :], op0=ALU.mult, op1=ALU.add).then_inc(added, 1)

            norms(2, NT + 2, add_second)

        @block.tensor
        def _(pe):
            pe.wait_ge(s_ident, 1)
            pe.wait_ge(s_identb, 1)
            for k in range(16):
                if k >= 4:
                    pe.wait_ge(t_evac, k - 3)
                if k < 8:
                    a, g = k // 4, k % 4
                    if a == 0:
                        pe.wait_ge(ld_x[g], 16)
                    for i in range(4):
                        mm = pe.transpose(psum[:, k % 4, i * P:(i + 1) * P], x_sb[:, 4 * g + i, a * P:(a + 1) * P], ident[:])
                else:
                    m = k - 8
                    if m == 0:
                        pe.wait_ge(s_bin, 1)
                    elif m == 4:
                        pe.wait_ge(ld_cross_w, 16 * 4)
                    src = w_bin[:, m] if m < 4 else w_raw[:, m]
                    for a in range(CT):
                        for o in range(CT):
                            mm = pe.transpose(psum[:, k % 4, (a * CT + o) * P:(a * CT + o + 1) * P],
                                              src[:, o, a * P:(a + 1) * P], ident[:])
                mm.then_inc(t_ready, 1)
            pe.wait_ge(t_evac, 16)
            def project_qk(j):
                b, m, o, ch = j // 8, j // 4 % 2, j // 2 % 2, j % 2
                if j >= 4:
                    pe.wait_ge(r_done, j - 3)
                t0 = b * T + ch * HALF
                for a in range(CT):
                    mm = pe.matmul(psum[:, 4 + j % 4, :], wt[:, m, a, o * P:(o + 1) * P], xt[:, a, t0:t0 + HALF],
                                   start=(a == 0), stop=(a == CT - 1))
                mm.then_inc(qk_ready, 1)

            for j in range(8):
                project_qk(j)
            for j in range(8):
                if j >= 4:
                    pe.wait_ge(v_evac, j - 3)
                for k in range(2):
                    t0 = (2 * j + k) * P
                    for a in range(CT):
                        mm = pe.matmul(psum[:, j % 4, k * C:(k + 1) * C], xt[:, a, t0:t0 + P], wt[:, 2, a, :],
                                       start=(a == 0), stop=(a == CT - 1))
                mm.then_inc(vp_ready, 1)

            def max_tile(n, i, k, slot, free):
                h, t = i // QT, i % QT
                if free is not None:
                    pe.wait_ge(sm_free, free)
                q = max_q[0]
                for c in range(T // 512):
                    mm = pe.matmul(psum[:, 2 * slot + c, :], stack_ap(q_stack, n, slice(0, STACK), h, q * HALF + t * P, P),
                                   stack_ap(k_stack, n, slice(0, STACK), h, c * 512, 512), start=True, stop=True)
                mm.then_inc(sm_ready, 1)

            max_q = [0]

            def shift_tile(q, k, slot, parts):
                pe.wait_ge(parts_done, parts)
                pe.wait_ge(sm_free, k - 1)
                dst = psum[:, 2 * slot, :].bitcast(BF16)[:, 0:P]
                pe.transpose(dst, mparts[:, q].rearrange("p j c -> p (j c)"), ident_b[:]).then_inc(sm_ready, 1)

            def out_tile(u, bank, free=None, entry=None):
                pe.wait_ge(o_copied, u + 1)
                if entry is None:
                    pe.wait_ge(exp_done, free)
                else:
                    wait_last(BLOCKS - 1, entry)
                for t in range(QT):
                    mm = pe.transpose(psum[:, bank, t * P:(t + 1) * P], o_sb[:, t * P:(t + 1) * P], ident[:])
                mm.then_inc(turned, 1)

            def wait_last(n, entry):
                back = entry - len(LAST_RING)
                if back < 0:
                    if entry < 3:
                        pe.wait_ge(exp_done, n * 2 * 32 + entry - 2)
                    else:
                        pe.wait_ge(sm_free, sm_index(n * 2, 0))
                    return
                q, e = divmod(back, ENTRIES)
                if e == OT_ENTRY:
                    pe.wait_ge(normed, n * 2 + q)
                else:
                    pe.wait_ge(exp_done, (n * 2 + q) * 32 + (e if e < OT_ENTRY else e - 1) + 1)

            def scores(n, q, kt, first, heads, last=False):
                u = n * 2 + q
                if kt == 0 and 0 in heads:
                    pe.wait_ge(rows_loaded[q], n * 16 + 16)
                for h in heads:
                    i = kt * G + h
                    if last:
                        wait_last(n, q * ENTRIES + (i if i < OT_ENTRY else i + 1))
                    elif i == OT_ENTRY + 2:
                        if not first:
                            pe.wait_ge(normed, u)
                    elif i >= 3 or not first:
                        back = i - 3 if i < OT_ENTRY or i > OT_ENTRY + 2 else i - 2
                        pe.wait_ge(exp_done, u * 32 + (back + 1))
                    pe.matmul(psum[:, st_bank(i, q if last else None), :], stack_ap(k_stack, n, slice(0, STACK + 3), h, kt * P, P),
                              stack_ap(q_stack, n, slice(0, STACK + 3), h, q * HALF, HALF), start=True, stop=True).then_inc(st_ready, 1)

            def values(n, q, kt, first):
                u = n * 2 + q
                pe.wait_ge(exp_done, u * 32 + (4 * kt + 4))
                if kt == 0:
                    pe.wait_ge(v_loaded[q], n * 16 + 16)
                    if not first:
                        pe.wait_ge(o_copied, u)
                for h in range(G):
                    mm = pe.matmul(psum[32 * h:32 * h + 32, O_BANK, :], v_ring[:, q, kt, 32 * h:32 * h + 32],
                                   probs[:, kt % 2 * G + h, :], start=(kt == 0), stop=(kt == TB - 1))
                mm.then_inc(pv_done, 1)

            pe.wait_ge(v_evac, 8)
            pe.wait_ge(stack_loaded, STACK_LOADS)
            for j in range(8, 16):
                project_qk(j)
                for i in (2 * (j - 8), 2 * (j - 8) + 1):
                    max_tile(0, i, i, i % 2, i - 1 if i >= 2 else None)
            max_q[0] = 1
            for i in range(G * QT):
                if i == AHEAD:
                    shift_tile(0, FIRST_MT, FIRST_MT % 2, 1)
                k = G * QT + i + (1 if i >= AHEAD else 0)
                max_tile(0, i, k, k % 2, k - 1)

            def context(step):
                if step == 0:
                    pe.wait_ge(sm_free, sm_index(UNITS - 2, 0) + 1)
                    pe.wait_ge(ld_ctx, 16 * (B + 3))
                    for a in range(CT):
                        for b in range(B):
                            mm = pe.transpose(psum[:, 2, (a * B + b) * S2:(a * B + b + 1) * S2], ctx_sb[0:S2, b, a * P:(a + 1) * P],
                                              ident[0:S2, 0:S2])
                elif step <= CT:
                    o = step - 1
                    pe.wait_ge(c_evac, 1)
                    for a in range(CT):
                        mm = pe.matmul(psum[:, 3 - o, 0:B * S2], wt[:, 5, a, o * P:(o + 1) * P],
                                       ctx_t[:, a].rearrange("p b k -> p (b k)"), start=(a == 0), stop=(a == CT - 1))
                else:
                    b = step - 1 - CT
                    pe.wait_ge(c_evac, 2 + b)
                    for a in range(CT):
                        mm = pe.matmul(psum[0:S2, 3 - b, 0:C], ctx_t[:, a, b, :], wt[:, 6, a, :], start=(a == 0), stop=(a == CT - 1))
                mm.then_inc(c_ready, 1)

            def unit_pe(n, q, first=False, maxima=True, rows=True, with_context=False):
                u = n * 2 + q
                max_q[0] = q

                def maxima_of(i):
                    if maxima:
                        k = sm_index(u, max_pos(i))
                        max_tile(n + 1, i, k, sm_slot(q, max_pos(i)), k - 1)

                if maxima and q == 0:
                    pe.wait_ge(stack_loaded, n * STACK_LOADS + 2 * STACK_LOADS)
                for kt in range(TB):
                    if kt == 2 and rows:
                        pos_ = MT_POS if maxima else 0
                        shift_tile(1 - q, sm_index(u, pos_), sm_slot(q, pos_), u + 2)
                    if with_context and 2 <= kt < 3 + CT + B:
                        context(kt - 2)
                    maxima_of(2 * kt)
                    scores(n, q, kt, first, (0, 1), last=not maxima)
                    maxima_of(2 * kt + 1)
                    scores(n, q, kt, first, (2,) if maxima else (2, 3), last=not maxima)
                    if not maxima and kt == 1:
                        out_tile(u - 1, ot_bank(q), entry=q * ENTRIES + OT_ENTRY)
                    if kt >= 1:
                        values(n, q, kt - 1, first)
                    elif not first:
                        values(n if q else n - 1, 1 - q, TB - 1, False)
                    if maxima:
                        scores(n, q, kt, first, (3,))
                    if maxima and kt == 1 and not first:
                        out_tile(u - 1, ot_bank(), u * 32 + (OT_ENTRY - 2))

            unit_pe(0, 0, first=True)
            unit_pe(0, 1)
            pe.wait_ge(more_ones, 1)
            with pe.Fori(1, BLOCKS - 1) as n:
                unit_pe(n, 0)
                unit_pe(n, 1)
            unit_pe(BLOCKS - 1, 0, maxima=False)
            unit_pe(BLOCKS - 1, 1, maxima=False, rows=False, with_context=True)
            values(BLOCKS - 1, 1, TB - 1, False)

            def cross_s(j):
                t, a = j // 2, j % 2
                if j == 0:
                    pe.wait_ge(added, NT)
                    pe.wait_ge(kv_done, B * CT + B)
                if j % 8 == 0:
                    pe.wait_ge(q2_evac, 2 * (j // 8) + 2)
                if j >= 2:
                    pe.wait_ge(sc_done, j - 1)
                n_ = HB // 2 * S2
                for s in range(2):
                    mm = pe.matmul(psum[:, 2 * (j % 2) + s, 0:n_], q2t[:, a, t * P:(t + 1) * P],
                                   k2bd[:, t // TB, a, s * n_:(s + 1) * n_], start=True, stop=True)
                mm.then_inc(s2_ready, 1)

            def project(stage):
                base, m = stage * NT, 3 + 4 * stage
                if stage == 0:
                    pe.wait_ge(sm_free, sm_index(UNITS - 2, 0) + 1)
                    pe.wait_ge(kv_done, B * CT + B)
                    pe.wait_ge(exp_done, 32 * UNITS)
                else:
                    pe.wait_ge(y2_done, 3 * NG)
                    pe.wait_ge(sc_done, 2 * NT)
                for t in range(NT + 10):
                    if t < NT:
                        k = base + t
                        b, tt = t // TB, t % TB
                        if k >= 2:
                            pe.wait_ge(yt_evac, k - 1)
                        for a in range(CT):
                            mm = pe.transpose(psum[:, t % 2, a * P:(a + 1) * P],
                                              y[:, tt, b * NG + 2 * a:b * NG + 2 * a + 2, :].rearrange("p n c -> p (n c)"), ident[:])
                        mm.then_inc(yt_ready, 1)
                    if stage == 0 and t == 0:
                        out_tile(UNITS - 1, last_bank(2 * ENTRIES), entry=2 * ENTRIES)
                    if t == 6:
                        if stage == 0:
                            pe.wait_ge(normed, UNITS)
                        else:
                            pe.wait_ge(y2_done, 4 * NG)
                    if 1 <= t <= NT:
                        k = base + t - 1
                        pe.wait_ge(yt_evac, k + 1)
                        if k >= 2:
                            pe.wait_ge(added, k - 1)
                        for a in range(CT):
                            mm = pe.matmul(psum[:, 2 + (t - 1) % 2, 0:C], yt[:, (t - 1) % 2, a, :], wt[:, m, a, :], start=(a == 0), stop=(a == CT - 1))
                        mm.then_inc(pj_ready, 1)
                    if 6 <= t < NT + 6:
                        k = base + t - 6
                        pe.wait_ge(ln_done, k + 1)
                        if k >= 2:
                            pe.wait_ge(xt_evac, k - 1)
                        for a in range(CT):
                            mm = pe.transpose(psum[:, 4 + t % 2, a * P:(a + 1) * P], x_sb[:, t - 6, a * P:(a + 1) * P], ident[:])
                        mm.then_inc(xt_ready, 1)
                    if stage == 0 and NT + 7 <= t < NT + 9:
                        cross_s(t - NT - 7)
                    if stage == 1:
                        router(t)
                    elif t >= 11 and t % 2 == 1:
                        queries((t - 11) // 2)

            def queries(j):
                ch, o = j // 2, j % 2
                pe.wait_ge(xt_evac, 4 * ch + 4)
                if j >= 2:
                    pe.wait_ge(q2_evac, j - 1)
                for a in range(CT):
                    mm = pe.matmul(psum[:, 6 + o, :], wt[:, 4, a, o * P:(o + 1) * P], xt[:, a, 512 * ch:512 * (ch + 1)],
                                   start=(a == 0), stop=(a == CT - 1))
                mm.then_inc(q2_ready, 1)

            def router(step):
                if 8 <= step < NT + 8:
                    t = step - 8
                    if t == 0:
                        pe.wait_ge(ld_wg, 16)
                    pe.wait_ge(xt_evac, NT + t + 1)
                    g, t0 = [(g, a) for g, (a, z) in enumerate(GROUPS) if a <= t < z][0]
                    if g >= 2 and t == t0:
                        pe.wait_ge(placed, g - 1)
                    for a in range(CT):
                        mm = pe.matmul(psum[:, 6 + g % 2, (t - t0) * E:(t - t0 + 1) * E], xt[:, a, t * P:(t + 1) * P], wg_sb[:, a, :], start=(a == 0), stop=(a == CT - 1))
                    mm.then_inc(lg_ready, 1)
                for g, (t0, t1) in enumerate(GROUPS):
                    if step == rank_step(g):
                        n = t1 - t0
                        pe.wait_ge(mask_ready, g + 1)
                        if g == 0:
                            pe.wait_ge(s_tri, 1)
                        of_group = chosen[:, t0:t1].rearrange("p t e -> p (t e)")
                        pe.matmul(psum[:, 6 + g % 2, 8 * E:(8 + n) * E], earlier, of_group, start=True, stop=True)
                        pe.matmul(psum[:, 6 + g % 2, 16 * E:(16 + n) * E], ones, of_group, start=True, stop=True).then_inc(ranks_ready, 1)

            project(0)

            pe.wait_ge(v2_ones, 1)

            def cross_t(j):
                c, a = j // 8, j % 2
                pe.wait_ge(exp2_done, j + 1)
                for s in range(2):
                    if j >= 1:
                        pe.wait_ge(ptr_evac, 2 * j + s - 1)
                    if j % 8 == 0 and c >= 1:
                        pe.wait_ge(y2_done, 4 * c)
                    for h in range(4):
                        mm = pe.transpose(psum[0:S2, 4 + s, h * P:(h + 1) * P], sc[:, j % 4, 4 * s + h, :], ident[:])
                    mm.then_inc(ptr_ready, 1)

            def cross_pv(c):
                b = c // 2
                pe.wait_ge(ptr_evac, 16 * (c + 1))
                for g in range(NG):
                    k = NG * c + g
                    if k >= 2:
                        pe.wait_ge(o2_copied, k - 1)
                    for h in range(G):
                        mm = pe.matmul(psum[32 * h:32 * h + 32, 6 + g % 2, :], v2[0:S2, b, G * g + h, :],
                                       pt[0:S2, G * g + h, :], start=True, stop=True)
                    mm.then_inc(pv2_ready, 1)
                    if g >= 1:
                        cross_o(k - 1)
                cross_o(NG * c + NG - 1)

            def cross_o(k):
                pe.wait_ge(o2_copied, k + 1)
                if k >= 2:
                    pe.wait_ge(y2_done, k - 1)
                for t in range(QT):
                    mm = pe.transpose(psum[:, 4 + k % 2, t * P:(t + 1) * P], o2_sb[:, k % 2, t * P:(t + 1) * P], ident[:])
                mm.then_inc(ot_ready, 1)

            for j in range(2 * NT + LAG):
                values_due = j >= LAG and (j - LAG) % 8 == 7
                if 2 <= j < 2 * NT and not (j >= LAG + 8 and (j - LAG) % 8 == 0):
                    cross_s(j)
                if j >= LAG:
                    cross_t(j - LAG)
                if values_due:
                    if j + 1 < 2 * NT:
                        cross_s(j + 1)
                    cross_pv((j - LAG) // 8)

            project(1)

            pe.wait_ge(tiles_known, 1)
            pe.wait_ge(lg_sub, 1)
            pe.wait_ge(ld_w2, 16 * (2 + E))
            pe.transpose(psum[:, 0, 0:E * HT], b1_in, ident[0:E * HT, 0:E * HT]).then_inc(b1_turned, 1)

            def tokens_in(i, s, loaded):
                pe.wait_ge(xs_loaded[s], loaded)
                if not (isinstance(i, int) and i < 2):
                    pe.wait_ge(xst_evac, i - 1)
                for a in range(CT):
                    mm = pe.transpose(psum[:, 6 + s, a * P:(a + 1) * P], xs_in[:, s, a * P:(a + 1) * P], ident[:])
                mm.then_inc(xs_t, 1)

            def up(i, s):
                pe.wait_ge(w1_taken, i + 1)
                pe.wait_ge(xst_evac, i + 1)
                if isinstance(i, int) and i == 0:
                    pe.wait_ge(b1_there, 1)
                elif not (isinstance(i, int) and i < 2):
                    pe.wait_ge(hid_done, i - 1)
                for h in range(HT):
                    for a in range(CT):
                        mm = pe.matmul(psum[:, s, h * P:(h + 1) * P], w1_now[:, s, a, h * P:(h + 1) * P], xst[:, s, a, :],
                                       start=(a == 0), stop=(a == CT - 1))
                mm.then_inc(up_ready, 1)

            def down(i, s):
                e = pe.value_load(tile_expert[0:1, bass.ds(i, 1)], min_val=0, max_val=E - 1)
                pe.wait_ge(relu_done, i + 1)
                if not (isinstance(i, int) and i < 2):
                    pe.wait_ge(y_biased, i - 1)
                for a in range(HT):
                    mm = pe.matmul(psum[:, 4 + s, 0:C], hid_t[:, s, a, :], w2_sb[:, bass.ds(e, 1), a, :],
                                   start=(a == 0), stop=(a == HT - 1))
                mm.then_inc(down_ready, 1)

            def expert_step(i, s, loaded):
                up(i, s)
                if loaded is not None:
                    tokens_in(i + 1, 1 - s, loaded)
                if not (isinstance(i, int) and i == 0):
                    down(i - 1, 1 - s)

            pe.wait_ge(ld_w2, 16 * (2 + E))
            tokens_in(0, 0, 16)
            expert_step(0, 0, 16)
            expert_step(1, 1, 32)
            expert_step(2, 0, 32)
            with pe.Fori(1, (SLOT_TILES - 3) // 2) as m:
                expert_step(m * 2 + 1, 1, m * 16 + 32)
                expert_step(m * 2 + 2, 0, m * 16 + 32)
            expert_step(SLOT_TILES - 2, 1, 16 * ((SLOT_TILES + 1) // 2))
            expert_step(SLOT_TILES - 1, 0, None)
            down(SLOT_TILES - 1, 0)


_INS = ["x", "ctx_1024", "mask_Bx1xSxS2_fk0",
        "L0_attn_Wq", "L0_attn_Wk", "L0_attn_Wv", "L0_attn_Wp", "L0_attn_bq", "L0_attn_bk", "L0_attn_bv", "L0_attn_bp",
        "L0_xattn_Wq", "L0_xattn_Wk", "L0_xattn_Wv", "L0_xattn_Wo", "L0_xattn_bq", "L0_xattn_bk", "L0_xattn_bv", "L0_xattn_bo",
        "L0_ffn_Wg", "L0_ffn_W1", "L0_ffn_b1", "L0_ffn_W2", "L0_ffn_b2"]


def kernel(**inputs):
    import numpy as np
    import concourse.bacc as bacc
    from concourse.bass_utils import run_bass_kernel_spmd

    nc = bacc.Bacc("TRN2", target_bir_lowering=False, num_devices=1)
    arrays, a = {}, {}
    for name in _INS:
        arrays[f"in_{name}"] = np.ascontiguousarray(inputs[name])
        a[name] = nc.dram_tensor(f"in_{name}", arrays[f"in_{name}"].shape, F32, kind="ExternalInput").ap()
    out = nc.dram_tensor("out", a["x"].shape, F32, kind="ExternalOutput").ap()

    def group(prefix, names):
        return [a[f"L0_{prefix}_{n}"] for n in names]

    decoder_layer(nc, a["x"], a["ctx_1024"], a["mask_Bx1xSxS2_fk0"],
                  group("attn", ("Wq", "Wk", "Wv", "Wp")), group("attn", ("bq", "bk", "bv", "bp")),
                  group("xattn", ("Wq", "Wk", "Wv", "Wo")), group("xattn", ("bq", "bk", "bv", "bo")),
                  *group("ffn", ("Wg", "W1", "b1", "W2", "b2")), out)
    r = run_bass_kernel_spmd(nc, [arrays], core_ids=[0])
    return r.results[0]["out"]
```
